# Optimizing a Trainium2 kernel written in Bass

```python
import numpy as np
import jax
import jax.numpy as jnp

def _softmax(x, axis=-1):
    return jax.nn.softmax(x, axis=axis)

def _gelu(x):
    return jax.nn.gelu(x, approximate=True)

def _silu(x):
    return jax.nn.silu(x)

def _sigmoid(x):
    return jax.nn.sigmoid(x)

def _layernorm(x, axis=-1, eps=1e-05):
    m = jnp.mean(x, axis=axis, keepdims=True)
    v = jnp.var(x, axis=axis, keepdims=True)
    return (x - m) / jnp.sqrt(v + eps)

def _scatter_add(tgt, idx, src, axis=0):
    return tgt.at[idx].add(src)

def _segment_sum(src, seg, n):
    return jax.ops.segment_sum(src, seg, n)
kernel_name = 'mk_gps_d2_gnn_r16_e6b05c'

def setup_inputs(seed: int=0):
    np.random.seed(seed)
    _w = jnp.asarray

    def _rec_inputs():
        import jax
        import jax.numpy as jnp
        _gk = jax.random.key(seed)
        x = -0.0001126 + 1 * jax.random.normal(jax.random.fold_in(_gk, 1), (625, 768), jnp.float32)
        _s = jax.random.randint(jax.random.fold_in(_gk, 2), (5000,), 0, 625, jnp.int32)
        _d = jax.random.randint(jax.random.fold_in(_gk, 3), (5000,), 0, 625, jnp.int32)
        _loop = jnp.arange(625, dtype=jnp.int32)
        src = jnp.concatenate([_s, _d, _loop])
        dst = jnp.concatenate([_d, _s, _loop])
        _o = jnp.argsort(dst, stable=True)
        src = src[_o]
        dst = dst[_o]
        edge_attr_32 = 0.000376506 + 0.999991 * jax.random.normal(jax.random.fold_in(_gk, 12), (10625, 32), jnp.float32)
        edge_weight1 = -0.00472126 + 0.997171 * jax.random.normal(jax.random.fold_in(_gk, 14), (10625, 1), jnp.float32)
        node_type_6 = jax.random.randint(jax.random.fold_in(_gk, 15), (625,), 0, 6, jnp.int32)
        return (x, src, dst, edge_attr_32, edge_weight1, node_type_6)
    x, src, dst, edge_attr_32, edge_weight1, node_type_6 = _rec_inputs()

    def _L0_gnn_setup():
        import jax, jax.numpy as jnp
        import numpy as np
        N, E, D, H, C = (625, 6250, 768, 4, 192)
        NEG_SLOPE = 0.2

        def gat_conv(x, src, dst, W, a_src, a_dst, b):
            h = (x @ W).reshape(N, H, C)
            as_n = (h * a_src).sum(-1)
            ad_n = (h * a_dst).sum(-1)
            e = jax.nn.leaky_relu(as_n[src] + ad_n[dst], NEG_SLOPE)
            m = jax.ops.segment_max(e, dst, num_segments=N)
            p = jnp.exp(e - m[dst])
            s = jax.ops.segment_sum(p, dst, num_segments=N)
            alpha = p / (s[dst] + 1e-16)
            out = jax.ops.segment_sum(alpha[:, :, None] * h[src], dst, num_segments=N)
            return out.reshape(N, H * C) + b
        key = jax.random.key(seed)
        ks = jax.random.split(key, 16)
        w = lambda k, shape: jax.random.normal(k, shape, dtype=jnp.float32) * 0.02
        inp = {}
        inp['x'] = jax.random.normal(ks[0], (N, D), dtype=jnp.float32)
        inp['edge_index'] = jax.random.randint(ks[1], (2, E), 0, N, dtype=jnp.int32)
        inp['batch'] = jnp.zeros((N,), dtype=jnp.int32)
        inp['edge_attr'] = jax.random.normal(ks[2], (E, 1), dtype=jnp.float32)
        inp['W_ah'] = w(ks[3], (D, D))
        inp['b_ah'] = jnp.zeros((D,), jnp.float32)
        for i in range(3):
            inp[f'W{i}'] = w(ks[4 + 3 * i], (D, H * C))
            inp[f'a_src{i}'] = w(ks[5 + 3 * i], (H, C))
            inp[f'a_dst{i}'] = w(ks[6 + 3 * i], (H, C))
            inp[f'b{i}'] = jnp.zeros((H * C,), jnp.float32)
        inp['W_out'] = w(ks[13], (3 * D, D))
        inp['b_out'] = jnp.zeros((D,), jnp.float32)
        return inp
    _L0_gnn_all = _L0_gnn_setup()
    _L0_gnn_in = {k: v for k, v in _L0_gnn_all.items() if k in ('W_ah', 'b_ah', 'W0', 'a_src0', 'a_dst0', 'b0', 'W1', 'a_src1', 'a_dst1', 'b1', 'W2', 'a_src2', 'a_dst2', 'b2', 'W_out', 'b_out')}
    del _L0_gnn_all

    def _L0_mix_setup():
        import jax, jax.numpy as jnp
        import numpy as np
        import math
        B, N, C = (8, 256, 768)
        H = 12
        DH = C // H
        M = 256
        LN_EPS = 1e-05

        def _phi(t, random_features):
            norm_sq = 0.5 * jnp.sum(t * t, axis=-1, keepdims=True)
            proj = jnp.einsum('bhnd,md->bhnm', t, random_features)
            return jnp.exp(proj - norm_sq) * (1.0 / math.sqrt(M))
        key = jax.random.key(seed)
        ks = jax.random.split(key, 7)
        x = jax.random.normal(ks[0], (B, N, C), dtype=jnp.float32)
        W_qkv = jax.random.normal(ks[1], (C, 3 * C), dtype=jnp.float32) * (1.0 / math.sqrt(C))
        W_proj = jax.random.normal(ks[2], (C, C), dtype=jnp.float32) * (1.0 / math.sqrt(C))
        b_proj = jnp.zeros((C,), dtype=jnp.float32)
        gamma = jnp.ones((C,), dtype=jnp.float32)
        beta = jnp.zeros((C,), dtype=jnp.float32)
        random_features = jax.random.normal(ks[3], (M, DH), dtype=jnp.float32) / math.sqrt(DH)
        return {'x': x, 'W_qkv': W_qkv, 'W_proj': W_proj, 'b_proj': b_proj, 'gamma': gamma, 'beta': beta, 'random_features': random_features}
    _L0_mix_all = _L0_mix_setup()
    _L0_mix_in = {k: v for k, v in _L0_mix_all.items() if k in ('W_qkv', 'W_proj', 'b_proj', 'gamma', 'beta', 'random_features')}
    del _L0_mix_all

    def _L0_ffn_setup():
        import jax, jax.numpy as jnp
        import numpy as np
        B, T, H, F, E = (512, 32, 768, 192, 3)
        key = jax.random.key(seed)
        ks = jax.random.split(key, 4)
        s = 0.02
        return {'x': jax.random.normal(ks[0], (B, T, H), jnp.float32), 'Wg': jax.random.normal(ks[1], (E, H), jnp.float32) * s, 'W1': jax.random.normal(ks[2], (E, H, F), jnp.float32) * s, 'b1': jnp.zeros((E, F), jnp.float32), 'W2': jax.random.normal(ks[3], (E, F, H), jnp.float32) * s, 'b2': jnp.zeros((E, H), jnp.float32)}
    _L0_ffn_all = _L0_ffn_setup()
    _L0_ffn_in = {k: v for k, v in _L0_ffn_all.items() if k in ('Wg', 'W1', 'b1', 'W2', 'b2')}
    del _L0_ffn_all

    def _L1_gnn_setup():
        import jax, jax.numpy as jnp
        import numpy as np
        N, E, D, T, EA = (3125, 8192, 768, 6, 32)
        H4 = D // 4
        EPS = 1e-05
        key = jax.random.key(seed)
        ks = jax.random.split(key, 24)

        def init(k, shape, fan_in):
            return (jax.random.normal(k, shape, jnp.float32) / np.sqrt(fan_in)).astype(jnp.float32)
        inp = {'x': jax.random.normal(ks[0], (N, D), jnp.float32), 'edge_index': jax.random.randint(ks[1], (2, E), 0, N, jnp.int64), 'edge_attr': jax.random.normal(ks[2], (E, EA), jnp.float32), 'node_types': jax.random.randint(ks[3], (N,), 0, T, jnp.int64), 'W_type': init(ks[4], (T, D, D), D), 'b_type': jnp.zeros((T, D), jnp.float32), 'msg_W1': init(ks[5], (2 * D, D), 2 * D), 'msg_b1': jnp.zeros((D,), jnp.float32), 'msg_W2': init(ks[6], (D, D), D), 'msg_b2': jnp.zeros((D,), jnp.float32), 'edge_W1': init(ks[7], (EA, H4), EA), 'edge_b1': jnp.zeros((H4,), jnp.float32), 'edge_W2': init(ks[8], (H4, 1), H4), 'edge_b2': jnp.zeros((1,), jnp.float32), 'agg_W1': init(ks[9], (D, D), D), 'agg_b1': jnp.zeros((D,), jnp.float32), 'agg_W2': init(ks[10], (D, D), D), 'agg_b2': jnp.zeros((D,), jnp.float32), 'out_W': init(ks[11], (D, D), D), 'out_b': jnp.zeros((D,), jnp.float32), 'ln_g': jnp.ones((D,), jnp.float32), 'ln_b': jnp.zeros((D,), jnp.float32)}
        return inp
    _L1_gnn_all = _L1_gnn_setup()
    _L1_gnn_in = {k: v for k, v in _L1_gnn_all.items() if k in ('W_type', 'b_type', 'msg_W1', 'msg_b1', 'msg_W2', 'msg_b2', 'edge_W1', 'edge_b1', 'edge_W2', 'edge_b2', 'agg_W1', 'agg_b1', 'agg_W2', 'agg_b2', 'out_W', 'out_b', 'ln_g', 'ln_b')}
    del _L1_gnn_all

    def _L1_mix_setup():
        import jax, jax.numpy as jnp
        import numpy as np
        DIM = 768
        NUM_HEADS = 12
        HEAD_DIM = DIM // NUM_HEADS
        ORDER = 2
        SCALE = HEAD_DIM ** (-0.5)
        key = jax.random.key(seed)
        k_x, k_qkv, k_pw, k_pb = jax.random.split(key, 4)
        B, N = (16, 577)
        x = jax.random.normal(k_x, (B, N, DIM), dtype=jnp.float32)
        qkv_w = jax.random.normal(k_qkv, (3 * DIM, DIM), dtype=jnp.float32) * 0.02
        proj_w = jax.random.normal(k_pw, (DIM, DIM), dtype=jnp.float32) * 0.02
        proj_b = jax.random.normal(k_pb, (DIM,), dtype=jnp.float32) * 0.02
        return {'x': x, 'qkv_w': qkv_w, 'proj_w': proj_w, 'proj_b': proj_b}
    _L1_mix_all = _L1_mix_setup()
    _L1_mix_in = {k: v for k, v in _L1_mix_all.items() if k in ('qkv_w', 'proj_w', 'proj_b')}
    del _L1_mix_all

    def _L1_ffn_setup():
        import jax, jax.numpy as jnp
        import numpy as np
        D_MODEL, D_FF, N_EXPERTS, TOP_K = (768, 192, 8, 2)
        B, S = (2, 1024)
        LN_EPS = 1e-05

        def _layernorm(x, gamma, beta):
            mu = jnp.mean(x, axis=-1, keepdims=True)
            var = jnp.mean(jnp.square(x - mu), axis=-1, keepdims=True)
            return (x - mu) * jax.lax.rsqrt(var + LN_EPS) * gamma + beta
        key = jax.random.key(seed)
        k1, k2, k3, k4 = jax.random.split(key, 4)
        return {'hidden_states': jax.random.normal(k1, (B, S, D_MODEL), dtype=jnp.float32), 'ln_gamma': jnp.ones((D_MODEL,), dtype=jnp.float32), 'ln_beta': jnp.zeros((D_MODEL,), dtype=jnp.float32), 'router_w': jax.random.normal(k2, (D_MODEL, N_EXPERTS), dtype=jnp.float32) * 0.02, 'w1': jax.random.normal(k3, (N_EXPERTS, D_MODEL, D_FF), dtype=jnp.float32) * 0.02, 'w2': jax.random.normal(k4, (N_EXPERTS, D_FF, D_MODEL), dtype=jnp.float32) * 0.02}
    _L1_ffn_all = _L1_ffn_setup()
    _L1_ffn_in = {k: v for k, v in _L1_ffn_all.items() if k in ('ln_gamma', 'ln_beta', 'router_w', 'w1', 'w2')}
    del _L1_ffn_all
    return {'x': x, 'src': src, 'dst': dst, 'edge_attr_32': edge_attr_32, 'edge_weight1': edge_weight1, 'node_type_6': node_type_6, 'L0_gnn_W_ah': _L0_gnn_in['W_ah'], 'L0_gnn_b_ah': _L0_gnn_in['b_ah'], 'L0_gnn_W0': _L0_gnn_in['W0'], 'L0_gnn_a_src0': _L0_gnn_in['a_src0'], 'L0_gnn_a_dst0': _L0_gnn_in['a_dst0'], 'L0_gnn_b0': _L0_gnn_in['b0'], 'L0_gnn_W1': _L0_gnn_in['W1'], 'L0_gnn_a_src1': _L0_gnn_in['a_src1'], 'L0_gnn_a_dst1': _L0_gnn_in['a_dst1'], 'L0_gnn_b1': _L0_gnn_in['b1'], 'L0_gnn_W2': _L0_gnn_in['W2'], 'L0_gnn_a_src2': _L0_gnn_in['a_src2'], 'L0_gnn_a_dst2': _L0_gnn_in['a_dst2'], 'L0_gnn_b2': _L0_gnn_in['b2'], 'L0_gnn_W_out': _L0_gnn_in['W_out'], 'L0_gnn_b_out': _L0_gnn_in['b_out'], 'L0_mix_W_qkv': _L0_mix_in['W_qkv'], 'L0_mix_W_proj': _L0_mix_in['W_proj'], 'L0_mix_b_proj': _L0_mix_in['b_proj'], 'L0_mix_gamma': _L0_mix_in['gamma'], 'L0_mix_beta': _L0_mix_in['beta'], 'L0_mix_random_features': _L0_mix_in['random_features'], 'L0_ffn_Wg': _L0_ffn_in['Wg'], 'L0_ffn_W1': _L0_ffn_in['W1'], 'L0_ffn_b1': _L0_ffn_in['b1'], 'L0_ffn_W2': _L0_ffn_in['W2'], 'L0_ffn_b2': _L0_ffn_in['b2'], 'L1_gnn_W_type': _L1_gnn_in['W_type'], 'L1_gnn_b_type': _L1_gnn_in['b_type'], 'L1_gnn_msg_W1': _L1_gnn_in['msg_W1'], 'L1_gnn_msg_b1': _L1_gnn_in['msg_b1'], 'L1_gnn_msg_W2': _L1_gnn_in['msg_W2'], 'L1_gnn_msg_b2': _L1_gnn_in['msg_b2'], 'L1_gnn_edge_W1': _L1_gnn_in['edge_W1'], 'L1_gnn_edge_b1': _L1_gnn_in['edge_b1'], 'L1_gnn_edge_W2': _L1_gnn_in['edge_W2'], 'L1_gnn_edge_b2': _L1_gnn_in['edge_b2'], 'L1_gnn_agg_W1': _L1_gnn_in['agg_W1'], 'L1_gnn_agg_b1': _L1_gnn_in['agg_b1'], 'L1_gnn_agg_W2': _L1_gnn_in['agg_W2'], 'L1_gnn_agg_b2': _L1_gnn_in['agg_b2'], 'L1_gnn_out_W': _L1_gnn_in['out_W'], 'L1_gnn_out_b': _L1_gnn_in['out_b'], 'L1_gnn_ln_g': _L1_gnn_in['ln_g'], 'L1_gnn_ln_b': _L1_gnn_in['ln_b'], 'L1_mix_qkv_w': _L1_mix_in['qkv_w'], 'L1_mix_proj_w': _L1_mix_in['proj_w'], 'L1_mix_proj_b': _L1_mix_in['proj_b'], 'L1_ffn_ln_gamma': _L1_ffn_in['ln_gamma'], 'L1_ffn_ln_beta': _L1_ffn_in['ln_beta'], 'L1_ffn_router_w': _L1_ffn_in['router_w'], 'L1_ffn_w1': _L1_ffn_in['w1'], 'L1_ffn_w2': _L1_ffn_in['w2']}

def reference(x, src, dst, edge_attr_32, edge_weight1, node_type_6, L0_gnn_W_ah, L0_gnn_b_ah, L0_gnn_W0, L0_gnn_a_src0, L0_gnn_a_dst0, L0_gnn_b0, L0_gnn_W1, L0_gnn_a_src1, L0_gnn_a_dst1, L0_gnn_b1, L0_gnn_W2, L0_gnn_a_src2, L0_gnn_a_dst2, L0_gnn_b2, L0_gnn_W_out, L0_gnn_b_out, L0_mix_W_qkv, L0_mix_W_proj, L0_mix_b_proj, L0_mix_gamma, L0_mix_beta, L0_mix_random_features, L0_ffn_Wg, L0_ffn_W1, L0_ffn_b1, L0_ffn_W2, L0_ffn_b2, L1_gnn_W_type, L1_gnn_b_type, L1_gnn_msg_W1, L1_gnn_msg_b1, L1_gnn_msg_W2, L1_gnn_msg_b2, L1_gnn_edge_W1, L1_gnn_edge_b1, L1_gnn_edge_W2, L1_gnn_edge_b2, L1_gnn_agg_W1, L1_gnn_agg_b1, L1_gnn_agg_W2, L1_gnn_agg_b2, L1_gnn_out_W, L1_gnn_out_b, L1_gnn_ln_g, L1_gnn_ln_b, L1_mix_qkv_w, L1_mix_proj_w, L1_mix_proj_b, L1_ffn_ln_gamma, L1_ffn_ln_beta, L1_ffn_router_w, L1_ffn_w1, L1_ffn_w2):
    import jax
    import jax.numpy as jnp

    def _L0_gnn_ref(x, edge_index, batch, edge_attr, W_ah, b_ah, W0, a_src0, a_dst0, b0, W1, a_src1, a_dst1, b1, W2, a_src2, a_dst2, b2, W_out, b_out):
        import jax, jax.numpy as jnp
        import numpy as np
        N, E, D, H, C = (625, 6250, 768, 4, 192)
        NEG_SLOPE = 0.2

        def gat_conv(x, src, dst, W, a_src, a_dst, b):
            h = (x @ W).reshape(N, H, C)
            as_n = (h * a_src).sum(-1)
            ad_n = (h * a_dst).sum(-1)
            e = jax.nn.leaky_relu(as_n[src] + ad_n[dst], NEG_SLOPE)
            m = jax.ops.segment_max(e, dst, num_segments=N)
            p = jnp.exp(e - m[dst])
            s = jax.ops.segment_sum(p, dst, num_segments=N)
            alpha = p / (s[dst] + 1e-16)
            out = jax.ops.segment_sum(alpha[:, :, None] * h[src], dst, num_segments=N)
            return out.reshape(N, H * C) + b
        loops = jnp.arange(N, dtype=edge_index.dtype)
        src = jnp.concatenate([edge_index[0], loops])
        dst = jnp.concatenate([edge_index[1], loops])
        x1 = jax.nn.relu(x @ W_ah + b_ah)
        xs = [jax.nn.relu(gat_conv(x1, src, dst, W, a_s, a_d, b)) for W, a_s, a_d, b in ((W0, a_src0, a_dst0, b0), (W1, a_src1, a_dst1, b1), (W2, a_src2, a_dst2, b2))]
        node_emb = jnp.concatenate(xs, axis=1)
        return jax.nn.relu(node_emb @ W_out + b_out)

    def _L0_mix_ref(x, W_qkv, W_proj, b_proj, gamma, beta, random_features):
        import jax, jax.numpy as jnp
        import numpy as np
        import math
        B, N, C = (8, 256, 768)
        H = 12
        DH = C // H
        M = 256
        LN_EPS = 1e-05

        def _phi(t, random_features):
            norm_sq = 0.5 * jnp.sum(t * t, axis=-1, keepdims=True)
            proj = jnp.einsum('bhnd,md->bhnm', t, random_features)
            return jnp.exp(proj - norm_sq) * (1.0 / math.sqrt(M))
        b, n, c = x.shape
        qkv = (x @ W_qkv).reshape(b, n, 3, H, DH)
        qkv = jnp.transpose(qkv, (2, 0, 3, 1, 4))
        q, k, v = (qkv[0], qkv[1], qkv[2])
        q_p = _phi(q, random_features)
        k_p = _phi(k, random_features)
        kv = jnp.einsum('bhnm,bhnd->bhmd', k_p, v)
        out = jnp.einsum('bhnm,bhmd->bhnd', q_p, kv)
        k_sum = jnp.sum(k_p, axis=2)
        normalizer = jnp.einsum('bhnm,bhm->bhn', q_p, k_sum)[..., None]
        out = out / (normalizer + 1e-06)
        x_attn = jnp.transpose(out, (0, 2, 1, 3)).reshape(b, n, c)
        x_attn = x_attn @ W_proj + b_proj
        y = x + x_attn
        mu = jnp.mean(y, axis=-1, keepdims=True)
        var = jnp.mean(jnp.square(y - mu), axis=-1, keepdims=True)
        return (y - mu) * jax.lax.rsqrt(var + LN_EPS) * gamma + beta

    def _L0_ffn_ref(x, Wg, W1, b1, W2, b2):
        import jax, jax.numpy as jnp
        import numpy as np
        B, T, H, F, E = (512, 32, 768, 192, 3)
        scores = jax.nn.softmax(jnp.mean(x, axis=1) @ Wg.T, axis=-1)
        _, idx = jax.lax.top_k(scores, 1)
        sel = idx[:, 0]
        h = jax.nn.gelu(jnp.einsum('bth,ehf->betf', x, W1) + b1[None, :, None, :], approximate=False)
        y = jnp.einsum('betf,efh->beth', h, W2) + b2[None, :, None, :]
        w = scores * jax.nn.one_hot(sel, E, dtype=scores.dtype)
        out = jnp.einsum('beth,be->bth', y, w)
        return out

    def _L1_gnn_ref(x, edge_index, edge_attr, node_types, W_type, b_type, msg_W1, msg_b1, msg_W2, msg_b2, edge_W1, edge_b1, edge_W2, edge_b2, agg_W1, agg_b1, agg_W2, agg_b2, out_W, out_b, ln_g, ln_b):
        import jax, jax.numpy as jnp
        import numpy as np
        N, E, D, T, EA = (3125, 8192, 768, 6, 32)
        H4 = D // 4
        EPS = 1e-05
        n = x.shape[0]
        all_h = jnp.einsum('ni,tio->tno', x, W_type)
        h = jnp.take_along_axis(all_h, node_types[None, :, None], axis=0)[0]
        h = h + b_type[node_types]
        row, col = (edge_index[0], edge_index[1])
        m_in = jnp.concatenate([h[row], h[col]], axis=1)
        m = jax.nn.relu(m_in @ msg_W1 + msg_b1) @ msg_W2 + msg_b2
        ew = jax.nn.sigmoid(jax.nn.relu(edge_attr @ edge_W1 + edge_b1) @ edge_W2 + edge_b2)
        m = m * ew
        agg = jax.ops.segment_sum(m, col, num_segments=n)
        agg = jax.nn.relu(agg @ agg_W1 + agg_b1) @ agg_W2 + agg_b2
        h = h + agg
        h = h @ out_W + out_b
        h = h + x
        mu = jnp.mean(h, axis=-1, keepdims=True)
        var = jnp.mean(jnp.square(h - mu), axis=-1, keepdims=True)
        h = (h - mu) * jax.lax.rsqrt(var + EPS) * ln_g + ln_b
        return h

    def _L1_mix_ref(x, qkv_w, proj_w, proj_b):
        import jax, jax.numpy as jnp
        import numpy as np
        DIM = 768
        NUM_HEADS = 12
        HEAD_DIM = DIM // NUM_HEADS
        ORDER = 2
        SCALE = HEAD_DIM ** (-0.5)
        B, N, C = x.shape
        qkv = jnp.einsum('bnc,oc->bno', x, qkv_w)
        qkv = qkv.reshape(B, N, 3, NUM_HEADS, HEAD_DIM).transpose(2, 0, 3, 1, 4)
        q, k, v = (qkv[0], qkv[1], qkv[2])
        q = q * SCALE
        qk = jnp.einsum('bhnd,bhmd->bhnm', q, k)
        attn = jnp.ones_like(qk)
        x_power = jnp.ones_like(qk)
        factorial = 1.0
        for i in range(1, ORDER + 1):
            if i > 1:
                factorial *= i
            attn = attn + x_power / factorial
            x_power = x_power * qk
        attn = jax.nn.relu(attn)
        attn = attn / jnp.sum(attn, axis=-1, keepdims=True)
        out = jnp.einsum('bhnm,bhmd->bhnd', attn, v)
        out = out.transpose(0, 2, 1, 3).reshape(B, N, C)
        out = jnp.einsum('bnc,oc->bno', out, proj_w) + proj_b
        return out

    def _L1_ffn_ref(hidden_states, ln_gamma, ln_beta, router_w, w1, w2):
        import jax, jax.numpy as jnp
        import numpy as np
        D_MODEL, D_FF, N_EXPERTS, TOP_K = (768, 192, 8, 2)
        B, S = (2, 1024)
        LN_EPS = 1e-05

        def _layernorm(x, gamma, beta):
            mu = jnp.mean(x, axis=-1, keepdims=True)
            var = jnp.mean(jnp.square(x - mu), axis=-1, keepdims=True)
            return (x - mu) * jax.lax.rsqrt(var + LN_EPS) * gamma + beta
        Bz, Sz, D = hidden_states.shape
        residual = hidden_states
        x = _layernorm(hidden_states, ln_gamma, ln_beta)
        tokens = x.reshape(-1, D)
        T = tokens.shape[0]
        logits = tokens @ router_w
        probs = jax.nn.softmax(logits, axis=-1)
        topw, topi = jax.lax.top_k(probs, TOP_K)
        topw = topw / jnp.sum(topw, axis=-1, keepdims=True)
        gates = jnp.zeros((T, N_EXPERTS), dtype=tokens.dtype)
        gates = gates.at[jnp.arange(T)[:, None], topi].set(topw)
        h = jnp.einsum('td,edf->etf', tokens, w1)
        h = jax.nn.silu(h)
        y = jnp.einsum('etf,efd->etd', h, w2)
        out = jnp.einsum('te,etd->td', gates, y)
        return residual + out.reshape(Bz, Sz, D)
    edge_index = jnp.stack([src, dst])
    batch0 = jnp.zeros((625,), jnp.int32)
    xn = _layernorm(x, axis=-1)
    x = x + _L0_gnn_ref(xn, edge_index, batch0, edge_weight1, L0_gnn_W_ah, L0_gnn_b_ah, L0_gnn_W0, L0_gnn_a_src0, L0_gnn_a_dst0, L0_gnn_b0, L0_gnn_W1, L0_gnn_a_src1, L0_gnn_a_dst1, L0_gnn_b1, L0_gnn_W2, L0_gnn_a_src2, L0_gnn_a_dst2, L0_gnn_b2, L0_gnn_W_out, L0_gnn_b_out) + _L0_mix_ref(xn[None], L0_mix_W_qkv, L0_mix_W_proj, L0_mix_b_proj, L0_mix_gamma, L0_mix_beta, L0_mix_random_features)[0]
    x = x + _L0_ffn_ref(_layernorm(x, axis=-1)[None], L0_ffn_Wg, L0_ffn_W1, L0_ffn_b1, L0_ffn_W2, L0_ffn_b2)[0]
    xn = _layernorm(x, axis=-1)
    x = x + _L1_gnn_ref(xn, edge_index, edge_attr_32, node_type_6, L1_gnn_W_type, L1_gnn_b_type, L1_gnn_msg_W1, L1_gnn_msg_b1, L1_gnn_msg_W2, L1_gnn_msg_b2, L1_gnn_edge_W1, L1_gnn_edge_b1, L1_gnn_edge_W2, L1_gnn_edge_b2, L1_gnn_agg_W1, L1_gnn_agg_b1, L1_gnn_agg_W2, L1_gnn_agg_b2, L1_gnn_out_W, L1_gnn_out_b, L1_gnn_ln_g, L1_gnn_ln_b) + _L1_mix_ref(xn[None], L1_mix_qkv_w, L1_mix_proj_w, L1_mix_proj_b)[0]
    x = x + _L1_ffn_ref(_layernorm(x, axis=-1)[None], L1_ffn_ln_gamma, L1_ffn_ln_beta, L1_ffn_router_w, L1_ffn_w1, L1_ffn_w2)[0]
    return x

_drawn_inputs = setup_inputs


def setup_inputs(seed=0):
    import zlib

    import numpy as np

    out = dict(_drawn_inputs(seed))
    spreads = {'L0_gnn_b_ah': (0.0, 0.8),
     'L0_gnn_b0': (0.0, 0.651),
     'L0_gnn_b1': (0.0, 0.68),
     'L0_gnn_b2': (0.0, 0.656),
     'L0_gnn_b_out': (0.0, 0.1),
     'L0_mix_b_proj': (0.0, 0.1),
     'L0_mix_gamma': (1.0, 0.2),
     'L0_mix_beta': (0.0, 0.1),
     'L0_ffn_b1': (0.0, 0.8),
     'L0_ffn_b2': (0.0, 0.469),
     'L1_gnn_b_type': (0.0, 0.494),
     'L1_gnn_msg_b1': (0.0, 0.361),
     'L1_gnn_msg_b2': (0.0, 0.1),
     'L1_gnn_edge_b1': (0.0, 2.0),
     'L1_gnn_agg_b1': (0.0, 2.0),
     'L1_gnn_agg_b2': (0.0, 0.696),
     'L1_gnn_out_b': (0.0, 0.706),
     'L1_gnn_ln_g': (1.0, 0.2),
     'L1_gnn_ln_b': (0.0, 0.36),
     'L1_ffn_ln_gamma': (1.0, 0.6),
     'L1_ffn_ln_beta': (0.0, 0.8)}
    factors = {'L0_gnn_W_ah': 5.766,
     'L0_gnn_W0': 3.735,
     'L0_gnn_a_src0': 8.0,
     'L0_gnn_a_dst0': 8.0,
     'L0_gnn_a_src1': 8.0,
     'L0_gnn_a_dst1': 147.07,
     'L0_gnn_W2': 3.887,
     'L0_gnn_a_src2': 8.0,
     'L0_gnn_a_dst2': 8.0,
     'L0_mix_W_qkv': 8.0,
     'L0_mix_W_proj': 8.0,
     'L0_mix_random_features': 8.0,
     'L0_ffn_W1': 4.088,
     'L0_ffn_W2': 3.808,
     'L1_gnn_edge_W1': 7.866,
     'L1_mix_qkv_w': 5.206,
     'L1_mix_proj_w': 5.058,
     'L1_mix_proj_b': 7.232,
     'L1_ffn_router_w': 3.646,
     'L1_ffn_w1': 3.237,
     'L1_ffn_w2': 3.12,
     'edge_attr_32': 2.77}
    for name, (base, spread) in spreads.items():
        noise = np.random.default_rng([zlib.crc32(name.encode()), seed]).standard_normal(out[name].shape)
        drawn = base * np.exp(spread * noise) if base else spread * noise
        out[name] = jnp.asarray(drawn.astype(out[name].dtype))
    for name, factor in factors.items():
        out[name] = (out[name] * factor).astype(out[name].dtype)
    return out
```

```python
import concourse.bass as bass
from concourse import mybir
from contextlib import ExitStack

F32, BF16, F16, I32 = mybir.dt.float32, mybir.dt.bfloat16, mybir.dt.float16, mybir.dt.int32
ACT = mybir.ActivationFunctionType
ALU = mybir.AluOpType
AX = mybir.AxisListType

N = 625
TN, NT = 125, 5
D, C = 768, 6
NP, HN = 628, 314
E = 10625
EJ = 85
ST = 88
GH, GC = 4, 192
MH, MD = 12, 64
RF = 256
EC = 500
ES = -(-E // EC)
TYPES, EXPERTS, FF = 6, 8, 192
NEG = -1.0e30


def row_order():
    rows = ["mix_b_proj", "mix_gamma", "mix_beta"]
    for i in range(3):
        rows += [f"a_src{i}", f"a_dst{i}"]
    rows += ["gnn_b_out", "ffn_b2_0", "ffn_b2_1", "ffn_b2_2",
             "msg_b1", "out_b", "ln_g", "ln_b", "mix1_proj_b", "moe_g", "moe_b"]
    return rows


def column_places():
    at, out = 0, {}
    for name, n in (("b_ah", 6), ("b0", 6), ("b1", 6), ("b2", 6), ("agg_b1", 6), ("agg_b2", 6),
                    ("b_type", 36), ("ffn_b1", 6), ("edge_b1", 2), ("edge_w2", 2), ("wg", 18), ("rw", 48)):
        out[name] = (at, n)
        at += n
    out["all"] = (0, at)
    return out


class PsumRing:

    def __init__(self, nc, ctx):
        self.tiles = [ctx.enter_context(nc.psum_tensor(f"ps{i}", [128, 1024], F32)) for i in range(4)]
        self.full = [ctx.enter_context(nc.semaphore(f"psum_computed{i}")) for i in range(4)]
        self.free = [ctx.enter_context(nc.semaphore(f"psum_drained{i}")) for i in range(4)]
        self.filled, self.freed, self.opened, self.where = [0] * 4, [0] * 4, 0, {}

    def open(self, pe, name, reads=1):
        s = self.opened % 4
        self.opened += 1
        if self.freed[s]:
            pe.wait_ge(self.free[s], self.freed[s])
        self.freed[s] += reads
        self.filled[s] += 1
        assert name not in self.where, name
        self.where[name] = (s, self.filled[s], self.freed[s])
        return self.tiles[s], self.full[s]

    def align(self):
        while self.opened % 4:
            self.opened += 1

    def looped(self, name, times):
        for s in range(4):
            self.filled[s] += times
            self.freed[s] += times
            self.where[f"{name}{s}"] = (s, self.filled[s], self.freed[s])

    def computed(self, eng, name):
        s, n, _ = self.where[name]
        eng.wait_ge(self.full[s], n)
        return self.tiles[s], self.free[s]

    def reads(self, eng, name, k, total):
        s, _, n = self.where[name]
        eng.wait_ge(self.free[s], n - total + k)

    def drained(self, eng, *names):
        most = {}
        for name in names:
            s, _, n = self.where[name]
            most[s] = max(most.get(s, 0), n)
        for s, n in most.items():
            eng.wait_ge(self.free[s], n)



def gps_block(nc, a, stop=None):
    ctx = ExitStack()
    with ctx:
        def sb(name, shape, dt=F32):
            return ctx.enter_context(nc.sbuf_tensor(name, shape, dt))

        sems = {}

        def sem(name):
            if name not in sems:
                sems[name] = ctx.enter_context(nc.semaphore(name))
            return sems[name]

        psum = PsumRing(nc, ctx)
        ring = [sb(f"wring{i}", [128, 3, D]) for i in range(5)]
        RG = [sb(f"region{i}", [128, 3904]) for i in range(9)]
        rowbuf = [sb(f"rowbuf{i}", [128, D]) for i in range(3)]

        def asR(r):
            return RG[r][0:TN, 0:NT * D].rearrange("p (t d) -> p t d", t=NT)

        def asT(r):
            return RG[r][:, 0:C * NP].rearrange("p (c n) -> p c n", c=C)

        def asV(r):
            return RG[r][0:TN, 0:NT * MH * 65].rearrange("p (t h d) -> p t h d", t=NT, h=MH)

        def asG(r):
            return RG[r][0:TN, 0:NT * GH * 193].rearrange("p (t h d) -> p t h d", t=NT, h=GH)

        def asN(r, w=N):
            return RG[r][0:TN, 0:NT * w].rearrange("p (t n) -> p t n", t=NT)

        def blocks(ps, p=TN, w=125):
            return ps[0:p, 0:640].rearrange("p (t n) -> p t n", n=128)[:, :, 0:w]

        def halves(ps, n, lo=0, hi=TN):
            return ps[lo:hi, :].rearrange("p (b n) -> p b n", b=2)[:, :, 0:n]

        def two(x):
            return x.rearrange("p (b n) -> p b n", b=2)

        ident = sb("ident", [128, 128])
        one = sb("one", [128, 1])
        rfe = sb("rfe", [128, RF])
        rfo = sb("rfo", [128, RF])
        PL = column_places()
        cols = sb("cols", [128, PL["all"][1]])
        slots = sb("slots", [128, 3, ST])
        rows_i = sb("rows_i", [128, 2, ST], I32)
        tmap = sb("tmap", [128, ST], I32)
        iota_n = sb("iota_n", [128, N + 1], F16)
        oh_raw = sb("oh_raw", [128, 1696])
        stats = sb("stats", [128, NT, 2, 6])
        mv = sb("mv", [128, NT, 2])
        lnt = sb("lnt", [128, 4, NT])
        asd = sb("asd", [128, 8, NT, GH])
        rden = sb("rden", [128, 4, NT])
        kvs = sb("kvs", [128, 2, 2, 65])
        eb2 = sb("eb2", [128, 1])
        idx = sb("idx", [128, 2, 2], I32)

        def oh_lo(u):
            return oh_raw[0:TN, u * 128:(u + 1) * 128]

        def oh_hi(u):
            return oh_raw[0:TN, 512 + u * 3 * ST:512 + (u + 1) * 3 * ST].rearrange("p (k s) -> p k s", k=3)

        def oh_src(u):
            return oh_raw[:, u * 313:(u + 1) * 313].bitcast(BF16)

        def oh_dst(u):
            return oh_raw[:, 1252 + u * 63:1252 + (u + 1) * 63].bitcast(BF16)

        def oh_dst32(u):
            return oh_raw[:, u * TN:(u + 1) * TN]

        so = {}
        at = 0
        for nm, n in (("src", EJ), ("dst", EJ), ("dt", EJ), ("dl", EJ), ("ind", 5 * EJ), ("incl", 5 * EJ),
                      ("excl", 5 * EJ), ("mask", 5 * EJ), ("tot", 5), ("base", 5), ("pos", EJ), ("part", 5 * EJ),
                      ("hi", EJ), ("lo", EJ), ("posi", EJ), ("hii", EJ), ("loi", EJ), ("nti", 5), ("ntf", 5),
                      ("incl5", 5), ("ts", 5), ("one5", 5), ("kio", ST), ("tmf", ST), ("tmp", ST), ("ew", EJ),
                      ("tri", TN)):
            so[nm] = (at, n)
            at += n
        assert at <= 3904

        def sv(nm, p=TN):
            o, n = so[nm]
            return RG[5][0:p, o:o + n]

        def sv5(nm):
            return sv(nm).rearrange("p (c j) -> p c j", c=5)

        srcdst = RG[6][0:TN, 3200:3200 + 2 * EJ].bitcast(I32)
        edge_w1 = RG[6][0:32, 3400:3400 + FF]
        small = RG[6][:, 3600:3904]

        def col(name, k, p=128):
            return cols[0:p, PL[name][0] + k:PL[name][0] + k + 1]

        PANELS = [("W_ah", a["W_ah"], 0, D, 128), ("Wv", a["W_qkv"], 2 * D, D, 128),
                  ("Wq", a["W_qkv"], 0, D, 128), ("Wk", a["W_qkv"], D, D, 128), ("Wproj", a["W_proj"], 0, D, 128)]
        for i in range(3):
            PANELS += [(f"W{i}", a[f"W{i}"], 0, D, 128), (f"Wout{i}", a["W_out"][i * D:(i + 1) * D, :], 0, D, 128)]
        PANELS += [("ffn1", a["ffn_W1"], 0, 3 * FF, 128), ("ffn2", a["ffn_W2"], 0, D, 96)]
        if stop != "L0":
            PANELS += [(f"Wt{t}", a["W_type"][t * D:(t + 1) * D, :], 0, D, 128) for t in range(TYPES)]
            PANELS += [("msgU", a["msg_W1"][0:D, :], 0, D, 128), ("msgV", a["msg_W1"][D:2 * D, :], 0, D, 128),
                       ("msg2", a["msg_W2"], 0, D, 128), ("agg1", a["agg_W1"], 0, D, 128),
                       ("agg2", a["agg_W2"], 0, D, 128), ("outW", a["out_W"], 0, D, 128),
                       ("Wv1", a["qkv1_w"], 2 * D, D, 128), ("Wq1", a["qkv1_w"], 0, D, 128),
                       ("Wk1", a["qkv1_w"], D, D, 128), ("Wproj1", a["proj1_w"], 0, D, 128),
                       ("moe1a", a["moe_w1"], 0, D, 128), ("moe1b", a["moe_w1"], D, D, 128),
                       ("moe2a", a["moe_w2"][0:D, :], 0, D, 128), ("moe2b", a["moe_w2"][D:2 * D, :], 0, D, 128)]
        pindex = {p[0]: i for i, p in enumerate(PANELS)}
        panel_last = {}

        def weights(eng, name, c):
            q = 2 * pindex[name] + c // 3
            eng.wait_ge(sem(f"weights_loaded{q % 5}"), 16 * (q // 5 + 1))
            return ring[q % 5][:, c % 3, :]

        ROWS = row_order()

        def row(eng, name):
            k = ROWS.index(name)
            eng.wait_ge(sem(f"row_loaded{k % 3}"), 16 * (k // 3 + 1))
            return rowbuf[k % 3][0:TN, :]

        def row5(eng, name):
            return row(eng, name).unsqueeze(1).broadcast_to([TN, NT, D])

        def eqk(which, odd):
            o = (2 * which + odd) * NP
            return RG[7][:, o:o + NP]

        def qp(b):
            return RG[8][:, b * 2 * NP:(b + 1) * 2 * NP].rearrange("p (m n) -> p m n", m=2)

        def kp(b):
            return RG[8 - b][0:TN, 4 * NP - 0:4 * NP + NT * RF].rearrange("p (t m) -> p t m", t=NT)

        def qk1(which, b):
            o = (2 * which + b) * NP
            return RG[4][:, o:o + NP]
        hid = [RG[7][0:96, u * 1000:(u + 1) * 1000].rearrange("p (m n) -> p m n", m=2) for u in range(3)]
        w1s = RG[3][:, 0:C * FF].rearrange("p (c f) -> p c f", c=C)
        w2s = RG[3][0:96, C * FF:C * FF + 2 * D].rearrange("p (c n) -> p c n", c=2)
        b2s = RG[3][0:TN, 2688:2688 + D]
        fh = RG[4][0:96, 0:2 * NP].rearrange("p (m n) -> p m n", m=2)
        neg = RG[7][0:TN, 0:1565].bitcast(BF16)[:, 0:NT * N].rearrange("p (t n) -> p t n", t=NT)
        lsum = sb("lsum", [128, C])
        gsm = sb("gsm", [128, 32])
        P_REGION = [8, 0]
        masks = RG[4][:, 0:1884].bitcast(BF16).rearrange("p (t n) -> p t n", t=TYPES)
        typed = [RG[4][:, 1884 + u * NP:1884 + (u + 1) * NP] for u in range(2)]
        types_i = RG[4][:, 3200:3200 + NP].bitcast(I32)
        ug = [RG[5][:, u * D:(u + 1) * D] for u in range(2)]
        vg = [RG[5][:, (2 + u) * D:(3 + u) * D] for u in range(2)]
        msg = [RG[6][:, u * 770:(u + 1) * 770] for u in range(2)]
        S4 = RG[7][0:TN, 0:NT * 770].rearrange("p (t b n) -> p t b n", t=NT, b=2)
        ewsum = RG[8][0:1, 0:NP]
        msg_b2 = RG[8][0:1, 640:640 + D]
        sel = RG[6][0:EXPERTS, 640:640 + 2 * D]
        gT = RG[6][0:EXPERTS, 0:NP]
        silu = [RG[5][:, u * NP:(u + 1) * NP] for u in range(2)]
        gate_v = RG[8][0:TN, 0:NT * EXPERTS * 5].rearrange("p (k t e) -> p k t e", k=5, t=NT)
        top_v = RG[8][0:TN, 240:240 + NT * 8].rearrange("p (t e) -> p t e", t=NT)
        gq = RG[8][0:TN, 300:300 + 4 * NT].rearrange("p (k t) -> p k t", k=4)

        u_dram = nc.dram_tensor("msg_source_part", [N, D], F32, kind="Internal").ap()
        v_dram = nc.dram_tensor("msg_target_part", [N, D], F32, kind="Internal").ap()
        acc_dram = nc.dram_tensor("layer0_sum", [N, D], F32, kind="Internal").ap()

        count_base = []
        scatter_base = []

        block = ctx.enter_context(nc.Block())

        @block.tensor
        def _(pe):
            def transposes(name, src, ready=None, count=0, chunks=C):
                for c in range(chunks):
                    ps, full = psum.open(pe, f"{name}{c}")
                    if ready is not None:
                        pe.wait_ge(ready, count)
                    for t in range(NT):
                        last = pe.transpose(ps[:, t * 128:t * 128 + TN], src(t, c), ident[0:TN, 0:TN])
                    last.then_inc(full, 1)

            def linear_T(name, panel, xT, parts=C, outer=None):
                for m in range(parts):
                    ps, full = psum.open(pe, f"{name}{m}")
                    for c in range(C):
                        w = weights(pe, panel, c)
                        for h in range(2):
                            last = pe.matmul(ps[:, 512 * h:512 * h + HN], w[:, m * 128:(m + 1) * 128],
                                             xT[:, c, h * HN:(h + 1) * HN], start=(c == 0),
                                             stop=(c == C - 1 and outer is None))
                    if outer is not None:
                        for h in range(2):
                            last = pe.matmul(ps[:, 512 * h:512 * h + HN], outer[0][:, m * 128:(m + 1) * 128],
                                             outer[1][:, h * HN:(h + 1) * HN], start=False, stop=True)
                    last.then_inc(full, 1)
                panel_last[panel] = f"{name}{parts - 1}"

            def linear_R(name, panels, chunk):
                n = C * len(panels)
                for t in range(NT):
                    ps, full = psum.open(pe, f"{name}{t}")
                    for c in range(n):
                        w = weights(pe, panels[c // C], c % C)
                        for h in range(2):
                            last = pe.matmul(ps[0:TN, 512 * h:512 * h + 384], chunk(c)[:, t * TN:(t + 1) * TN],
                                             w[:, h * 384:(h + 1) * 384], start=(c == 0), stop=(c == n - 1))
                    last.then_inc(full, 1)
                for p in panels:
                    panel_last[p] = f"{name}{NT - 1}"

            def chunk_of(r):
                return lambda c: asT(r)[:, c, :]

            def of_R(r):
                return lambda t, c: asR(r)[:, t, c * 128:(c + 1) * 128]

            pe.wait_ge(sem("consts"), 2)
            pe.wait_ge(sem("small_loads"), 16 * 5)
            logit, logit_full = psum.open(pe, "edge_logit")

            def hidden(s):
                n = min(EC, E - s * EC)
                pe.wait_ge(sem(f"attr_loaded{s % 4}"), 16 * (s // 4 + 1))
                ps, full = psum.tiles[1 + s % 3], psum.full[1 + s % 3]
                if s >= 3:
                    pe.wait_ge(psum.free[1 + s % 3], s // 3)
                for m in range(2):
                    last = pe.matmul(ps[0:96, 512 * m:512 * m + n], edge_w1[:, m * 96:(m + 1) * 96],
                                     RG[8][0:32, (s % 4) * EC:(s % 4) * EC + n], start=True, stop=True)
                last.then_inc(full, 1)

            def logits(s):
                pe.wait_ge(psum.free[1 + s % 3], s // 3 + 1)
                for j in range(s * 4, min(s * 4 + 4, EJ)):
                    for m in range(2):
                        last = pe.matmul(logit[0:TN, j:j + 1], hid[s % 3][:, m, (j - s * 4) * TN:(j - s * 4 + 1) * TN],
                                         col("edge_w2", m, 96), start=(m == 0), stop=(m == 1))
                last.then_inc(logit_full if s == ES - 1 else sem("hidden_used"), 1)
            hidden(0)
            hidden(1)
            for s in range(ES):
                if s + 2 < ES:
                    hidden(s + 2)
                logits(s)
            for u in range(3):
                uses = len(range(u, ES, 3))
                psum.filled[1 + u] += uses
                psum.freed[1 + u] += uses
            psum.opened = 4

            ps, full = psum.open(pe, "rank")
            pe.wait_ge(sem("rank_totals"), 1)
            pe.matmul(ps[0:TN, 0:NT], sv("tri"), sv("tot"), start=True, stop=True)
            pe.matmul(ps[:, 512:512 + NT], one[0:TN, :].broadcast_to([TN, 128]), sv("tot"),
                      start=True, stop=True).then_inc(full, 1)

            transposes("xnT", of_R(1), sem("normed"), 1)
            psum.drained(pe, *[f"xnT{c}" for c in range(C)])
            linear_T("x1T", "W_ah", asT(2))
            linear_R("V", ["Wv"], chunk_of(2))

            ps, full = psum.open(pe, "sorted")

            def permute(j, u, first=False, final=False):
                pe.wait_ge(sem("onehot_edge"), j + 1)
                return pe.matmul(ps[:, 0:3 * ST], oh_lo(u), oh_raw[0:TN, 512 + u * 3 * ST:512 + (u + 1) * 3 * ST],
                                 start=first, stop=final, skip_group_check=True)
            for u in range(4):
                permute(u, u, first=(u == 0)).then_inc(sem("onehot_used"), 1)
            with pe.Fori(1, EJ // 4) as i:
                for u in range(4):
                    permute(4 * i + u, u).then_inc(sem("onehot_used"), 1)
            permute(EJ - 1, 0, final=True).then_inc(full, 1)

            psum.align()
            count_base.append((list(psum.filled), list(psum.freed)))
            with pe.Fori(0, ST // 4) as i:
                for u in range(4):
                    pe.wait_ge(psum.free[u], i + count_base[0][1][u])
                    pe.wait_ge(sem("onehot_dst"), 4 * i + u + 1)
                    for t in range(NT):
                        last = pe.matmul(psum.tiles[u][0:TN, t * 128:t * 128 + TN],
                                         oh_src(u)[:, t * TN:(t + 1) * TN], oh_dst(u)[:, 0:TN], start=True, stop=True)
                    last.then_inc(psum.full[u], 1)
            psum.looped("counts", ST // 4)

            def mix0_chunk(c):
                for nm, panel in (("q", "Wq"), ("k", "Wk")):
                    ps, full = psum.open(pe, f"{nm}{c}", 2)
                    for k in range(C):
                        w = weights(pe, panel, k)
                        for h in range(2):
                            last = pe.matmul(ps[:, 512 * h:512 * h + HN], w[:, c * 128:(c + 1) * 128],
                                             asT(2)[:, k, h * HN:(h + 1) * HN], start=(k == 0), stop=(k == C - 1))
                    last.then_inc(full, 1)
                    panel_last[panel] = f"{nm}{c}"

            def mix0_features(h):
                c, odd = h // 2, h % 2
                rf = rfo if odd else rfe
                for m in range(2):
                    ps, full = psum.open(pe, f"qp{h}_{m}")
                    if m == 0:
                        pe.wait_ge(sem("squares"), 4 * (c + 1))
                    for x in range(2):
                        last = pe.matmul(ps[:, 512 * x:512 * x + HN], rf[:, m * 128:(m + 1) * 128],
                                         eqk(0, odd)[:, x * HN:(x + 1) * HN], start=True, stop=True)
                    last.then_inc(full, 1)
                for part, tiles in (("a", range(4)), ("b", range(4, 5))):
                    ps, full = psum.open(pe, f"kp{h}{part}")
                    for t in tiles:
                        last = pe.matmul(ps[0:TN, (t % 4) * RF:(t % 4 + 1) * RF], eqk(1, odd)[:, t * TN:(t + 1) * TN],
                                         rf[:, :], start=True, stop=True)
                    last.then_inc(full, 1)

            def mix0_out(h):
                b = h % 2
                ps, full = psum.open(pe, f"kv{h}")
                psum.drained(pe, f"kp{h}a", f"kp{h}b", *([f"V{t}" for t in range(NT)] if h == 0 else []))
                for m in range(2):
                    for t in range(NT):
                        last = pe.matmul(ps[:, 512 * m:512 * m + 65], kp(b)[:, t, m * 128:(m + 1) * 128],
                                         asV(4)[:, t, h, :], start=(t == 0), stop=(t == NT - 1))
                last.then_inc(full, 1)
                ps, full = psum.open(pe, f"mo{h}")
                psum.drained(pe, f"kv{h}", f"qp{h}_0", f"qp{h}_1")
                for t in range(NT):
                    for m in range(2):
                        last = pe.matmul(ps[0:TN, t * 65:(t + 1) * 65], qp(b)[:, m, t * TN:(t + 1) * TN],
                                         kvs[:, b, m, :], start=(m == 0), stop=(m == 1))
                last.then_inc(full, 1)

            for c in range(C):
                mix0_chunk(c)
                mix0_features(2 * c)
                if c:
                    mix0_out(2 * c - 1)
                mix0_features(2 * c + 1)
                mix0_out(2 * c)
            mix0_out(MH - 1)
            psum.drained(pe, f"mo{MH - 1}")
            transposes("moT", of_R(5))
            for t in range(NT):
                ps, full = psum.open(pe, f"A{t}")
                psum.drained(pe, *[f"counts{u}" for u in range(4)])
                for s in range(NT):
                    last = pe.transpose(ps[0:TN, s * 128:s * 128 + TN], asN(6)[:, s, t * TN:(t + 1) * TN],
                                        ident[0:TN, 0:TN])
                last.then_inc(full, 1)
            psum.drained(pe, *[f"moT{c}" for c in range(C)])
            linear_R("mp", ["Wproj"], chunk_of(8))

            for g in range(3):
                linear_R(f"h{g}_", [f"W{g}"], chunk_of(3))
                for hh in range(GH):
                    ps, full = psum.open(pe, f"asb{g}{hh}")
                    pe.wait_ge(sem("scores_src"), g + 1)
                    for t in range(NT):
                        last = pe.matmul(ps[0:TN, t * 128:t * 128 + TN],
                                         asd[0:TN, 0, t, hh:hh + 1].broadcast_to([TN, TN]),
                                         ident[0:TN, 0:TN], start=True, stop=True)
                    last.then_inc(full, 1)

                def offsets(hh):
                    for k in range(2):
                        ps, full = psum.open(pe, f"off{g}{hh}{k}", NT)
                        pe.wait_ge(sem("offsets"), 2 * (g + 1))
                        for t in range(NT):
                            last = pe.matmul(ps[0:TN, t * 128:t * 128 + TN],
                                             asd[0:TN, 5 + k, t, hh:hh + 1].broadcast_to([TN, TN]),
                                             ident[0:TN, 0:TN], start=True, stop=True)
                        last.then_inc(full, 1)

                def attend(hh):
                    P = asN(P_REGION[hh % 2])
                    for part, tiles in (("a", range(4)), ("b", range(4, 5))):
                        ps, full = psum.open(pe, f"gat{g}{hh}{part}")
                        pe.wait_ge(sem("attention"), NT * (GH * g + hh + 1))
                        for t in tiles:
                            for s in range(NT):
                                last = pe.matmul(ps[0:TN, (t % 4) * 256:(t % 4) * 256 + 193],
                                                 P[:, s, t * TN:(t + 1) * TN], asG(4)[:, s, hh, :],
                                                 start=(s == 0), stop=(s == NT - 1))
                        last.then_inc(full, 1)
                offsets(0)
                offsets(1)
                for hh in range(GH):
                    attend(hh)
                    if hh + 2 < GH:
                        offsets(hh + 2)
                for c in range(C):
                    ps, full = psum.open(pe, f"embT{g}_{c}")
                    if c == 0:
                        psum.drained(pe, f"gat{g}{GH - 1}a", f"gat{g}{GH - 1}b")
                    for t in range(NT):
                        last = pe.transpose(ps[:, t * 128:t * 128 + TN], asR(5)[:, t, c * 128:(c + 1) * 128],
                                            ident[0:TN, 0:TN])
                    last.then_inc(full, 1)
                psum.drained(pe, *[f"embT{g}_{c}" for c in range(C)])
                linear_R(f"wo{g}_", [f"Wout{g}"], chunk_of(2))

            transposes("xlT", of_R(5), sem("normed"), 2)
            ps, full = psum.open(pe, "gate")
            psum.drained(pe, *[f"xlT{c}" for c in range(C)])
            pe.wait_ge(sem("sums"), 1)
            for c in range(C):
                last = pe.matmul(ps[:, 0:3], lsum[:, c:c + 1].broadcast_to([128, 128]),
                                 cols[:, PL["wg"][0] + 3 * c:PL["wg"][0] + 3 * c + 3], start=(c == 0), stop=(c == C - 1))
            last.then_inc(full, 1)
            pe.wait_ge(sem("chosen"), 1)
            for m in range(2):
                ps, full = psum.open(pe, f"f1_{m}")
                for c in range(C):
                    for h in range(2):
                        last = pe.matmul(ps[0:96, 512 * h:512 * h + HN], w1s[:, c, m * 96:(m + 1) * 96],
                                         asT(2)[:, c, h * HN:(h + 1) * HN], start=(c == 0), stop=(c == C - 1))
                last.then_inc(full, 1)
            for t in range(NT):
                ps, full = psum.open(pe, f"f2_{t}")
                if t == 0:
                    psum.drained(pe, "f1_0", "f1_1")
                for m in range(2):
                    for h in range(2):
                        last = pe.matmul(ps[0:TN, 512 * h:512 * h + 384], fh[:, m, t * TN:(t + 1) * TN],
                                         w2s[:, m, h * 384:(h + 1) * 384], start=(m == 0), stop=(m == 1))
                last.then_inc(full, 1)
            if stop == "L0":
                return

            transposes("x1nT", of_R(1), sem("normed"), 3)
            psum.drained(pe, *[f"x1nT{c}" for c in range(C)])
            for t in range(TYPES):
                linear_T(f"ty{t}_", f"Wt{t}", asT(2))
            pe.wait_ge(sem("typed"), C * (TYPES - 1))
            linear_R("U", ["msgU"], chunk_of(3))
            linear_R("Vm", ["msgV"], chunk_of(3))
            psum.align()
            scatter_base.append((list(psum.filled), list(psum.freed)))
            with pe.Fori(0, ST // 4) as i:
                for u in range(4):
                    pe.wait_ge(psum.free[u], i + scatter_base[0][1][u])
                    pe.wait_ge(sem("messages"), 4 * i + u + 1)
                    pe.wait_ge(sem("onehot_dst1"), 4 * i + u + 1)
                    for b in range(2):
                        last = pe.matmul(psum.tiles[u][0:TN, 512 * b:512 * b + 385], oh_dst32(u),
                                         msg[u % 2][:, 385 * b:385 * (b + 1)], start=True, stop=True)
                    last.then_inc(psum.full[u], 1)
            psum.looped("scattered", ST // 4)
            psum.drained(pe, *[f"scattered{u}" for u in range(4)])
            transposes("ST", lambda t, c: S4[:, t, c // 3, (c % 3) * 128:(c % 3 + 1) * 128])
            ps, full = psum.open(pe, "ewT")
            for t in range(NT):
                last = pe.transpose(ps[0:1, t * 128:t * 128 + TN], S4[:, t, 0, 384:385], ident[0:TN, 0:TN])
            last.then_inc(full, 1)
            psum.drained(pe, *[f"ST{c}" for c in range(C)], "ewT")
            pe.wait_ge(sem("msg_b2"), 16)
            linear_T("m2_", "msg2", asT(4), outer=(msg_b2, ewsum))
            psum.drained(pe, *[f"m2_{c}" for c in range(C)])
            linear_T("a1_", "agg1", asT(5))
            psum.drained(pe, *[f"a1_{c}" for c in range(C)])
            linear_T("a2_", "agg2", asT(6))
            psum.drained(pe, *[f"a2_{c}" for c in range(C)])
            linear_R("o_", ["outW"], chunk_of(3))

            linear_R("V1", ["Wv1"], chunk_of(2))

            def mix1_chunk(c):
                for nm, panel in (("q1_", "Wq1"), ("k1_", "Wk1")):
                    ps, full = psum.open(pe, f"{nm}{c}")
                    for k in range(C):
                        w = weights(pe, panel, k)
                        for h in range(2):
                            last = pe.matmul(ps[:, 512 * h:512 * h + HN], w[:, c * 128:(c + 1) * 128],
                                             asT(2)[:, k, h * HN:(h + 1) * HN], start=(k == 0), stop=(k == C - 1))
                    last.then_inc(full, 1)
                    panel_last[panel] = f"{nm}{c}"

            def mix1_scores(h):
                c, o = h // 2, 64 * (h % 2)
                for s in range(NT):
                    ps, full = psum.open(pe, f"sc{h}_{s}")
                    if s == 0:
                        psum.drained(pe, f"q1_{c}", f"k1_{c}")
                    for x in range(2):
                        last = pe.matmul(ps[0:TN, 512 * x:512 * x + HN], qk1(1, c % 2)[o:o + 64, s * TN:(s + 1) * TN],
                                         qk1(0, c % 2)[o:o + 64, x * HN:(x + 1) * HN], start=True, stop=True)
                    last.then_inc(full, 1)

            def mix1_out(h):
                P = asN(5 + h % 2, NP)
                ps, full = psum.open(pe, f"ao{h}")
                psum.drained(pe, *[f"sc{h}_{s}" for s in range(NT)], *([f"V1{t}" for t in range(NT)] if h == 0 else []))
                for t in range(NT):
                    for s in range(NT):
                        last = pe.matmul(ps[0:TN, t * 65:(t + 1) * 65], P[:, s, t * TN:(t + 1) * TN],
                                         asV(3)[:, s, h, :], start=(s == 0), stop=(s == NT - 1))
                last.then_inc(full, 1)
            for h in range(MH):
                if h % 2 == 0:
                    mix1_chunk(h // 2)
                mix1_scores(h)
                if h:
                    mix1_out(h - 1)
            mix1_out(MH - 1)
            psum.drained(pe, f"ao{MH - 1}")
            transposes("aoT", of_R(7))
            psum.drained(pe, *[f"aoT{c}" for c in range(C)])
            linear_R("p1_", ["Wproj1"], chunk_of(8))

            transposes("tokT", of_R(7), sem("tokens"), 1)
            ps, full = psum.open(pe, "router")
            psum.drained(pe, *[f"tokT{c}" for c in range(C)])
            for t in range(NT):
                for c in range(C):
                    last = pe.matmul(ps[0:TN, t * 8:t * 8 + 8], asT(2)[:, c, t * TN:(t + 1) * TN],
                                     cols[:, PL["rw"][0] + 8 * c:PL["rw"][0] + 8 * c + 8],
                                     start=(c == 0), stop=(c == C - 1))
            last.then_inc(full, 1)

            def up(j):
                ps, full = psum.open(pe, f"up{j}")
                for c in range(C):
                    w = weights(pe, "moe1a" if j < C else "moe1b", c)
                    for h in range(2):
                        last = pe.matmul(ps[:, 512 * h:512 * h + HN], w[:, (j % C) * 128:(j % C + 1) * 128],
                                         asT(2)[:, c, h * HN:(h + 1) * HN], start=(c == 0), stop=(c == C - 1))
                last.then_inc(full, 1)

            def gates_of(j):
                ps, full = psum.open(pe, f"gb{j}")
                for h in range(2):
                    last = pe.matmul(ps[:, 512 * h:512 * h + HN], sel[:, j * 128:(j + 1) * 128],
                                     gT[:, h * HN:(h + 1) * HN], start=True, stop=True)
                last.then_inc(full, 1)
            up(0)
            ps, full = psum.open(pe, "gT")
            pe.wait_ge(sem("gates"), 1)
            for t in range(NT):
                last = pe.transpose(ps[0:EXPERTS, t * 128:t * 128 + TN], gate_v[:, 3, t, :], ident[0:TN, 0:TN])
            last.then_inc(full, 1)
            psum.drained(pe, "gT")
            pe.wait_ge(sem("sel"), 3)
            for j in range(12):
                gates_of(j)
                if j + 1 < 12:
                    up(j + 1)
            panel_last["moe1a"], panel_last["moe1b"] = "up5", "up11"
            psum.drained(pe, *[f"gb{j}" for j in range(12)])
            linear_R("y_", ["moe2a", "moe2b"], lambda c: asT(3 + c // C)[:, c % C, :])

        @block.sync
        def _(sp):
            def attr(s):
                if s >= 4:
                    sp.wait_ge(psum.full[1 + (s - 4) % 3], (s - 4) // 3 + 1)
                n = min(EC, E - s * EC)
                sp.dma_start(RG[8][0:32, (s % 4) * EC:(s % 4) * EC + n], a["attrT"][:, s * EC:s * EC + n])\
                  .then_inc(sem(f"attr_loaded{s % 4}"), 16)

            def half(q):
                name, w, c0, n, p = PANELS[q // 2]
                if q >= 5:
                    prev = PANELS[(q - 5) // 2][0]
                    if prev in panel_last:
                        psum.computed(sp, panel_last[prev])
                    else:
                        sp.wait_ge(sem("chosen"), 1)
                src = w.rearrange("(c p) n -> p c n", p=p)[:, 3 * (q % 2):3 * (q % 2) + 3, c0:c0 + n]
                sp.dma_start(ring[q % 5][0:p, :, 0:n], src).then_inc(sem(f"weights_loaded{q % 5}"), 16)

            def load_row(k):
                if k >= 3:
                    sp.wait_ge(sem("row_used"), k - 2)
                sp.dma_start(rowbuf[k % 3][0:TN, :], a["rows"][k:k + 1, :].broadcast_to([TN, D]))\
                  .then_inc(sem(f"row_loaded{k % 3}"), 16)

            sp.dma_start(srcdst, a["srcdst"]).then_inc(sem("edges_loaded"), 16)
            for s in range(4):
                attr(s)
            sp.dma_start(asR(0), a["x"].rearrange("(t p) d -> p t d", p=TN)).then_inc(sem("x_loaded"), 16)
            for q in range(5):
                half(q)
            for k in range(3):
                load_row(k)
            for s in range(4, ES):
                attr(s)
            behind = {"W0": [3, 4, 5], "Wout0": [6, 7], "Wout1": [8, 9], "W2": [10, 11], "ffn1": [12],
                      "Wt0": [13, 14, 15], "msg2": [16], "outW": [17], "Wv1": [18], "Wq1": [19]}
            for q in range(5, 2 * len(PANELS)):
                half(q)
                if q % 2:
                    for k in behind.get(PANELS[q // 2][0], []):
                        load_row(k)
            if stop == "L0":
                sp.wait_ge(sem("final"), 1)
                sp.dma_start(a["out"].rearrange("(t p) d -> p t d", p=TN), asR(0)).then_inc(sem("stored"), 16)
                sp.wait_ge(sem("stored"), 16)
                return
            for t in range(NT):
                psum.drained(sp, f"y_{t}")
                sp.dma_start(a["out"][t * TN:(t + 1) * TN, :], asR(0)[:, t, :]).then_inc(sem("stored"), 16)
            sp.wait_ge(sem("stored"), 16 * NT)

        @block.scalar
        def _(act):
            A = act.activation

            def root(k):
                act.wait_ge(sem("ln_inverse"), k)
                A(lnt[0:TN, 2, :], lnt[0:TN, 1, :], ACT.Sqrt).then_inc(sem("ln_root"), 1)

            act.dma_start(cols[:, :], a["cols"]).then_inc(sem("small_loads"), 16)
            act.dma_start(edge_w1, a["edge_W1"]).then_inc(sem("small_loads"), 16)
            act.dma_start(eb2[:, :], a["edge_b2"].broadcast_to([128, 1])).then_inc(sem("small_loads"), 16)
            act.dma_start(rfe[0:64, :], a["rfT"]).then_inc(sem("small_loads"), 16)
            act.dma_start(rfo[64:128, :], a["rfT"]).then_inc(sem("small_loads"), 16)
            act.wait_ge(sem("small_loads"), 16 * 5)

            for s in range(ES):
                n = min(EC, E - s * EC)
                u = s % 3
                act.wait_ge(psum.full[1 + u], s // 3 + 1)
                if s >= 3:
                    act.wait_ge(sem("hidden_used"), s - 2)
                for m in range(2):
                    last = A(hid[u][:, m, 0:n], psum.tiles[1 + u][0:96, 512 * m:512 * m + n], ACT.Relu,
                             bias=col("edge_b1", m, 96))
                last.then_inc(psum.free[1 + u], 1)
                if s == 10:
                    root(1)
            ps, free = psum.computed(act, "edge_logit")
            A(sv("ew"), ps[0:TN, 0:EJ], ACT.Sigmoid, bias=eb2[0:TN, :]).then_inc(free, 1)

            def turned(name, r, func=ACT.Identity, bias=None, sums=None):
                for c in range(C):
                    ps, free = psum.computed(act, f"{name}{c}")
                    dst = asT(r)[:, c, 0:N].rearrange("p (t n) -> p t n", t=NT)
                    kw = {"bias": col(bias, c)} if bias else {}
                    if sums is not None:
                        kw["accum_out"] = sums[:, c:c + 1]
                    A(dst, blocks(ps, 128), func, **kw).then_inc(free, 1)

            turned("xnT", 2)
            for m in range(C):
                ps, free = psum.computed(act, f"x1T{m}")
                A(two(asT(3)[:, m, :]), halves(ps, HN, 0, 128), ACT.Relu, bias=col("b_ah", m)).then_inc(free, 1)

            def values(name, r):
                for t in range(NT):
                    ps, free = psum.computed(act, f"{name}{t}")
                    A(asV(r)[:, t, :, 0:64].rearrange("p (b h) d -> p b h d", b=2),
                      halves(ps, 384).rearrange("p b (h d) -> p b h d", h=6), ACT.Identity).then_inc(free, 1)
            values("V", 4)

            def squares(c):
                for k, nm in enumerate(("q", "k")):
                    psum.drained(act, f"{nm}{c}")
                    A(eqk(k, 0)[64:128, :], eqk(k, 0)[0:64, :], ACT.Square).then_inc(sem("squares"), 1)
                    A(eqk(k, 1)[0:64, :], eqk(k, 1)[64:128, :], ACT.Square).then_inc(sem("squares"), 1)

            def features(h):
                b = h % 2
                if h >= 2:
                    psum.computed(act, f"mo{h - 2}")
                for m in range(2):
                    ps, free = psum.computed(act, f"qp{h}_{m}")
                    A(two(qp(b)[:, m, :]), halves(ps, HN, 0, 128), ACT.Exp).then_inc(free, 1)
                ps, free = psum.computed(act, f"kp{h}a")
                A(kp(b)[:, 0:4, :], ps[0:TN, :].rearrange("p (t m) -> p t m", t=4), ACT.Exp).then_inc(free, 1)
                ps, free = psum.computed(act, f"kp{h}b")
                A(kp(b)[:, 4, :], ps[0:TN, 0:RF], ACT.Exp).then_inc(free, 1)
            for c in range(C):
                squares(c)
                features(2 * c)
                features(2 * c + 1)
            psum.computed(act, f"mo{MH - 1}")
            turned("moT", 8)
            root(2)

            for g in range(3):
                if g:
                    psum.computed(act, f"gat{g - 1}{GH - 1}b")
                for t in range(NT):
                    ps, free = psum.computed(act, f"h{g}_{t}")
                    A(asG(4)[:, t, :, 0:GC].rearrange("p (b h) d -> p b h d", b=2),
                      halves(ps, 384).rearrange("p b (h d) -> p b h d", h=2), ACT.Identity).then_inc(free, 1)

                def weights_of(hh):
                    P = asN(P_REGION[hh % 2])
                    if hh >= 2:
                        psum.computed(act, f"gat{g}{hh - 2}b")
                    elif g:
                        psum.computed(act, f"gat{g - 1}{hh + 2}b")
                    elif hh == 0:
                        psum.computed(act, "mp4")
                    else:
                        act.wait_ge(sem("sum_spilled"), 16)
                    ps, free = psum.computed(act, f"off{g}{hh}1")
                    for s in range(NT + 1):
                        if s < NT:
                            A(P[:, s, :].rearrange("p (t n) -> p t n", t=NT), blocks(ps), ACT.Identity,
                              bias=asd[0:TN, 7, s, hh:hh + 1]).then_inc(free, 1)
                        if s:
                            psum.reads(act, f"off{g}{hh}0", s, NT)
                            A(P[:, s - 1, :], P[:, s - 1, :], ACT.Exp).then_inc(sem("exped"), 1)

                def normalised(hh):
                    for k, (part, tiles) in enumerate((("a", range(4)), ("b", range(4, 5)))):
                        ps, free = psum.computed(act, f"gat{g}{hh}{part}")
                        act.wait_ge(sem("row_inverse"), 2 * (GH * g + hh) + k + 1)
                        if hh == 0 and k == 0:
                            psum.computed(act, f"embT{g - 1}_5" if g else "moT5")
                        for t in tiles:
                            last = A(asR(5)[:, t, hh * GC:(hh + 1) * GC], ps[0:TN, (t % 4) * 256:(t % 4) * 256 + GC],
                                     ACT.Copy, scale=rden[0:TN, 2 * (hh % 2) + 1, t:t + 1])
                        last.then_inc(free, 1)
                weights_of(0)
                weights_of(1)
                for hh in range(GH):
                    normalised(hh)
                    if hh + 2 < GH:
                        weights_of(hh + 2)
                psum.computed(act, f"wo{g - 1}_4" if g else "k5")
                turned(f"embT{g}_", 2, ACT.Relu, f"b{g}")

            root(3)
            psum.computed(act, "wo2_4")
            turned("xlT", 2, sums=lsum)
            act.wait_ge(sem("gate_shifted"), 1)
            A(gsm[:, 3:6], gsm[:, 0:3], ACT.Exp).then_inc(sem("gate_exp"), 1)
            act.wait_ge(sem("chosen"), 1)
            for m in range(2):
                ps, free = psum.computed(act, f"f1_{m}")
                A(two(fh[:, m, :]), halves(ps, HN, 0, 96), ACT.Gelu, bias=gsm[0:96, 29 + m:30 + m]).then_inc(free, 1)
            if stop == "L0":
                return

            root(4)
            psum.computed(act, "f1_1")
            turned("x1nT", 2)
            psum.computed(act, "xlT5")
            for nm, r in (("U", 5), ("Vm", 6)):
                for t in range(NT):
                    ps, free = psum.computed(act, f"{nm}{t}")
                    A(two(asR(r)[:, t, :]), halves(ps, 384), ACT.Identity).then_inc(free, 1)
            full0 = scatter_base[0][0]
            with act.Fori(0, ST // 4) as i:
                for u in range(4):
                    j = 4 * i + u
                    act.wait_ge(sem("edge_sum"), j + 1)
                    act.wait_ge(psum.full[(u + 2) % 4], i + full0[(u + 2) % 4] + (1 if u >= 2 else 0))
                    dst = msg[u % 2].rearrange("p (b n) -> p b n", b=2)
                    w = slots[:, 2, bass.ds(j, 1)]
                    A(dst[:, :, 0:384], two(ug[u % 2]), ACT.Relu, scale=w)
                    A(dst[:, :, 384:385], w.unsqueeze(1).broadcast_to([128, 2, 1]), ACT.Identity)\
                        .then_inc(sem("messages"), 1)
            turned("ST", 4)
            ps, free = psum.computed(act, "ewT")
            A(ewsum[:, 0:N].rearrange("p (t n) -> p t n", t=NT), blocks(ps, 1), ACT.Identity).then_inc(free, 1)
            for m in range(C):
                ps, free = psum.computed(act, f"m2_{m}")
                A(two(asT(5)[:, m, :]), halves(ps, HN, 0, 128), ACT.Identity).then_inc(free, 1)
            for m in range(C):
                ps, free = psum.computed(act, f"a1_{m}")
                A(two(asT(6)[:, m, :]), halves(ps, HN, 0, 128), ACT.Relu, bias=col("agg_b1", m)).then_inc(free, 1)
            psum.computed(act, "o_4")
            root(5)
            values("V1", 3)
            two_col = gsm[:, 31:32]
            for h in range(MH):
                c = h // 2
                if h % 2 == 0:
                    ps, free = psum.computed(act, f"q1_{c}")
                    psum.computed(act, f"sc{2 * c - 3}_4" if c >= 2 else "m2_5")
                    A(two(qk1(0, c % 2)), halves(ps, HN, 0, 128), ACT.Identity).then_inc(free, 1)
                psum.computed(act, f"ao{h - 2}" if h >= 2 else f"a{h + 1}_5")
                for s in range(NT):
                    ps, free = psum.computed(act, f"sc{h}_{s}")
                    A(two(asN(5 + h % 2, NP)[:, s, :]), halves(ps, HN), ACT.Relu, bias=two_col[0:TN, :],
                      scale=0.0625).then_inc(free, 1)
            turned("aoT", 8)
            root(6)
            root(7)
            psum.computed(act, "k1_5")
            turned("tokT", 2)
            act.wait_ge(sem("router_shifted"), 1)
            A(gate_v[:, 1], gate_v[:, 0], ACT.Exp).then_inc(sem("router_exp"), 1)
            for j in range(12):
                ps, free = psum.computed(act, f"up{j}")
                if j >= 2:
                    psum.drained(act, f"gb{j - 2}")
                A(two(silu[j % 2]), halves(ps, HN, 0, 128), ACT.Silu).then_inc(free, 1)
                if j == 0:
                    ps, free = psum.computed(act, "gT")
                    A(gT[:, 0:N].rearrange("p (t n) -> p t n", t=NT), blocks(ps, EXPERTS), ACT.Identity)\
                        .then_inc(free, 1)

        @block.gpsimd
        def _(pool):
            pool.memset(ident[:, :], 0.0).then_inc(sem("pool_memset"), 1)
            pool.memset(sv("tri"), 1.0).then_inc(sem("pool_memset"), 1)
            pool.iota(sv("kio", 128), pattern=[[1, ST]], base=0, channel_multiplier=0,
                      allow_small_or_imprecise_dtypes=True).then_inc(sem("iotas"), 1)
            pool.iota(iota_n[:, :], pattern=[[1, N + 1]], base=0, channel_multiplier=0,
                      allow_small_or_imprecise_dtypes=True).then_inc(sem("iotas"), 1)
            pool.wait_ge(sem("pool_memset"), 2)
            pool.affine_select(out=ident[:, :], in_=ident[:, :], compare_op=ALU.not_equal, fill=1.0, base=0,
                               pattern=[[-1, 128]], channel_multiplier=1).then_inc(sem("consts"), 1)
            pool.affine_select(out=sv("tri"), in_=sv("tri"), compare_op=ALU.is_gt, fill=0.0, base=0,
                               pattern=[[1, TN]], channel_multiplier=-1).then_inc(sem("iotas"), 1)
            pool.iota(gsm[:, 26:29], pattern=[[-1, 3]], base=3, channel_multiplier=0,
                      allow_small_or_imprecise_dtypes=True).then_inc(sem("iotas"), 1)

            pool.wait_ge(sem("sum0"), 1)
            pool.dma_start(acc_dram.rearrange("(t p) d -> p t d", p=TN), asR(0)).then_inc(sem("sum_spilled"), 16)
            for g in range(3):
                for hh in range(GH):
                    P = asN(P_REGION[hh % 2])
                    for s in range(NT):
                        n = NT * (GH * g + hh) + s
                        pool.wait_ge(sem("exped"), n + 1)
                        pool.tensor_tensor(P[:, s, :], P[:, s, :], asN(6)[:, s, :], ALU.mult)\
                            .then_inc(sem("attention"), 1)
            psum.computed(pool, "gat23b")
            pool.wait_ge(sem("sum_spilled"), 16)
            pool.dma_start(asR(0), acc_dram.rearrange("(t p) d -> p t d", p=TN)).then_inc(sem("sum_back"), 16)
            if stop == "L0":
                return

            psum.computed(pool, "f2_4")
            pool.dma_start(types_i[:, 0:N], a["types"].broadcast_to([128, N])).then_inc(sem("types_loaded"), 16)
            pool.dma_start(msg_b2, a["msg_b2"]).then_inc(sem("msg_b2"), 16)
            for n in range(C * (TYPES - 1)):
                m = n % C
                pool.wait_ge(sem("typed_part"), n + 1)
                pool.tensor_tensor(asT(3)[:, m, :], asT(3)[:, m, :], typed[n % 2], ALU.add)\
                    .then_inc(sem("typed"), 1)
            psum.drained(pool, *[f"U{t}" for t in range(NT)])
            pool.dma_start(u_dram.rearrange("(t p) d -> p t d", p=TN), asR(5)).then_inc(sem("parts_stored"), 16)
            pool.wait_ge(sem("row_used"), ROWS.index("msg_b1") + 1)
            pool.dma_start(v_dram.rearrange("(t p) d -> p t d", p=TN), asR(6)).then_inc(sem("parts_stored"), 16)
            pool.wait_ge(sem("parts_stored"), 32)

            def gather(j, u, wait):
                b = u % 2
                if wait:
                    pool.wait_ge(sem("messages"), j - 1)
                pool.tensor_copy(idx[:, b, :], rows_i[:, :, bass.ds(j, 1)].rearrange("p k o -> p (k o)"))\
                    .then_inc(sem("indices"), 1)
                pool.wait_ge(sem("indices"), j + 1)
                pool.sem_inc(sem("gathers_begun"), 1)
                for dst, src, k in ((ug[b], u_dram, 0), (vg[b], v_dram, 1)):
                    pool.indirect_dma_start(out=dst, out_offset=None, in_=src,
                                            in_offset=bass.IndirectOffsetOnAxis(ap=idx[:, b, k:k + 1], axis=0))\
                        .then_inc(sem(f"gathered{b}"), 16)
            for u in range(4):
                gather(u, u, u >= 2)
            with pool.Fori(1, ST // 4) as i:
                for u in range(4):
                    gather(4 * i + u, u, True)

            psum.computed(pool, "ao11")
            pool.memset(sel, 1.0).then_inc(sem("sel"), 1)
            pool.wait_ge(sem("sel"), 1)
            pool.affine_select(out=sel, in_=sel, compare_op=ALU.is_ge, fill=0.0, base=0, pattern=[[1, 2 * D]],
                               channel_multiplier=-FF).then_inc(sem("sel"), 1)
            pool.wait_ge(sem("sel"), 2)
            pool.affine_select(out=sel, in_=sel, compare_op=ALU.is_ge, fill=0.0, base=FF - 1, pattern=[[-1, 2 * D]],
                               channel_multiplier=FF).then_inc(sem("sel"), 1)

        @block.vector
        def _(dve):
            steps = [0]

            def link(ins):
                steps[0] += 1
                ins.then_inc(sem("dve_step"), 1)
                dve.wait_ge(sem("dve_step"), steps[0])

            def statistics(src, k):
                for t in range(NT):
                    for b in range(2):
                        last = dve.bn_stats(stats[0:TN, t, b, :], src[:, t, b * 384:(b + 1) * 384])
                link(last)
                for t in range(NT):
                    last = dve.bn_aggr(mv[0:TN, t, :], stats[0:TN, t, :, :].rearrange("p b s -> p (b s)"))
                link(last)
                r = lnt[0:TN, :, :]
                link(dve.tensor_scalar(r[:, 0, :], mv[0:TN, :, 1], 1e-5, None, ALU.add))
                dve.reciprocal(r[:, 1, :], r[:, 0, :]).then_inc(sem("ln_inverse"), 1)
                dve.wait_ge(sem("ln_root"), k)
                link(dve.tensor_tensor(r[:, 3, :], r[:, 2, :], r[:, 2, :], ALU.mult))
                link(dve.tensor_tensor(r[:, 3, :], r[:, 3, :], r[:, 0, :], ALU.mult))
                link(dve.tensor_scalar(r[:, 3, :], r[:, 3, :], -0.5, 1.5, ALU.mult, ALU.add))
                link(dve.tensor_tensor(r[:, 3, :], r[:, 3, :], r[:, 2, :], ALU.mult))

            def normalise(src, dst, k):
                statistics(src, k)
                for t in range(NT):
                    last = dve.tensor_scalar(dst[:, t, :], src[:, t, :], mv[0:TN, t, 0:1], lnt[0:TN, 3, t:t + 1],
                                             ALU.subtract, ALU.mult)
                return last

            dve.memset(one[:, :], 1.0)
            dve.memset(sv("mask"), 1.0)
            dve.memset(sv("one5", 128), 1.0)
            dve.memset(rfe[64:128, :], -0.5)
            dve.memset(rfo[0:64, :], -0.5)
            dve.memset(gsm[:, 31:32], 2.0)
            dve.memset(asT(2)[:, :, N:NP], 0.0)
            link(dve.memset(asV(4)[:, :, :, 64:65], 1.0))
            dve.memset(sv5("mask")[:, :, 0:1], 0.0).then_inc(sem("consts"), 1)

            dve.wait_ge(sem("edges_loaded"), 16)
            dve.wait_ge(sem("consts"), 2)
            dve.wait_ge(sem("iotas"), 4)
            dve.tensor_copy(sv("src"), srcdst[:, 0:EJ])
            link(dve.tensor_copy(sv("dst"), srcdst[:, EJ:2 * EJ]))
            link(dve.tensor_scalar(sv("dt"), sv("dst"), float(TN), None, ALU.is_ge))
            for c in range(2, NT):
                link(dve.scalar_tensor_tensor(sv("dt"), sv("dst"), float(c * TN), sv("dt"), ALU.is_ge, ALU.add))
            link(dve.scalar_tensor_tensor(sv("dl"), sv("dt"), -float(TN), sv("dst"), ALU.mult, ALU.add))
            link(dve.tensor_scalar(sv("dl"), sv("dl"), 1.0, None, ALU.add))
            for c in range(NT):
                last = dve.tensor_scalar(sv5("ind")[:, c, :], sv("dt"), float(c), None, ALU.is_equal)
            link(last)
            link(dve.tensor_tensor_scan(sv("incl"), sv("mask"), sv("ind"), 0.0, ALU.mult, ALU.add))
            link(dve.tensor_tensor(sv("excl"), sv("incl"), sv("ind"), ALU.subtract))
            dve.tensor_copy(sv("tot"), sv5("incl")[:, :, EJ - 1]).then_inc(sem("rank_totals"), 1)

            dve.wait_ge(sem("x_loaded"), 16)
            normalise(asR(0), asR(1), 1).then_inc(sem("normed"), 1)

            ps, free = psum.computed(dve, "rank")
            dve.wait_ge(sem("iotas"), 4)
            nti, posi = sv("nti", 128).bitcast(I32), sv("posi").bitcast(I32)
            hii, loi = sv("hii").bitcast(I32), sv("loi").bitcast(I32)
            link(dve.tensor_scalar(nti, ps[:, 512:512 + NT], 127.0, None, ALU.add))
            link(dve.tensor_scalar(nti, nti, 7, None, ALU.arith_shift_right))
            link(dve.tensor_copy(sv("ntf", 128), nti))
            link(dve.tensor_tensor_scan(sv("incl5", 128), sv("one5", 128), sv("ntf", 128), 0.0, ALU.mult, ALU.add))
            link(dve.tensor_tensor(sv("ts", 128), sv("incl5", 128), sv("ntf", 128), ALU.subtract))
            dve.scalar_tensor_tensor(sv("base"), sv("ts"), 128.0, ps[0:TN, 0:NT], ALU.mult, ALU.add)\
               .then_inc(free, 1)
            psum.drained(dve, "rank")
            link(dve.tensor_tensor(sv5("part"), sv5("excl"), sv("base").unsqueeze(2).broadcast_to([TN, NT, EJ]),
                                   ALU.add))
            link(dve.tensor_tensor(sv("part"), sv("part"), sv("ind"), ALU.mult))
            link(dve.tensor_reduce(sv("pos"), sv5("part").rearrange("p c j -> p j c"), AX.X, ALU.add))
            link(dve.tensor_copy(posi, sv("pos")))
            link(dve.tensor_scalar(hii, posi, 7, None, ALU.arith_shift_right))
            link(dve.tensor_scalar(loi, posi, 127, None, ALU.bitwise_and))
            link(dve.tensor_copy(sv("hi"), hii))
            dve.tensor_copy(sv("lo"), loi).then_inc(sem("places"), 1)
            link(dve.tensor_scalar(sv("tmf", 128), sv("kio", 128), sv("ts", 128)[:, 1:2], None, ALU.is_ge))
            for c in range(2, NT):
                link(dve.scalar_tensor_tensor(sv("tmf", 128), sv("kio", 128), sv("ts", 128)[:, c:c + 1],
                                              sv("tmf", 128), ALU.is_ge, ALU.add))
            link(dve.tensor_copy(tmap[:, :], sv("tmf", 128)))

            psum.drained(dve, "edge_logit")

            def place(j, u):
                for k, nm in enumerate(("src", "dl", "ew")):
                    dve.tensor_scalar(oh_hi(u)[:, k, :], sv("kio"), sv("hi")[:, bass.ds(j, 1)],
                                             sv(nm)[:, bass.ds(j, 1)], ALU.is_equal, ALU.mult)
                dve.tensor_scalar(oh_lo(u), iota_n[0:TN, 0:128], sv("lo")[:, bass.ds(j, 1)], None,
                                  ALU.is_equal).then_inc(sem("onehot_edge"), 1)
            for j in range(4):
                place(j, j)
            with dve.Fori(1, EJ // 4) as i:
                for u in range(4):
                    dve.wait_ge(sem("onehot_used"), 4 * i + u - 3)
                    place(4 * i + u, u)
            dve.wait_ge(sem("onehot_used"), EJ - 4)
            place(EJ - 1, 0)
            link(dve.memset(asN(6), 0.0))
            for t in range(NT):
                last = dve.tensor_copy(asN(6)[:, t, t * TN:(t + 1) * TN], ident[0:TN, 0:TN])
            link(last)
            ps, free = psum.computed(dve, "sorted")
            dve.tensor_copy(slots[:, :, :].rearrange("p k s -> p (k s)"), ps[:, 0:3 * ST]).then_inc(free, 1)
            psum.drained(dve, "sorted")
            dve.tensor_copy(rows_i[:, 0, :], slots[:, 0, :])
            link(dve.scalar_tensor_tensor(sv("tmp", 128), sv("tmf", 128), float(TN), slots[:, 1, :], ALU.mult, ALU.add))
            dve.tensor_scalar(rows_i[:, 1, :], sv("tmp", 128), -1.0, 0.0, ALU.add, ALU.max)\
               .then_inc(sem("slots_ready"), 1)
            dve.wait_ge(sem("slots_ready"), 1)

            def target(j, i, u, dst, full0, name, sources=None):
                dve.wait_ge(psum.full[u], i + full0[u])
                if sources is not None:
                    dve.tensor_scalar(sources, iota_n[:, 0:N], slots[:, 0, bass.ds(j, 1)], None, ALU.is_equal)
                dve.tensor_scalar(dst, iota_n[:, 1:TN + 1], slots[:, 1, bass.ds(j, 1)], None, ALU.is_equal)\
                   .then_inc(sem(name), 1)

            def tile_of(j):
                return dve.value_load(tmap[0:1, bass.ds(j, 1)], min_val=0, max_val=NT - 1)

            def add_tile(i, u, v, base, dst, src):
                dve.wait_ge(psum.full[u], i + (base[0][u] + 1))
                w = (u - 1) % 4
                dve.wait_ge(psum.free[w], i + (base[1][w] + (1 if u else 0)))
                dve.tensor_tensor(dst(v), dst(v), src(u), ALU.add).then_inc(psum.free[u], 1)

            AT = asN(6).rearrange("p t (v n) -> p t v n", v=NT)

            def count_dst(v):
                return AT[:, :, bass.ds(v, 1), :]

            def count_src(u):
                return blocks(psum.tiles[u]).unsqueeze(2)
            base = count_base[0]
            v = [tile_of(j) for j in range(2)]
            for u in range(4):
                target(u, 0, u, oh_dst(u)[:, 0:TN], base[0], "onehot_dst",
                       oh_src(u)[:, 0:N])
                if u >= 2:
                    add_tile(0, u - 2, v[u - 2], base, count_dst, count_src)
            with dve.Fori(1, ST // 4) as i:
                v = [tile_of(4 * i + k - 2) for k in range(4)]
                for u in range(4):
                    target(4 * i + u, i, u, oh_dst(u)[:, 0:TN], base[0], "onehot_dst",
                       oh_src(u)[:, 0:N])
                    add_tile(i if u >= 2 else i - 1, (u - 2) % 4, v[u], base, count_dst, count_src)
            v = [tile_of(j) for j in range(ST - 2, ST)]
            for u in range(2):
                add_tile(ST // 4 - 1, 2 + u, v[u], base, count_dst, count_src)

            def copies(c):
                for k, nm in enumerate(("q", "k")):
                    ps, free = psum.computed(dve, f"{nm}{c}")
                    if c:
                        psum.computed(dve, f"kp{2 * c - 1}b")
                    dve.tensor_copy(two(eqk(k, 0)[0:64, :]), halves(ps, HN, 0, 64)).then_inc(free, 1)
                    dve.tensor_copy(two(eqk(k, 1)[64:128, :]), halves(ps, HN, 64, 128)).then_inc(free, 1)

            def head_out(name, h, eps, dst, widths=65):
                ps, free = psum.computed(dve, name)
                v = ps[0:TN, 0:NT * 65].rearrange("p (t d) -> p t d", t=NT)
                r = rden[0:TN, :, :]
                link(dve.tensor_scalar(r[:, 0, :], v[:, :, 64], eps, None, ALU.add))
                link(dve.reciprocal(r[:, 1, :], r[:, 0, :]))
                dve.tensor_tensor(dst[:, :, h * 64:(h + 1) * 64], v[:, :, 0:64],
                                  r[:, 1, :].unsqueeze(2).broadcast_to([TN, NT, 64]), ALU.mult).then_inc(free, 1)

            def mix0_head(h):
                ps, free = psum.computed(dve, f"kv{h}")
                if h >= 2:
                    psum.computed(dve, f"mo{h - 2}")
                dve.tensor_copy(kvs[:, h % 2, :, :], halves(ps, 65, 0, 128)).then_inc(free, 1)
                head_out(f"mo{h}", h, 256e-6, asR(5))
            for c in range(C):
                copies(c)
                if c:
                    mix0_head(2 * c - 1)
                mix0_head(2 * c)
            mix0_head(MH - 1)
            for t in range(NT):
                ps, free = psum.computed(dve, f"A{t}")
                dve.tensor_scalar(neg[:, t, :].rearrange("p (s n) -> p s n", s=NT), blocks(ps), 0.0, NEG,
                                  ALU.is_equal, ALU.mult).then_inc(free, 1)
            dve.memset(asG(4)[:, :, :, GC:GC + 1], 1.0)
            dve.tensor_tensor(asR(1), asR(1), row5(dve, "mix_b_proj"), ALU.add).then_inc(sem("row_used"), 1)
            dve.wait_ge(sem("row_used"), 1)
            for t in range(NT):
                ps, free = psum.computed(dve, f"mp{t}")
                dve.tensor_tensor(two(asR(1)[:, t, :]), two(asR(1)[:, t, :]), halves(ps, 384), ALU.add)\
                   .then_inc(free, 1)
            psum.drained(dve, *[f"mp{t}" for t in range(NT)])
            link(normalise(asR(1), asR(1), 2))
            dve.tensor_tensor(asR(1), asR(1), row5(dve, "mix_gamma"), ALU.mult).then_inc(sem("row_used"), 1)
            dve.wait_ge(sem("row_used"), 2)
            dve.tensor_tensor(asR(1), asR(1), row5(dve, "mix_beta"), ALU.add).then_inc(sem("row_used"), 1)
            dve.wait_ge(sem("row_used"), 3)
            dve.tensor_tensor(asR(0), asR(0), asR(1), ALU.add).then_inc(sem("sum0"), 1)

            unread = oh_raw[0:TN, :].bitcast(BF16)
            s8 = asd[0:TN]
            for g in range(3):
                psum.drained(dve, *[f"h{g}_{t}" for t in range(NT)])
                for k, nm in enumerate(("a_src", "a_dst")):
                    r = row(dve, f"{nm}{g}")
                    for t in range(NT):
                        for hh in range(GH):
                            w = (GH * t + hh) % 16 * GC
                            last = dve.tensor_tensor_reduce(unread[:, w:w + GC], asG(4)[:, t, hh, 0:GC],
                                                            r[:, hh * GC:(hh + 1) * GC], 1.0, 0.0, ALU.mult, ALU.add,
                                                            s8[:, k, t, hh:hh + 1])
                        if t % 2:
                            link(last)
                    last.then_inc(sem("row_used"), 1)
                    dve.wait_ge(sem("row_used"), 4 + 2 * g + k)
                dve.tensor_scalar(s8[:, 7], s8[:, 0], 0.2, None, ALU.mult).then_inc(sem("scores_src"), 1)
                for hh in range(GH):
                    ps, free = psum.computed(dve, f"asb{g}{hh}")
                    if hh:
                        psum.drained(dve, f"asb{g}{hh - 1}")
                    for t in range(NT):
                        dst = unread[:, t * N:(t + 1) * N].rearrange("p (s n) -> p s n", s=NT)
                        last = dve.tensor_tensor_reduce(dst, blocks(ps),
                                                        neg[:, t, :].rearrange("p (s n) -> p s n", s=NT), 1.0,
                                                        3.0 * NEG, ALU.add, ALU.max, s8[:, 2, t, hh:hh + 1])
                    last.then_inc(free, 1)
                psum.drained(dve, *[f"asb{g}{hh}" for hh in range(GH)])
                link(dve.tensor_tensor(s8[:, 3], s8[:, 2], s8[:, 1], ALU.add))
                link(dve.scalar_tensor_tensor(s8[:, 4], s8[:, 3], 0.2, s8[:, 3], ALU.mult, ALU.max))
                dve.tensor_tensor(s8[:, 5], s8[:, 1], s8[:, 4], ALU.subtract).then_inc(sem("offsets"), 1)
                dve.scalar_tensor_tensor(s8[:, 6], s8[:, 1], 0.2, s8[:, 4], ALU.mult, ALU.subtract)\
                   .then_inc(sem("offsets"), 1)

                def weights_of(hh):
                    P = asN(P_REGION[hh % 2])
                    ps, free = psum.computed(dve, f"off{g}{hh}0")
                    for s in range(NT):
                        psum.reads(dve, f"off{g}{hh}1", s + 1, NT)
                        p = P[:, s, :].rearrange("p (t n) -> p t n", t=NT)
                        dve.scalar_tensor_tensor(p, blocks(ps), s8[:, 0, s, hh:hh + 1], p, ALU.add, ALU.max)\
                           .then_inc(free, 1)

                def denominators(hh):
                    b = 2 * (hh % 2)
                    for part, lo, hi in (("a", 0, 4), ("b", 4, 5)):
                        ps, free = psum.computed(dve, f"gat{g}{hh}{part}")
                        if hh >= 2:
                            psum.drained(dve, f"gat{g}{hh - 2}{part}")
                        link(dve.tensor_scalar(rden[0:TN, b, lo:hi],
                                               ps[0:TN, :].rearrange("p (t n) -> p t n", t=4)[:, 0:hi - lo, GC],
                                               1e-16, None, ALU.add))
                        dve.reciprocal(rden[0:TN, b + 1, lo:hi], rden[0:TN, b, lo:hi]).then_inc(sem("row_inverse"), 1)
                weights_of(0)
                weights_of(1)
                for hh in range(GH):
                    denominators(hh)
                    if hh + 2 < GH:
                        weights_of(hh + 2)
                for t in range(NT):
                    ps, free = psum.computed(dve, f"wo{g}_{t}")
                    dst = two(asR(1)[:, t, :])
                    if g == 0:
                        dve.tensor_copy(dst, halves(ps, 384)).then_inc(free, 1)
                    else:
                        dve.tensor_tensor(dst, dst, halves(ps, 384), ALU.add).then_inc(free, 1)
                psum.drained(dve, *[f"wo{g}_{t}" for t in range(NT)])
            dve.tensor_tensor(asR(1), asR(1), row5(dve, "gnn_b_out"), ALU.add).then_inc(sem("row_used"), 1)
            dve.wait_ge(sem("row_used"), 10)
            dve.wait_ge(sem("sum_back"), 16)
            link(dve.scalar_tensor_tensor(asR(0), asR(1), 0.0, asR(0), ALU.max, ALU.add))
            normalise(asR(0), asR(5), 3).then_inc(sem("normed"), 1)

            psum.drained(dve, *[f"xlT{c}" for c in range(C)])
            dve.sem_inc(sem("sums"), 1)
            ps, free = psum.computed(dve, "gate")
            G = gsm
            dve.tensor_scalar(G[:, 0:3], ps[:, 0:3], 1.0 / N, None, ALU.mult).then_inc(free, 1)
            psum.drained(dve, "gate")
            link(dve.tensor_reduce(G[:, 6:7], G[:, 0:3], AX.X, ALU.max))
            dve.tensor_scalar(G[:, 0:3], G[:, 0:3], G[:, 6:7], None, ALU.subtract).then_inc(sem("gate_shifted"), 1)
            dve.wait_ge(sem("gate_exp"), 1)
            link(dve.tensor_reduce(G[:, 8:9], G[:, 3:6], AX.X, ALU.add))
            link(dve.reciprocal(G[:, 9:10], G[:, 8:9]))
            link(dve.tensor_scalar(G[:, 10:13], G[:, 3:6], G[:, 9:10], None, ALU.mult))
            link(dve.tensor_reduce(G[:, 6:7], G[:, 10:13], AX.X, ALU.max))
            link(dve.scalar_tensor_tensor(G[:, 16:19], G[:, 10:13], G[:, 6:7], G[:, 26:29], ALU.is_equal, ALU.mult))
            link(dve.tensor_reduce(G[:, 19:20], G[:, 16:19], AX.X, ALU.max))
            link(dve.tensor_scalar(G[:, 20:23], G[:, 16:19], G[:, 19:20], None, ALU.is_equal))
            link(dve.tensor_tensor(G[:, 23:26], G[:, 20:23], G[:, 10:13], ALU.mult))
            for e in range(3):
                pick, score = G[:, 20 + e:21 + e], G[:, 23 + e:24 + e]

                def take(dst, src, w, p):
                    if e == 0:
                        return dve.tensor_scalar(dst, src, w[0:p, :], None, ALU.mult)
                    return dve.scalar_tensor_tensor(dst, src, w[0:p, :], dst, ALU.mult, ALU.add)
                for half in range(2):
                    weights(dve, "ffn1", 3 * half)
                    src = ring[(2 * pindex["ffn1"] + half) % 5][:, :, e * FF:(e + 1) * FF]
                    take(w1s[:, 3 * half:3 * half + 3, :], src, pick, 128)
                for m in range(2):
                    src = weights(dve, "ffn2", 2 * e + m)[0:96, :]
                    take(w2s[:, m, :], src, score, 96)
                link(take(gsm[0:96, 29:31], cols[0:96, PL["ffn_b1"][0] + 2 * e:PL["ffn_b1"][0] + 2 * e + 2], pick, 96))
                take(b2s, row(dve, f"ffn_b2_{e}"), score, TN).then_inc(sem("row_used"), 1)
                dve.wait_ge(sem("row_used"), 11 + e)
            dve.tensor_tensor(asR(0), asR(0), b2s.unsqueeze(1).broadcast_to([TN, NT, D]), ALU.add)\
               .then_inc(sem("chosen"), 1)
            dve.wait_ge(sem("chosen"), 1)
            for t in range(NT):
                ps, free = psum.computed(dve, f"f2_{t}")
                dst = two(asR(0)[:, t, :])
                dve.tensor_tensor(dst, dst, halves(ps, 384), ALU.add).then_inc(free, 1)
            psum.drained(dve, *[f"f2_{t}" for t in range(NT)])
            if stop == "L0":
                dve.sem_inc(sem("final"), 1)
                return

            normalise(asR(0), asR(1), 4).then_inc(sem("normed"), 1)
            link(dve.memset(types_i[:, N:NP], 0.0))
            dve.wait_ge(sem("types_loaded"), 16)
            for t in range(TYPES):
                last = dve.tensor_scalar(masks[:, t, :], types_i, float(t), None, ALU.is_equal)
            link(last)
            n = 0
            for t in range(TYPES):
                for m in range(C):
                    ps, free = psum.computed(dve, f"ty{t}_{m}")
                    dst = asT(3)[:, m, :] if t == 0 else typed[n % 2]
                    if t:
                        if n >= 2:
                            dve.wait_ge(sem("typed"), n - 1)
                        n += 1
                    dve.scalar_tensor_tensor(two(dst), halves(ps, HN, 0, 128), col("b_type", C * t + m),
                                             two(masks[:, t, :]), ALU.add, ALU.mult).then_inc(free, 1)
                    if t:
                        psum.drained(dve, f"ty{t}_{m}")
                        dve.sem_inc(sem("typed_part"), 1)
            dve.wait_ge(sem("typed"), C * (TYPES - 1))
            dve.memset(asT(4)[:, :, N:NP], 0.0)
            psum.computed(dve, "xlT5")
            link(dve.memset(S4, 0.0))
            link(dve.memset(ewsum[:, N:NP], 0.0))
            psum.drained(dve, *[f"Vm{t}" for t in range(NT)])
            dve.tensor_tensor(asR(6), asR(6), row5(dve, "msg_b1"), ALU.add).then_inc(sem("row_used"), 1)

            def sum_parts(j, i, u):
                dve.wait_ge(sem(f"gathered{u % 2}"), 64 * i + 32 * (u // 2 + 1))
                dve.tensor_tensor(ug[u % 2], ug[u % 2], vg[u % 2], ALU.add).then_inc(sem("edge_sum"), 1)

            def sum_dst(v):
                return S4[:, bass.ds(v, 1), :, :]

            def sum_src(u):
                return halves(psum.tiles[u], 385).unsqueeze(1)
            base = scatter_base[0]
            v = [tile_of(j) for j in range(2)]
            for u in range(4):
                sum_parts(u, 0, u)
                target(u, 0, u, oh_dst32(u), base[0], "onehot_dst1")
                if u >= 2:
                    add_tile(0, u - 2, v[u - 2], base, sum_dst, sum_src)
            with dve.Fori(1, ST // 4) as i:
                v = [tile_of(4 * i + k - 2) for k in range(4)]
                for u in range(4):
                    sum_parts(4 * i + u, i, u)
                    target(4 * i + u, i, u, oh_dst32(u), base[0], "onehot_dst1")
                    add_tile(i if u >= 2 else i - 1, (u - 2) % 4, v[u], base, sum_dst, sum_src)
            v = [tile_of(j) for j in range(ST - 2, ST)]
            for u in range(2):
                add_tile(ST // 4 - 1, 2 + u, v[u], base, sum_dst, sum_src)
            dve.tensor_tensor(asR(1), asR(1), row5(dve, "out_b"), ALU.add).then_inc(sem("row_used"), 1)
            for m in range(C):
                ps, free = psum.computed(dve, f"a2_{m}")
                dst = two(asT(3)[:, m, :])
                dve.scalar_tensor_tensor(dst, halves(ps, HN, 0, 128), col("agg_b2", m), dst, ALU.add, ALU.add)\
                   .then_inc(free, 1)
            dve.wait_ge(sem("row_used"), 15)
            for t in range(NT):
                ps, free = psum.computed(dve, f"o_{t}")
                dst = two(asR(1)[:, t, :])
                dve.tensor_tensor(dst, dst, halves(ps, 384), ALU.add).then_inc(free, 1)
            psum.drained(dve, *[f"o_{t}" for t in range(NT)])
            link(dve.memset(asV(3)[:, :, :, 64:65], 1.0))
            dve.sem_inc(sem("ones1"), 1)
            link(normalise(asR(1), asR(1), 5))
            dve.tensor_tensor(asR(1), asR(1), row5(dve, "ln_g"), ALU.mult).then_inc(sem("row_used"), 1)
            dve.wait_ge(sem("row_used"), 16)
            dve.tensor_tensor(asR(1), asR(1), row5(dve, "ln_b"), ALU.add).then_inc(sem("row_used"), 1)
            dve.wait_ge(sem("row_used"), 17)
            link(dve.tensor_tensor(asR(0), asR(0), asR(1), ALU.add))

            dve.tensor_tensor(asR(0), asR(0), row5(dve, "mix1_proj_b"), ALU.add).then_inc(sem("row_used"), 1)
            for h in range(MH):
                c = h // 2
                if h % 2 == 0:
                    ps, free = psum.computed(dve, f"k1_{c}")
                    psum.computed(dve, f"sc{2 * c - 3}_4" if c >= 2 else "m2_5")
                    dve.tensor_copy(two(qk1(1, c % 2)), halves(ps, HN, 0, 128)).then_inc(free, 1)
                if h:
                    head_out(f"ao{h - 1}", h - 1, 0.0, asR(7))
            head_out(f"ao{MH - 1}", MH - 1, 0.0, asR(7))
            dve.wait_ge(sem("row_used"), 18)
            for t in range(NT):
                ps, free = psum.computed(dve, f"p1_{t}")
                dst = two(asR(0)[:, t, :])
                dve.tensor_tensor(dst, dst, halves(ps, 384), ALU.add).then_inc(free, 1)
            psum.drained(dve, *[f"p1_{t}" for t in range(NT)])

            link(normalise(asR(0), asR(1), 6))
            link(dve.tensor_tensor(asR(0), asR(0), asR(1), ALU.add))
            link(normalise(asR(1), asR(7), 7))
            dve.tensor_tensor(asR(7), asR(7), row5(dve, "moe_g"), ALU.mult).then_inc(sem("row_used"), 1)
            dve.wait_ge(sem("row_used"), 19)
            dve.tensor_tensor(asR(7), asR(7), row5(dve, "moe_b"), ALU.add).then_inc(sem("tokens"), 1)
            dve.wait_ge(sem("tokens"), 1)
            ps, free = psum.computed(dve, "router")

            def wide(x):
                return x.unsqueeze(2).broadcast_to([TN, NT, EXPERTS])
            lg = ps[0:TN, 0:NT * EXPERTS].rearrange("p (t e) -> p t e", t=NT)
            link(dve.tensor_reduce(gq[:, 0, :], lg, AX.X, ALU.max))
            dve.tensor_tensor(gate_v[:, 0], lg, wide(gq[:, 0, :]), ALU.subtract).then_inc(free, 1)
            psum.drained(dve, "router")
            dve.sem_inc(sem("router_shifted"), 1)
            for e in range(EXPERTS):
                dve.memset(gate_v[:, 4, :, e:e + 1], float(EXPERTS - e))
            link(dve.memset(gT[:, N:NP], 0.0))
            dve.wait_ge(sem("router_exp"), 1)
            link(dve.tensor_reduce(gq[:, 1, :], gate_v[:, 1], AX.X, ALU.add))
            link(dve.reciprocal(gq[:, 2, :], gq[:, 1, :]))
            link(dve.tensor_tensor(gate_v[:, 1], gate_v[:, 1], wide(gq[:, 2, :]), ALU.mult))
            link(dve.tensor_copy(gate_v[:, 0], gate_v[:, 1]))
            for k in range(2):
                link(dve.tensor_reduce(gq[:, 0, :], gate_v[:, 0], AX.X, ALU.max))
                link(dve.tensor_tensor(gate_v[:, 2], gate_v[:, 0], wide(gq[:, 0, :]), ALU.is_equal))
                link(dve.tensor_tensor(gate_v[:, 2], gate_v[:, 2], gate_v[:, 4], ALU.mult))
                link(dve.tensor_reduce(gq[:, 1, :], gate_v[:, 2], AX.X, ALU.max))
                link(dve.tensor_tensor(gate_v[:, 2], gate_v[:, 2], wide(gq[:, 1, :]), ALU.is_equal))
                if k == 0:
                    link(dve.tensor_copy(gate_v[:, 3], gate_v[:, 2]))
                    link(dve.scalar_tensor_tensor(gate_v[:, 0], gate_v[:, 2], -2.0, gate_v[:, 0], ALU.mult, ALU.add))
                else:
                    link(dve.tensor_tensor(gate_v[:, 3], gate_v[:, 3], gate_v[:, 2], ALU.add))
            link(dve.tensor_tensor(gate_v[:, 3], gate_v[:, 3], gate_v[:, 1], ALU.mult))
            link(dve.tensor_reduce(gq[:, 1, :], gate_v[:, 3], AX.X, ALU.add))
            link(dve.reciprocal(gq[:, 2, :], gq[:, 1, :]))
            dve.tensor_tensor(gate_v[:, 3], gate_v[:, 3], wide(gq[:, 2, :]), ALU.mult).then_inc(sem("gates"), 1)
            psum.computed(dve, "ao11")
            for j in range(12):
                psum.drained(dve, f"up{j}")
                ps, free = psum.computed(dve, f"gb{j}")
                dve.tensor_tensor(two(asT(3 + j // C)[:, j % C, :]), two(silu[j % 2]), halves(ps, HN, 0, 128),
                                  ALU.mult).then_inc(free, 1)
            for t in range(NT):
                ps, free = psum.computed(dve, f"y_{t}")
                dst = two(asR(0)[:, t, :])
                dve.tensor_tensor(dst, dst, halves(ps, 384), ALU.add).then_inc(free, 1)


def kernel(**inputs):
    import numpy as np
    import concourse.bacc as bacc
    from concourse.bass_utils import run_bass_kernel_spmd as run

    v = {k: np.asarray(x) for k, x in inputs.items()}
    g0, m0, f0, g1 = "L0_gnn_", "L0_mix_", "L0_ffn_", "L1_gnn_"

    def chunks(x, p=128):
        x = x.reshape(-1, x.shape[-1] // p, p)
        return x.transpose(2, 0, 1).reshape(p, -1)

    parts = {"b_ah": chunks(v[g0 + "b_ah"]), "b0": chunks(v[g0 + "b0"]), "b1": chunks(v[g0 + "b1"]),
             "b2": chunks(v[g0 + "b2"]), "agg_b1": chunks(v[g1 + "agg_b1"]), "agg_b2": chunks(v[g1 + "agg_b2"]),
             "b_type": chunks(v[g1 + "b_type"]), "ffn_b1": chunks(v[f0 + "b1"], 96),
             "edge_b1": chunks(v[g1 + "edge_b1"], 96), "edge_w2": chunks(v[g1 + "edge_W2"].T, 96),
             "wg": v[f0 + "Wg"].T.reshape(C, 128, 3).transpose(1, 0, 2).reshape(128, 18),
             "rw": v["L1_ffn_router_w"].reshape(C, 128, 8).transpose(1, 0, 2).reshape(128, 48)}
    places = column_places()
    cols = np.zeros((128, places["all"][1]), np.float32)
    for name, x in parts.items():
        cols[0:x.shape[0], places[name][0]:places[name][0] + x.shape[1]] = x
    rows = [v[m0 + "b_proj"], v[m0 + "gamma"], v[m0 + "beta"]]
    for i in range(3):
        rows += [v[f"{g0}a_src{i}"].reshape(-1), v[f"{g0}a_dst{i}"].reshape(-1)]
    rows += [v[g0 + "b_out"], *v[f0 + "b2"], v[g1 + "msg_b1"], v[g1 + "out_b"], v[g1 + "ln_g"], v[g1 + "ln_b"],
             v["L1_mix_proj_b"], v["L1_ffn_ln_gamma"], v["L1_ffn_ln_beta"]]

    def flat(x):
        return x.transpose(1, 0, 2).reshape(x.shape[1], -1)
    arrays = {
        "x": v["x"], "srcdst": np.stack([v["src"].reshape(EJ, TN).T, v["dst"].reshape(EJ, TN).T], 1).reshape(TN, -1),
        "attrT": v["edge_attr_32"].T, "types": v["node_type_6"].reshape(1, N), "cols": cols, "rows": np.stack(rows),
        "W_ah": v[g0 + "W_ah"], "W0": v[g0 + "W0"], "W1": v[g0 + "W1"], "W2": v[g0 + "W2"], "W_out": v[g0 + "W_out"],
        "W_qkv": v[m0 + "W_qkv"], "W_proj": v[m0 + "W_proj"], "rfT": v[m0 + "random_features"].T,
        "ffn_W1": flat(v[f0 + "W1"]), "ffn_W2": v[f0 + "W2"].reshape(-1, D),
        "W_type": v[g1 + "W_type"].reshape(-1, D), "msg_W1": v[g1 + "msg_W1"], "msg_W2": v[g1 + "msg_W2"],
        "msg_b2": v[g1 + "msg_b2"].reshape(1, D), "edge_W1": v[g1 + "edge_W1"], "edge_b2": v[g1 + "edge_b2"].reshape(1, 1),
        "agg_W1": v[g1 + "agg_W1"], "agg_W2": v[g1 + "agg_W2"], "out_W": v[g1 + "out_W"],
        "qkv1_w": v["L1_mix_qkv_w"].T, "proj1_w": v["L1_mix_proj_w"].T,
        "moe_w1": flat(v["L1_ffn_w1"]), "moe_w2": v["L1_ffn_w2"].reshape(-1, D),
    }
    nc = bacc.Bacc("TRN2", target_bir_lowering=False, num_devices=1)
    aps, given = {}, {}
    for name, x in arrays.items():
        x = np.ascontiguousarray(x)
        given[f"in_{name}_dram"] = x
        aps[name] = nc.dram_tensor(f"in_{name}_dram", x.shape, mybir.dt.from_np(x.dtype), kind="ExternalInput").ap()
    aps["out"] = nc.dram_tensor("out_0_dram", (N, D), F32, kind="ExternalOutput").ap()
    gps_block(nc, aps)
    r = run(nc, [given], core_ids=[0])
    return r.results[0]["out_0_dram"]
```

```python
import concourse.bass as bass
from concourse import mybir
from contextlib import ExitStack

F32, BF16, F16, I32 = mybir.dt.float32, mybir.dt.bfloat16, mybir.dt.float16, mybir.dt.int32
ACT = mybir.ActivationFunctionType
ALU = mybir.AluOpType
AX = mybir.AxisListType

N = 625
TN, NT = 125, 5
D, C = 768, 6
NP, HN = 628, 314
E = 10625
EJ = 85
ST = 88
GH, GC = 4, 192
MH, MD = 12, 64
RF = 256
EC = 500
ES = -(-E // EC)
TYPES, EXPERTS, FF = 6, 8, 192
NEG = -1.0e30


def row_order():
    rows = ["mix_b_proj", "mix_gamma", "mix_beta"]
    for i in range(3):
        rows += [f"a_src{i}", f"a_dst{i}"]
    rows += ["gnn_b_out", "ffn_b2_0", "ffn_b2_1", "ffn_b2_2",
             "msg_b1", "mix1_proj_b", "out_b", "ln_g", "ln_b"]
    return rows


def column_places():
    at, out = 0, {}
    for name, n in (("b_ah", 6), ("b0", 6), ("b1", 6), ("b2", 6), ("agg_b1", 6), ("agg_b2", 6),
                    ("b_type", 36), ("ffn_b1", 6), ("edge_b1", 2), ("edge_w2", 2), ("wg", 18), ("rw", 48), ("moe_g", 6), ("moe_b", 6)):
        out[name] = (at, n)
        at += n
    out["all"] = (0, at)
    return out


class PsumRing:

    def __init__(self, nc, ctx):
        self.tiles = [ctx.enter_context(nc.psum_tensor(f"ps{i}", [128, 1024], F32)) for i in range(4)]
        self.full = [ctx.enter_context(nc.semaphore(f"psum_computed{i}")) for i in range(4)]
        self.free = [ctx.enter_context(nc.semaphore(f"psum_drained{i}")) for i in range(4)]
        self.filled, self.freed, self.opened, self.where = [0] * 4, [0] * 4, 0, {}

    def open(self, pe, name, reads=1):
        s = self.opened % 4
        self.opened += 1
        if self.freed[s]:
            pe.wait_ge(self.free[s], self.freed[s])
        self.freed[s] += reads
        self.filled[s] += 1
        assert name not in self.where, name
        self.where[name] = (s, self.filled[s], self.freed[s])
        return self.tiles[s], self.full[s]

    def align(self):
        while self.opened % 4:
            self.opened += 1

    def looped(self, name, times):
        for s in range(4):
            self.filled[s] += times
            self.freed[s] += times
            self.where[f"{name}{s}"] = (s, self.filled[s], self.freed[s])

    def computed(self, eng, name):
        s, n, _ = self.where[name]
        eng.wait_ge(self.full[s], n)
        return self.tiles[s], self.free[s]

    def reads(self, eng, name, k, total):
        s, _, n = self.where[name]
        eng.wait_ge(self.free[s], n - total + k)

    def drained(self, eng, *names):
        most = {}
        for name in names:
            s, _, n = self.where[name]
            most[s] = max(most.get(s, 0), n)
        for s, n in most.items():
            eng.wait_ge(self.free[s], n)



def gps_block(nc, a, stop=None):
    ctx = ExitStack()
    with ctx:
        def sb(name, shape, dt=F32):
            return ctx.enter_context(nc.sbuf_tensor(name, shape, dt))

        sems = {}

        def sem(name):
            if name not in sems:
                sems[name] = ctx.enter_context(nc.semaphore(name))
            return sems[name]

        psum = PsumRing(nc, ctx)
        ring = [sb(f"wring{i}", [128, 3, D]) for i in range(5)]
        RG = [sb(f"region{i}", [128, 3904]) for i in range(9)]
        rowbuf = [sb(f"rowbuf{i}", [128, D]) for i in range(3)]

        def asR(r):
            return RG[r][0:TN, 0:NT * D].rearrange("p (t d) -> p t d", t=NT)

        def asT(r):
            return RG[r][:, 0:C * NP].rearrange("p (c n) -> p c n", c=C)

        def asV(r):
            return RG[r][0:TN, 0:NT * MH * 65].rearrange("p (t h d) -> p t h d", t=NT, h=MH)

        def asG(r):
            return RG[r][0:TN, 0:NT * GH * 193].rearrange("p (t h d) -> p t h d", t=NT, h=GH)

        def asN(r, w=N):
            return RG[r][0:TN, 0:NT * w].rearrange("p (t n) -> p t n", t=NT)

        def blocks(ps, p=TN, w=125):
            return ps[0:p, 0:640].rearrange("p (t n) -> p t n", n=128)[:, :, 0:w]

        def halves(ps, n, lo=0, hi=TN):
            return ps[lo:hi, :].rearrange("p (b n) -> p b n", b=2)[:, :, 0:n]

        def two(x):
            return x.rearrange("p (b n) -> p b n", b=2)

        ident = sb("ident", [128, 128])
        one = sb("one", [128, 1])
        mix0_consts = sb("mix0_consts", [128, 2 * RF + 260])
        rfe, rfo = mix0_consts[:, 0:RF], mix0_consts[:, RF:2 * RF]
        kvs = mix0_consts[:, 2 * RF:2 * RF + 260].rearrange("p (b m d) -> p b m d", b=2, m=2)
        PL = column_places()
        cols = sb("cols", [128, PL["all"][1]])
        slots = sb("slots", [128, 3, ST])
        rows_i = sb("rows_i", [128, 2, ST], I32)
        tmap = sb("tmap", [128, ST], I32)
        iota_n = sb("iota_n", [128, N + 1], F16)
        oh_raw = sb("oh_raw", [128, 1696])
        stats = sb("stats", [128, NT, 2, 6])
        mv = sb("mv", [128, NT, 2])
        lnt = sb("lnt", [128, 4, NT])
        asd = sb("asd", [128, 8, NT, GH])
        rden = sb("rden", [128, 4, NT])
        eb2 = sb("eb2", [128, 1])

        def oh_lo(u):
            return oh_raw[0:TN, u * 128:(u + 1) * 128]

        def oh_hi(u):
            return oh_raw[0:TN, 512 + u * 3 * ST:512 + (u + 1) * 3 * ST].rearrange("p (k s) -> p k s", k=3)

        def oh_src(u):
            return oh_raw[:, u * 313:(u + 1) * 313].bitcast(BF16)

        def oh_dst(u):
            return oh_raw[:, 1252 + u * 63:1252 + (u + 1) * 63].bitcast(BF16)

        def oh_dst32(u):
            return oh_raw[:, u * TN:(u + 1) * TN]

        so = {}
        at = 0
        for nm, n in (("src", EJ), ("dl", EJ), ("ew", EJ), ("dst", EJ), ("dt", EJ), ("ind", 5 * EJ), ("incl", 5 * EJ),
                      ("excl", 5 * EJ), ("mask", 5 * EJ), ("tot", 5), ("base", 5), ("pos", EJ), ("part", 5 * EJ),
                      ("hi", EJ), ("lo", EJ), ("posi", EJ), ("hii", EJ), ("loi", EJ), ("nti", 5), ("ntf", 5),
                      ("incl5", 5), ("ts", 5), ("one5", 5), ("kio", ST), ("tmf", ST), ("tmp", ST),
                      ("tri", TN)):
            so[nm] = (at, n)
            at += n
        assert at <= 3904

        def sv(nm, p=TN):
            o, n = so[nm]
            return RG[5][0:p, o:o + n]

        def sv5(nm):
            return sv(nm).rearrange("p (c j) -> p c j", c=5)

        srcdst = RG[6][0:TN, 3200:3200 + 2 * EJ].bitcast(I32)
        edge_w1 = RG[6][0:32, 3400:3400 + FF]
        small = RG[6][:, 3600:3904]

        def col(name, k, p=128):
            return cols[0:p, PL[name][0] + k:PL[name][0] + k + 1]

        PANELS = [("W_ah", a["W_ah"], 0, D, 128), ("Wv", a["W_qkv"], 2 * D, D, 128),
                  ("Wq", a["W_qkv"], 0, D, 128), ("Wk", a["W_qkv"], D, D, 128), ("Wproj", a["W_proj"], 0, D, 128)]
        for i in range(3):
            PANELS += [(f"W{i}", a[f"W{i}"], 0, D, 128), (f"Wout{i}", a["W_out"][i * D:(i + 1) * D, :], 0, D, 128)]
        PANELS += [("ffn1", a["ffn_W1"], 0, 3 * FF, 128), ("ffn2", a["ffn_W2"], 0, D, 96)]
        if stop != "L0":
            PANELS += [(f"Wt{t}", a["W_type"][t * D:(t + 1) * D, :], 0, D, 128) for t in range(TYPES)]
            PANELS += [("msgU", a["msg_W1"][0:D, :], 0, D, 128), ("msgV", a["msg_W1"][D:2 * D, :], 0, D, 128),
                       ("Wv1", a["qkv1_w"], 2 * D, D, 128), ("Wq1", a["qkv1_w"], 0, D, 128),
                       ("Wk1", a["qkv1_w"], D, D, 128),
                       ("msg2", a["msg_W2"], 0, D, 128), ("agg1", a["agg_W1"], 0, D, 128),
                       ("agg2", a["agg_W2"], 0, D, 128), ("outW", a["out_W"], 0, D, 128),
                       ("Wproj1", a["proj1_w"], 0, D, 128),
                       ("moe1a", a["moe_w1"], 0, D, 128), ("moe1b", a["moe_w1"], D, D, 128),
                       ("moe2a", a["moe_w2"][0:D, :], 0, D, 128), ("moe2b", a["moe_w2"][D:2 * D, :], 0, D, 128)]
        pindex = {p[0]: i for i, p in enumerate(PANELS)}
        panel_last = {}

        def weights(eng, name, c):
            q = 2 * pindex[name] + c // 3
            eng.wait_ge(sem(f"weights_loaded{q % 5}"), 16 * (q // 5 + 1))
            return ring[q % 5][:, c % 3, :]

        ROWS = row_order()

        def row(eng, name):
            k = ROWS.index(name)
            eng.wait_ge(sem(f"row_loaded{k % 3}"), 16 * (k // 3 + 1))
            return rowbuf[k % 3][0:TN, :]

        def row5(eng, name):
            return row(eng, name).unsqueeze(1).broadcast_to([TN, NT, D])

        def eqk(which, odd):
            o = (2 * which + odd) * NP
            return RG[7][:, o:o + NP]

        def qp(b):
            return RG[8][:, b * 2 * NP:(b + 1) * 2 * NP].rearrange("p (m n) -> p m n", m=2)

        def kp(b):
            return RG[8 - b][0:TN, 4 * NP - 0:4 * NP + NT * RF].rearrange("p (t m) -> p t m", t=NT)

        def qk1(which, b):
            o = (2 * which + b) * NP
            return RG[4][:, o:o + NP]
        hid = [RG[7][0:96, u * 1000:(u + 1) * 1000].rearrange("p (m n) -> p m n", m=2) for u in range(3)]
        w1s = RG[3][:, 0:C * FF].rearrange("p (c f) -> p c f", c=C)
        w2s = RG[3][0:96, C * FF:C * FF + 2 * D].rearrange("p (c n) -> p c n", c=2)
        b2s = RG[3][0:TN, 2688:2688 + D]
        fh = RG[4][0:96, 0:2 * NP].rearrange("p (m n) -> p m n", m=2)
        neg = RG[7][0:TN, 0:1565].bitcast(BF16)[:, 0:NT * N].rearrange("p (t n) -> p t n", t=NT)
        lsum = sb("lsum", [128, C])
        gsm = sb("gsm", [128, 32])
        P_REGION = [8, 0]
        masks = RG[4][:, 0:1884].bitcast(BF16).rearrange("p (t n) -> p t n", t=TYPES)
        typed = [RG[4][:, 1884 + u * NP:1884 + (u + 1) * NP] for u in range(2)]
        types_i = RG[4][:, 3200:3200 + NP].bitcast(I32)
        msg = [RG[r][:, at:at + D] for r, at in ((4, 4 * NP), (5, NT * 626), (6, NT * 626))]
        msg += [oh_raw[:, 500:500 + D], mix0_consts[:, 0:D]]
        NM = len(msg)
        S4 = RG[7][0:TN, 0:NT * 770].rearrange("p (t b n) -> p t b n", t=NT, b=2)
        ewsum = RG[8][0:1, 0:NP]
        msg_b2 = RG[8][0:1, 640:640 + D]
        sel = RG[6][0:EXPERTS, 640:640 + 2 * D]
        gT = RG[6][0:EXPERTS, 0:NP]
        silu = [RG[5][:, u * NP:(u + 1) * NP] for u in range(2)]
        gate_v = RG[8][0:TN, 0:NT * EXPERTS * 5].rearrange("p (k t e) -> p k t e", k=5, t=NT)
        top_v = RG[8][0:TN, 240:240 + NT * 8].rearrange("p (t e) -> p t e", t=NT)
        gq = RG[8][0:TN, 300:300 + 4 * NT].rearrange("p (k t) -> p k t", k=4)

        u_dram = nc.dram_tensor("msg_source_part", [N, D], F32, kind="Internal").ap()
        v_dram = nc.dram_tensor("msg_target_part", [N, D], F32, kind="Internal").ap()
        typed_dram = nc.dram_tensor("typed_nodes", [128, C * NP], F32, kind="Internal").ap()
        acc_dram = nc.dram_tensor("layer0_sum", [N, D], F32, kind="Internal").ap()

        mixer1 = [("V1", t) for t in range(NT)]
        for h in range(MH):
            mixer1 += ([("q1_", h // 2), ("k1_", h // 2)] if h % 2 == 0 else []) + [(f"sc{h}_", s) for s in range(NT)]
            mixer1 += [("ao", h - 1)] if h else []
        mixer1.append(("ao", MH - 1))

        def tiles_behind(groups, k, first):
            j = k - first
            if k == len(groups) - 1:
                return range(j, ST)
            return range(j, j + 1) if 0 <= j < ST else range(0)

        mixer0 = []
        for c in range(C):
            def features_of(h):
                return [("qp", h, 0), ("qp", h, 1), ("kp", h, 0), ("kp", h, 1)]
            mixer0 += [("q", c, 0), ("k", c, 0)] + features_of(2 * c)
            if c:
                mixer0 += [("kv", 2 * c - 1, 0), ("mo", 2 * c - 1, 0)]
            mixer0 += features_of(2 * c + 1) + [("kv", 2 * c, 0), ("mo", 2 * c, 0)]
        mixer0 += [("kv", MH - 1, 0), ("mo", MH - 1, 0)]

        beside_edges = [("xnT", c) for c in range(C)] + [("x1T", m) for m in range(C)]
        FIRST_BESIDE = 5

        def behind_edges(s):
            k = s - FIRST_BESIDE
            return beside_edges[k:k + 1] if 0 <= k else []
        assert ES - FIRST_BESIDE >= len(beside_edges)


        block = ctx.enter_context(nc.Block())

        @block.tensor
        def _(pe):
            def transposes_part(name, src, c, ready=None, count=0):
                ps, full = psum.open(pe, f"{name}{c}")
                if ready is not None:
                    pe.wait_ge(ready, count)
                for t in range(NT):
                    last = pe.transpose(ps[:, t * 128:t * 128 + TN], src(t, c), ident[0:TN, 0:TN])
                last.then_inc(full, 1)

            def transposes(name, src, ready=None, count=0):
                for c in range(C):
                    transposes_part(name, src, c, ready, count)

            def linear_T(name, panel, xT, parts=C, outer=None):
                for m in range(parts):
                    ps, full = psum.open(pe, f"{name}{m}")
                    for c in range(C):
                        w = weights(pe, panel, c)
                        for h in range(2):
                            last = pe.matmul(ps[:, 512 * h:512 * h + HN], w[:, m * 128:(m + 1) * 128],
                                             xT[:, c, h * HN:(h + 1) * HN], start=(c == 0),
                                             stop=(c == C - 1 and outer is None))
                    if outer is not None:
                        for h in range(2):
                            last = pe.matmul(ps[:, 512 * h:512 * h + HN], outer[0][:, m * 128:(m + 1) * 128],
                                             outer[1][:, h * HN:(h + 1) * HN], start=False, stop=True)
                    last.then_inc(full, 1)
                panel_last[panel] = f"{name}{parts - 1}"

            def linear_R(name, panels, chunk):
                n = C * len(panels)
                for t in range(NT):
                    ps, full = psum.open(pe, f"{name}{t}")
                    for c in range(n):
                        w = weights(pe, panels[c // C], c % C)
                        for h in range(2):
                            last = pe.matmul(ps[0:TN, 512 * h:512 * h + 384], chunk(c)[:, t * TN:(t + 1) * TN],
                                             w[:, h * 384:(h + 1) * 384], start=(c == 0), stop=(c == n - 1))
                    last.then_inc(full, 1)
                for p in panels:
                    panel_last[p] = f"{name}{NT - 1}"

            def chunk_of(r):
                return lambda c: asT(r)[:, c, :]

            def of_R(r):
                return lambda t, c: asR(r)[:, t, c * 128:(c + 1) * 128]

            pe.wait_ge(sem("consts"), 2)
            pe.wait_ge(sem("small_loads"), 16 * 5)

            def hidden(s):
                n = min(EC, E - s * EC)
                ps, full = psum.open(pe, f"hidden{s}")
                pe.wait_ge(sem(f"attr_loaded{s % 4}"), 16 * (s // 4 + 1))
                for m in range(2):
                    last = pe.matmul(ps[0:96, 512 * m:512 * m + n], edge_w1[:, m * 96:(m + 1) * 96],
                                     RG[8][0:32, (s % 4) * EC:(s % 4) * EC + n], start=True, stop=True)
                last.then_inc(full, 1)

            def logits(s):
                ps, full = psum.open(pe, f"logits{s}")
                psum.drained(pe, f"hidden{s}")
                for j in range(s * 4, min(s * 4 + 4, EJ)):
                    for m in range(2):
                        last = pe.matmul(ps[0:TN, j - s * 4:j - s * 4 + 1],
                                         hid[s % 3][:, m, (j - s * 4) * TN:(j - s * 4 + 1) * TN],
                                         col("edge_w2", m, 96), start=(m == 0), stop=(m == 1))
                last.then_inc(full, 1)

            def ranks():
                ps, full = psum.open(pe, "rank")
                pe.wait_ge(sem("rank_totals"), 1)
                pe.matmul(ps[0:TN, 0:NT], sv("tri"), sv("tot"), start=True, stop=True)
                pe.matmul(ps[:, 512:512 + NT], one[0:TN, :].broadcast_to([TN, 128]), sv("tot"),
                          start=True, stop=True).then_inc(full, 1)

            def linear_T_part(name, panel, xT, m, reads=1):
                ps, full = psum.open(pe, f"{name}{m}", reads)
                for c in range(C):
                    w = weights(pe, panel, c)
                    for h in range(2):
                        last = pe.matmul(ps[:, 512 * h:512 * h + HN], w[:, m * 128:(m + 1) * 128],
                                         xT[:, c, h * HN:(h + 1) * HN], start=(c == 0), stop=(c == C - 1))
                last.then_inc(full, 1)
                panel_last[panel] = f"{name}{m}"
            hidden(0)
            hidden(1)
            for s in range(ES):
                if s + 2 < ES:
                    hidden(s + 2)
                logits(s)
                if s == FIRST_BESIDE - 1:
                    ranks()
                for nm, k in behind_edges(s):
                    if nm == "xnT":
                        transposes_part("xnT", of_R(1), k, sem("normed"), 1)
                    else:
                        if k == 0:
                            psum.drained(pe, *[f"xnT{c}" for c in range(C)])
                        linear_T_part("x1T", "W_ah", asT(2), k)
            linear_R("V", ["Wv"], chunk_of(2))

            ps, full = psum.open(pe, "sorted")

            def permute(j, u, first=False, final=False):
                pe.wait_ge(sem("onehot_edge"), j + 1)
                return pe.matmul(ps[:, 0:3 * ST], oh_lo(u), oh_raw[0:TN, 512 + u * 3 * ST:512 + (u + 1) * 3 * ST],
                                 start=first, stop=final, skip_group_check=True)
            for u in range(4):
                permute(u, u, first=(u == 0)).then_inc(sem("onehot_used"), 1)
            with pe.Fori(1, EJ // 4) as i:
                for u in range(4):
                    permute(4 * i + u, u).then_inc(sem("onehot_used"), 1)
            permute(EJ - 1, 0, final=True).then_inc(full, 1)

            def count_edges(j):
                ps, full = psum.open(pe, f"counts{j}")
                pe.wait_ge(sem("onehot_dst"), j + 1)
                for t in range(NT):
                    last = pe.matmul(ps[0:TN, t * 128:t * 128 + TN], oh_src(j % 4)[:, t * TN:(t + 1) * TN],
                                     oh_dst(j % 4)[:, 0:TN], start=True, stop=True)
                last.then_inc(full, 1)

            def mix0_query_features(h, m):
                c, odd = h // 2, h % 2
                ps, full = psum.open(pe, f"qp{h}_{m}")
                if m == 0:
                    pe.wait_ge(sem("squares"), 4 * (c + 1))
                for x in range(2):
                    last = pe.matmul(ps[:, 512 * x:512 * x + HN], (rfo if odd else rfe)[:, m * 128:(m + 1) * 128],
                                     eqk(0, odd)[:, x * HN:(x + 1) * HN], start=True, stop=True)
                last.then_inc(full, 1)

            def mix0_key_features(h, part):
                odd = h % 2
                ps, full = psum.open(pe, f"kp{h}{'ab'[part]}")
                for t in (range(4, 5) if part else range(4)):
                    last = pe.matmul(ps[0:TN, (t % 4) * RF:(t % 4 + 1) * RF], eqk(1, odd)[:, t * TN:(t + 1) * TN],
                                     rfo if odd else rfe, start=True, stop=True)
                last.then_inc(full, 1)

            def mix0_key_values(h):
                b = h % 2
                ps, full = psum.open(pe, f"kv{h}")
                psum.drained(pe, f"kp{h}a", f"kp{h}b", *([f"V{t}" for t in range(NT)] if h == 0 else []))
                for m in range(2):
                    for t in range(NT):
                        last = pe.matmul(ps[:, 512 * m:512 * m + 65], kp(b)[:, t, m * 128:(m + 1) * 128],
                                         asV(4)[:, t, h, :], start=(t == 0), stop=(t == NT - 1))
                last.then_inc(full, 1)

            def mix0_out(h):
                b = h % 2
                ps, full = psum.open(pe, f"mo{h}")
                psum.drained(pe, f"kv{h}", f"qp{h}_0", f"qp{h}_1")
                for t in range(NT):
                    for m in range(2):
                        last = pe.matmul(ps[0:TN, t * 65:(t + 1) * 65], qp(b)[:, m, t * TN:(t + 1) * TN],
                                         kvs[:, b, m, :], start=(m == 0), stop=(m == 1))
                last.then_inc(full, 1)
            for k, (nm, n, part) in enumerate(mixer0):
                if nm in ("q", "k"):
                    linear_T_part(nm, "Wq" if nm == "q" else "Wk", asT(2), n, 2)
                elif nm == "qp":
                    mix0_query_features(n, part)
                elif nm == "kp":
                    mix0_key_features(n, part)
                elif nm == "kv":
                    mix0_key_values(n)
                else:
                    mix0_out(n)
                for j in tiles_behind(mixer0, k, 0):
                    count_edges(j)
            psum.drained(pe, f"mo{MH - 1}")
            transposes("moT", of_R(5))
            for t in range(NT):
                ps, full = psum.open(pe, f"A{t}")
                psum.drained(pe, *[f"counts{j}" for j in range(ST - 4, ST)])
                for s in range(NT):
                    last = pe.transpose(ps[0:TN, s * 128:s * 128 + TN], asN(6)[:, s, t * TN:(t + 1) * TN],
                                        ident[0:TN, 0:TN])
                last.then_inc(full, 1)
            psum.drained(pe, *[f"moT{c}" for c in range(C)])
            linear_R("mp", ["Wproj"], chunk_of(8))

            for g in range(3):
                linear_R(f"h{g}_", [f"W{g}"], chunk_of(3))
                for hh in range(GH):
                    ps, full = psum.open(pe, f"asb{g}{hh}")
                    pe.wait_ge(sem("scores_src"), g + 1)
                    for t in range(NT):
                        last = pe.matmul(ps[0:TN, t * 128:t * 128 + TN],
                                         asd[0:TN, 0, t, hh:hh + 1].broadcast_to([TN, TN]),
                                         ident[0:TN, 0:TN], start=True, stop=True)
                    last.then_inc(full, 1)

                def offsets(hh):
                    for k in range(2):
                        ps, full = psum.open(pe, f"off{g}{hh}{k}", NT)
                        pe.wait_ge(sem("offsets"), 2 * (g + 1))
                        for t in range(NT):
                            last = pe.matmul(ps[0:TN, t * 128:t * 128 + TN],
                                             asd[0:TN, 5 + k, t, hh:hh + 1].broadcast_to([TN, TN]),
                                             ident[0:TN, 0:TN], start=True, stop=True)
                        last.then_inc(full, 1)

                def attend(hh):
                    P = asN(P_REGION[hh % 2])
                    for part, tiles in (("a", range(4)), ("b", range(4, 5))):
                        ps, full = psum.open(pe, f"gat{g}{hh}{part}")
                        pe.wait_ge(sem("attention"), NT * (GH * g + hh + 1))
                        for t in tiles:
                            for s in range(NT):
                                last = pe.matmul(ps[0:TN, (t % 4) * 256:(t % 4) * 256 + 193],
                                                 P[:, s, t * TN:(t + 1) * TN], asG(4)[:, s, hh, :],
                                                 start=(s == 0), stop=(s == NT - 1))
                        last.then_inc(full, 1)
                offsets(0)
                offsets(1)
                for hh in range(GH):
                    attend(hh)
                    if hh + 2 < GH:
                        offsets(hh + 2)
                for c in range(C):
                    ps, full = psum.open(pe, f"embT{g}_{c}")
                    if c == 0:
                        psum.drained(pe, f"gat{g}{GH - 1}a", f"gat{g}{GH - 1}b")
                    for t in range(NT):
                        last = pe.transpose(ps[:, t * 128:t * 128 + TN], asR(5)[:, t, c * 128:(c + 1) * 128],
                                            ident[0:TN, 0:TN])
                    last.then_inc(full, 1)
                psum.drained(pe, *[f"embT{g}_{c}" for c in range(C)])
                linear_R(f"wo{g}_", [f"Wout{g}"], chunk_of(2))

            transposes("xlT", of_R(5), sem("normed"), 2)
            ps, full = psum.open(pe, "gate")
            psum.drained(pe, *[f"xlT{c}" for c in range(C)])
            pe.wait_ge(sem("sums"), 1)
            for c in range(C):
                last = pe.matmul(ps[:, 0:3], lsum[:, c:c + 1].broadcast_to([128, 128]),
                                 cols[:, PL["wg"][0] + 3 * c:PL["wg"][0] + 3 * c + 3], start=(c == 0), stop=(c == C - 1))
            last.then_inc(full, 1)
            pe.wait_ge(sem("chosen"), 1)
            for m in range(2):
                ps, full = psum.open(pe, f"f1_{m}")
                for c in range(C):
                    for h in range(2):
                        last = pe.matmul(ps[0:96, 512 * h:512 * h + HN], w1s[:, c, m * 96:(m + 1) * 96],
                                         asT(2)[:, c, h * HN:(h + 1) * HN], start=(c == 0), stop=(c == C - 1))
                last.then_inc(full, 1)
            for t in range(NT):
                ps, full = psum.open(pe, f"f2_{t}")
                if t == 0:
                    psum.drained(pe, "f1_0", "f1_1")
                for m in range(2):
                    for h in range(2):
                        last = pe.matmul(ps[0:TN, 512 * h:512 * h + 384], fh[:, m, t * TN:(t + 1) * TN],
                                         w2s[:, m, h * 384:(h + 1) * 384], start=(m == 0), stop=(m == 1))
                last.then_inc(full, 1)
            if stop == "L0":
                return

            transposes("x1nT", of_R(1), sem("normed"), 3)
            psum.drained(pe, *[f"x1nT{c}" for c in range(C)])
            for t in range(TYPES):
                linear_T(f"ty{t}_", f"Wt{t}", asT(2))
            pe.wait_ge(sem("typed"), C * (TYPES - 1))
            linear_R("U", ["msgU"], chunk_of(3))
            linear_R("Vm", ["msgV"], chunk_of(3))
            def mix1_scores(h, s):
                c, o = h // 2, 64 * (h % 2)
                ps, full = psum.open(pe, f"sc{h}_{s}")
                if s == 0:
                    psum.drained(pe, f"q1_{c}", f"k1_{c}")
                for x in range(2):
                    last = pe.matmul(ps[0:TN, 512 * x:512 * x + 313], qk1(1, c % 2)[o:o + 64, s * TN:(s + 1) * TN],
                                     qk1(0, c % 2)[o:o + 64, x * 313:(x + 1) * 313], start=True, stop=True)
                last.then_inc(full, 1)

            def mix1_out(h):
                P = asN(5 + h % 2, 626)
                ps, full = psum.open(pe, f"ao{h}")
                psum.drained(pe, *[f"sc{h}_{s}" for s in range(NT)], *([f"V1{t}" for t in range(NT)] if h == 0 else []))
                for t in range(NT):
                    for s in range(NT):
                        last = pe.matmul(ps[0:TN, t * 65:(t + 1) * 65], P[:, s, t * TN:(t + 1) * TN],
                                         asV(3)[:, s, h, :], start=(s == 0), stop=(s == NT - 1))
                last.then_inc(full, 1)

            def values_of(t):
                ps, full = psum.open(pe, f"V1{t}")
                for c in range(C):
                    w = weights(pe, "Wv1", c)
                    for h in range(2):
                        last = pe.matmul(ps[0:TN, 512 * h:512 * h + 384], asT(2)[:, c, t * TN:(t + 1) * TN],
                                         w[:, h * 384:(h + 1) * 384], start=(c == 0), stop=(c == C - 1))
                last.then_inc(full, 1)
                panel_last["Wv1"] = f"V1{t}"

            def scatter(j):
                ps, full = psum.open(pe, f"scattered{j}")
                pe.wait_ge(sem("messages"), j + 1)
                pe.wait_ge(sem("onehot_dst1"), j + 1)
                onehot = oh_dst32(j % 4)
                for b in range(2):
                    pe.matmul(ps[0:TN, 512 * b:512 * b + 384], onehot, msg[j % NM][:, 384 * b:384 * (b + 1)],
                              start=True, stop=True)
                pe.matmul(ps[0:TN, 384:385], onehot, slots[:, 2, j:j + 1], start=True, stop=True).then_inc(full, 1)
            for k, (nm, n) in enumerate(mixer1):
                if nm == "V1":
                    values_of(n)
                elif nm in ("q1_", "k1_"):
                    linear_T_part(nm, "Wq1" if nm == "q1_" else "Wk1", asT(2), n)
                elif nm == "ao":
                    mix1_out(n)
                else:
                    mix1_scores(int(nm[2:-1]), n)
                for j in tiles_behind(mixer1, k, 2):
                    scatter(j)

            psum.drained(pe, f"ao{MH - 1}")
            transposes("aoT", of_R(8))
            psum.drained(pe, *[f"scattered{j}" for j in range(ST - 4, ST)])
            transposes("ST", lambda t, c: S4[:, t, c // 3, (c % 3) * 128:(c % 3 + 1) * 128])
            ps, full = psum.open(pe, "ewT")
            for t in range(NT):
                last = pe.transpose(ps[0:1, t * 128:t * 128 + TN], S4[:, t, 0, 384:385], ident[0:TN, 0:TN])
            last.then_inc(full, 1)
            psum.drained(pe, *[f"ST{c}" for c in range(C)], "ewT")
            pe.wait_ge(sem("msg_b2"), 16)
            pe.wait_ge(sem("ewsum_padded"), 1)
            linear_T("m2_", "msg2", asT(4), outer=(msg_b2, ewsum))
            psum.drained(pe, *[f"m2_{c}" for c in range(C)])
            linear_T("a1_", "agg1", asT(6))
            psum.drained(pe, *[f"a1_{c}" for c in range(C)])
            linear_T("a2_", "agg2", asT(7))
            psum.drained(pe, *[f"a2_{c}" for c in range(C)])
            linear_R("o_", ["outW"], chunk_of(3))
            psum.drained(pe, *[f"aoT{c}" for c in range(C)])
            linear_R("p1_", ["Wproj1"], chunk_of(5))

            transposes("tokT", of_R(7), sem("tokens"), 2)
            ps, full = psum.open(pe, "router")
            psum.drained(pe, *[f"tokT{c}" for c in range(C)])
            for t in range(NT):
                for c in range(C):
                    last = pe.matmul(ps[0:TN, t * 8:t * 8 + 8], asT(2)[:, c, t * TN:(t + 1) * TN],
                                     cols[:, PL["rw"][0] + 8 * c:PL["rw"][0] + 8 * c + 8],
                                     start=(c == 0), stop=(c == C - 1))
            last.then_inc(full, 1)

            def up(j):
                ps, full = psum.open(pe, f"up{j}")
                for c in range(C):
                    w = weights(pe, "moe1a" if j < C else "moe1b", c)
                    for h in range(2):
                        last = pe.matmul(ps[:, 512 * h:512 * h + HN], w[:, (j % C) * 128:(j % C + 1) * 128],
                                         asT(2)[:, c, h * HN:(h + 1) * HN], start=(c == 0), stop=(c == C - 1))
                last.then_inc(full, 1)

            def gates_of(j):
                ps, full = psum.open(pe, f"gb{j}")
                for h in range(2):
                    last = pe.matmul(ps[:, 512 * h:512 * h + HN], sel[:, j * 128:(j + 1) * 128],
                                     gT[:, h * HN:(h + 1) * HN], start=True, stop=True)
                last.then_inc(full, 1)
            up(0)
            ps, full = psum.open(pe, "gT")
            pe.wait_ge(sem("gates"), 1)
            for t in range(NT):
                last = pe.transpose(ps[0:EXPERTS, t * 128:t * 128 + TN], gate_v[:, 3, t, :], ident[0:TN, 0:TN])
            last.then_inc(full, 1)
            psum.drained(pe, "gT")
            pe.wait_ge(sem("sel"), 3)
            for j in range(12):
                gates_of(j)
                if j + 1 < 12:
                    up(j + 1)
            panel_last["moe1a"], panel_last["moe1b"] = "up5", "up11"
            psum.drained(pe, *[f"gb{j}" for j in range(12)])
            linear_R("y_", ["moe2a", "moe2b"], lambda c: asT(3 + c // C)[:, c % C, :])

        @block.sync
        def _(sp):
            def attr(s):
                if s >= 4:
                    psum.computed(sp, f"hidden{s - 4}")
                n = min(EC, E - s * EC)
                sp.dma_start(RG[8][0:32, (s % 4) * EC:(s % 4) * EC + n], a["attrT"][:, s * EC:s * EC + n])\
                  .then_inc(sem(f"attr_loaded{s % 4}"), 16)

            def half(q):
                name, w, c0, n, p = PANELS[q // 2]
                if q >= 5:
                    prev = PANELS[(q - 5) // 2][0]
                    if prev in panel_last:
                        psum.computed(sp, panel_last[prev])
                    else:
                        sp.wait_ge(sem("chosen"), 1)
                src = w.rearrange("(c p) n -> p c n", p=p)[:, 3 * (q % 2):3 * (q % 2) + 3, c0:c0 + n]
                sp.dma_start(ring[q % 5][0:p, :, 0:n], src).then_inc(sem(f"weights_loaded{q % 5}"), 16)

            def load_row(k):
                if k >= 3:
                    sp.wait_ge(sem("row_used"), k - 2)
                sp.dma_start(rowbuf[k % 3][0:TN, :], a["rows"][k:k + 1, :].broadcast_to([TN, D]))\
                  .then_inc(sem(f"row_loaded{k % 3}"), 16)

            sp.dma_start(srcdst, a["srcdst"]).then_inc(sem("edges_loaded"), 16)
            for s in range(4):
                attr(s)
            sp.dma_start(asR(0), a["x"].rearrange("(t p) d -> p t d", p=TN)).then_inc(sem("x_loaded"), 16)
            for q in range(5):
                half(q)
            for k in range(3):
                load_row(k)
            for s in range(4, ES):
                attr(s)
            behind = {"W0": [3, 4, 5], "Wout0": [6, 7], "Wout1": [8, 9], "W2": [10, 11], "ffn1": [12],
                      "Wt0": [13, 14, 15], "Wk1": [16, 17]}
            for q in range(5, 2 * len(PANELS)):
                half(q)
                if q % 2:
                    for k in behind.get(PANELS[q // 2][0], []):
                        load_row(k)
            if stop == "L0":
                sp.wait_ge(sem("final"), 1)
                sp.dma_start(a["out"].rearrange("(t p) d -> p t d", p=TN), asR(0)).then_inc(sem("stored"), 16)
                sp.wait_ge(sem("stored"), 16)
                return
            for t in range(NT):
                psum.drained(sp, f"y_{t}")
                sp.dma_start(a["out"][t * TN:(t + 1) * TN, :], asR(0)[:, t, :]).then_inc(sem("stored"), 16)
            sp.wait_ge(sem("stored"), 16 * NT)

        @block.scalar
        def _(act):
            A = act.activation

            def root(k, lo=0, hi=NT):
                act.wait_ge(sem("ln_inverse"), k)
                A(lnt[0:TN, 2, lo:hi], lnt[0:TN, 1, lo:hi], ACT.Sqrt).then_inc(sem("ln_root"), 1)

            act.dma_start(cols[:, :], a["cols"]).then_inc(sem("small_loads"), 16)
            act.dma_start(edge_w1, a["edge_W1"]).then_inc(sem("small_loads"), 16)
            act.dma_start(eb2[:, :], a["edge_b2"].broadcast_to([128, 1])).then_inc(sem("small_loads"), 16)
            act.dma_start(rfe[0:64, :], a["rfT"]).then_inc(sem("small_loads"), 16)
            act.dma_start(rfo[64:128, :], a["rfT"]).then_inc(sem("small_loads"), 16)
            act.wait_ge(sem("small_loads"), 16 * 5)

            def turned(name, r, func=ACT.Identity, bias=None, sums=None, scale=None):
                for c in range(C):
                    ps, free = psum.computed(act, f"{name}{c}")
                    dst = asT(r)[:, c, 0:N].rearrange("p (t n) -> p t n", t=NT)
                    kw = {"bias": col(bias, c)} if bias else {}
                    if scale:
                        kw["scale"] = col(scale, c)
                    if sums is not None:
                        kw["accum_out"] = sums[:, c:c + 1]
                    A(dst, blocks(ps, 128), func, **kw).then_inc(free, 1)

            def turned_part(name, r, c):
                ps, free = psum.computed(act, f"{name}{c}")
                A(asT(r)[:, c, 0:N].rearrange("p (t n) -> p t n", t=NT), blocks(ps, 128), ACT.Identity)\
                    .then_inc(free, 1)

            def hidden(s):
                n = min(EC, E - s * EC)
                ps, free = psum.computed(act, f"hidden{s}")
                if s >= 3:
                    psum.computed(act, f"logits{s - 3}")
                for m in range(2):
                    last = A(hid[s % 3][:, m, 0:n], ps[0:96, 512 * m:512 * m + n], ACT.Relu,
                             bias=col("edge_b1", m, 96))
                last.then_inc(free, 1)
            hidden(0)
            hidden(1)
            for s in range(ES):
                if s + 2 < ES:
                    hidden(s + 2)
                ps, free = psum.computed(act, f"logits{s}")
                n = min(4, EJ - 4 * s)
                A(sv("ew")[:, 4 * s:4 * s + n], ps[0:TN, 0:n], ACT.Identity).then_inc(free, 1)
                if s == 2:
                    root(1)
                for nm, k in behind_edges(s):
                    if nm == "xnT":
                        turned_part("xnT", 2, k)
                    else:
                        ps, free = psum.computed(act, f"x1T{k}")
                        A(two(asT(3)[:, k, :]), halves(ps, HN, 0, 128), ACT.Relu, bias=col("b_ah", k)).then_inc(free, 1)
            psum.drained(act, *[f"logits{s}" for s in range(ES - 4, ES)])
            A(sv("ew"), sv("ew"), ACT.Sigmoid, bias=eb2[0:TN, :]).then_inc(sem("edge_weights"), 1)

            def values(name, r):
                for t in range(NT):
                    ps, free = psum.computed(act, f"{name}{t}")
                    A(asV(r)[:, t, :, 0:64].rearrange("p (b h) d -> p b h d", b=2),
                      halves(ps, 384).rearrange("p b (h d) -> p b h d", h=6), ACT.Identity).then_inc(free, 1)
            values("V", 4)

            def squares(c):
                for k, nm in enumerate(("q", "k")):
                    psum.drained(act, f"{nm}{c}")
                    A(eqk(k, 0)[64:128, :], eqk(k, 0)[0:64, :], ACT.Square).then_inc(sem("squares"), 1)
                    A(eqk(k, 1)[0:64, :], eqk(k, 1)[64:128, :], ACT.Square).then_inc(sem("squares"), 1)

            def features(h):
                b = h % 2
                if h >= 2:
                    psum.computed(act, f"mo{h - 2}")
                for m in range(2):
                    ps, free = psum.computed(act, f"qp{h}_{m}")
                    A(two(qp(b)[:, m, :]), halves(ps, HN, 0, 128), ACT.Exp).then_inc(free, 1)
                ps, free = psum.computed(act, f"kp{h}a")
                A(kp(b)[:, 0:4, :], ps[0:TN, :].rearrange("p (t m) -> p t m", t=4), ACT.Exp).then_inc(free, 1)
                ps, free = psum.computed(act, f"kp{h}b")
                A(kp(b)[:, 4, :], ps[0:TN, 0:RF], ACT.Exp).then_inc(free, 1)
            for c in range(C):
                squares(c)
                features(2 * c)
                features(2 * c + 1)
            psum.computed(act, f"mo{MH - 1}")
            turned("moT", 8)
            root(2)

            for g in range(3):
                if g:
                    psum.computed(act, f"gat{g - 1}{GH - 1}b")
                for t in range(NT):
                    ps, free = psum.computed(act, f"h{g}_{t}")
                    A(asG(4)[:, t, :, 0:GC].rearrange("p (b h) d -> p b h d", b=2),
                      halves(ps, 384).rearrange("p b (h d) -> p b h d", h=2), ACT.Identity).then_inc(free, 1)

                def weights_of(hh):
                    P = asN(P_REGION[hh % 2])
                    if hh >= 2:
                        psum.computed(act, f"gat{g}{hh - 2}b")
                    elif g:
                        psum.computed(act, f"gat{g - 1}{hh + 2}b")
                    elif hh == 0:
                        psum.computed(act, "mp4")
                    else:
                        act.wait_ge(sem("sum_spilled"), 16)
                    ps, free = psum.computed(act, f"off{g}{hh}1")
                    for s in range(NT + 1):
                        if s < NT:
                            A(P[:, s, :].rearrange("p (t n) -> p t n", t=NT), blocks(ps), ACT.Identity,
                              bias=asd[0:TN, 7, s, hh:hh + 1]).then_inc(free, 1)
                        if s:
                            psum.reads(act, f"off{g}{hh}0", s, NT)
                            A(P[:, s - 1, :], P[:, s - 1, :], ACT.Exp).then_inc(sem("exped"), 1)

                def normalised(hh):
                    for k, (part, tiles) in enumerate((("a", range(4)), ("b", range(4, 5)))):
                        ps, free = psum.computed(act, f"gat{g}{hh}{part}")
                        act.wait_ge(sem("row_inverse"), 2 * (GH * g + hh) + k + 1)
                        if hh == 0 and k == 0:
                            psum.computed(act, f"embT{g - 1}_5" if g else "moT5")
                        for t in tiles:
                            last = A(asR(5)[:, t, hh * GC:(hh + 1) * GC], ps[0:TN, (t % 4) * 256:(t % 4) * 256 + GC],
                                     ACT.Copy, scale=rden[0:TN, 2 * (hh % 2) + 1, t:t + 1])
                        last.then_inc(free, 1)
                weights_of(0)
                weights_of(1)
                for hh in range(GH):
                    normalised(hh)
                    if hh + 2 < GH:
                        weights_of(hh + 2)
                psum.computed(act, f"wo{g - 1}_4" if g else "k5")
                turned(f"embT{g}_", 2, ACT.Relu, f"b{g}")

            root(3)
            psum.computed(act, "wo2_4")
            turned("xlT", 2, sums=lsum)
            act.wait_ge(sem("gate_shifted"), 1)
            A(gsm[:, 3:6], gsm[:, 0:3], ACT.Exp).then_inc(sem("gate_exp"), 1)
            act.wait_ge(sem("chosen"), 1)
            for m in range(2):
                ps, free = psum.computed(act, f"f1_{m}")
                A(two(fh[:, m, :]), halves(ps, HN, 0, 96), ACT.Gelu, bias=gsm[0:96, 29 + m:30 + m]).then_inc(free, 1)
            if stop == "L0":
                return

            root(4)
            psum.computed(act, "f1_1")
            turned("x1nT", 2)
            psum.computed(act, "xlT5")
            for nm, r in (("U", 5), ("Vm", 6)):
                for t in range(NT):
                    ps, free = psum.computed(act, f"{nm}{t}")
                    A(two(asR(r)[:, t, :]), halves(ps, 384), ACT.Identity).then_inc(free, 1)
            two_col = gsm[:, 31:32]

            def message(j):
                act.wait_ge(sem(f"gathered{j % NM}"), 16 * (j // NM + 1))
                A(msg[j % NM], msg[j % NM], ACT.Relu, scale=slots[:, 2, j:j + 1]).then_inc(sem("messages"), 1)
            for k, (nm, n) in enumerate(mixer1):
                for j in tiles_behind(mixer1, k, 2):
                    message(j)
                if nm == "V1":
                    if n == 0:
                        act.wait_ge(sem("typed_spilled"), 16)
                        act.wait_ge(sem("ones1"), 1)
                    ps, free = psum.computed(act, f"V1{n}")
                    A(asV(3)[:, n, :, 0:64].rearrange("p (b h) d -> p b h d", b=2),
                      halves(ps, 384).rearrange("p b (h d) -> p b h d", h=6), ACT.Identity).then_inc(free, 1)
                elif nm == "q1_":
                    ps, free = psum.computed(act, f"q1_{n}")
                    if n >= 2:
                        psum.computed(act, f"sc{2 * n - 3}_4")
                    A(two(qk1(0, n % 2)), halves(ps, HN, 0, 128), ACT.Identity).then_inc(free, 1)
                elif nm[0:2] == "sc":
                    h = int(nm[2:-1])
                    if n == 0:
                        if h >= 2:
                            psum.computed(act, f"ao{h - 2}")
                        act.wait_ge(sem("parts_stored"), 32)
                    ps, free = psum.computed(act, f"sc{h}_{n}")
                    A(two(asN(5 + h % 2, 626)[:, n, :]), halves(ps, 313), ACT.Relu, bias=two_col[0:TN, :],
                      scale=0.0625).then_inc(free, 1)
            psum.computed(act, f"ao{MH - 1}")
            turned("aoT", 5)
            turned("ST", 4)
            ps, free = psum.computed(act, "ewT")
            A(ewsum[:, 0:N].rearrange("p (t n) -> p t n", t=NT), blocks(ps, 1), ACT.Identity).then_inc(free, 1)
            for m in range(C):
                ps, free = psum.computed(act, f"m2_{m}")
                A(two(asT(6)[:, m, :]), halves(ps, HN, 0, 128), ACT.Identity).then_inc(free, 1)
            for m in range(C):
                ps, free = psum.computed(act, f"a1_{m}")
                A(two(asT(7)[:, m, :]), halves(ps, HN, 0, 128), ACT.Relu, bias=col("agg_b1", m)).then_inc(free, 1)
            root(5)
            for k in (6, 7):
                root(k, 0, 3)
            for k in (8, 9):
                root(k, 3, NT)
            turned("tokT", 2, bias="moe_b", scale="moe_g")
            act.wait_ge(sem("router_shifted"), 1)
            A(gate_v[:, 1], gate_v[:, 0], ACT.Exp).then_inc(sem("router_exp"), 1)
            for j in range(12):
                ps, free = psum.computed(act, f"up{j}")
                if j >= 2:
                    psum.drained(act, f"gb{j - 2}")
                A(two(silu[j % 2]), halves(ps, HN, 0, 128), ACT.Silu).then_inc(free, 1)
                if j == 0:
                    ps, free = psum.computed(act, "gT")
                    A(gT[:, 0:N].rearrange("p (t n) -> p t n", t=NT), blocks(ps, EXPERTS), ACT.Identity)\
                        .then_inc(free, 1)

        @block.gpsimd
        def _(pool):
            pool.memset(ident[:, :], 0.0).then_inc(sem("pool_memset"), 1)
            pool.memset(sv("tri"), 1.0).then_inc(sem("pool_memset"), 1)
            pool.iota(sv("kio", 128), pattern=[[1, ST]], base=0, channel_multiplier=0,
                      allow_small_or_imprecise_dtypes=True).then_inc(sem("iotas"), 1)
            pool.iota(iota_n[:, :], pattern=[[1, N + 1]], base=0, channel_multiplier=0,
                      allow_small_or_imprecise_dtypes=True).then_inc(sem("iotas"), 1)
            pool.wait_ge(sem("pool_memset"), 2)
            pool.affine_select(out=ident[:, :], in_=ident[:, :], compare_op=ALU.not_equal, fill=1.0, base=0,
                               pattern=[[-1, 128]], channel_multiplier=1).then_inc(sem("consts"), 1)
            pool.affine_select(out=sv("tri"), in_=sv("tri"), compare_op=ALU.is_gt, fill=0.0, base=0,
                               pattern=[[1, TN]], channel_multiplier=-1).then_inc(sem("iotas"), 1)
            pool.iota(gsm[:, 26:29], pattern=[[-1, 3]], base=3, channel_multiplier=0,
                      allow_small_or_imprecise_dtypes=True).then_inc(sem("iotas"), 1)

            pool.wait_ge(sem("sum0"), 1)
            pool.dma_start(acc_dram.rearrange("(t p) d -> p t d", p=TN), asR(0)).then_inc(sem("sum_spilled"), 16)
            for g in range(3):
                for hh in range(GH):
                    P = asN(P_REGION[hh % 2])
                    for s in range(NT):
                        n = NT * (GH * g + hh) + s
                        pool.wait_ge(sem("exped"), n + 1)
                        pool.tensor_tensor(P[:, s, :], P[:, s, :], asN(6)[:, s, :], ALU.mult)\
                            .then_inc(sem("attention"), 1)
            psum.computed(pool, "gat23b")
            pool.wait_ge(sem("sum_spilled"), 16)
            pool.dma_start(asR(0), acc_dram.rearrange("(t p) d -> p t d", p=TN)).then_inc(sem("sum_back"), 16)
            if stop == "L0":
                return

            psum.computed(pool, "f2_4")
            pool.dma_start(types_i[:, 0:N], a["types"].broadcast_to([128, N])).then_inc(sem("types_loaded"), 16)
            for n in range(C * (TYPES - 1)):
                m = n % C
                pool.wait_ge(sem("typed_part"), n + 1)
                pool.tensor_tensor(asT(3)[:, m, :], asT(3)[:, m, :], typed[n % 2], ALU.add)\
                    .then_inc(sem("typed"), 1)
            pool.wait_ge(sem("typed"), C * (TYPES - 1))
            pool.dma_start(typed_dram, RG[3][:, 0:C * NP]).then_inc(sem("typed_spilled"), 16)
            psum.drained(pool, *[f"U{t}" for t in range(NT)])
            pool.dma_start(u_dram.rearrange("(t p) d -> p t d", p=TN), asR(5)).then_inc(sem("parts_stored"), 16)
            pool.wait_ge(sem("row_used"), ROWS.index("msg_b1") + 1)
            pool.dma_start(v_dram.rearrange("(t p) d -> p t d", p=TN), asR(6)).then_inc(sem("parts_stored"), 16)
            pool.wait_ge(sem("parts_stored"), 32)

            def source_part(j):
                if j >= NM:
                    psum.computed(pool, f"scattered{j - NM}")
                pool.indirect_dma_start(out=msg[j % NM], out_offset=None, in_=u_dram,
                                        in_offset=bass.IndirectOffsetOnAxis(ap=rows_i[:, 0, j:j + 1], axis=0))\
                    .then_inc(sem(f"source_gathered{j % NM}"), 16)

            def target_part(j):
                pool.wait_ge(sem(f"source_gathered{j % NM}"), 16 * (j // NM + 1))
                pool.indirect_dma_start(out=msg[j % NM], out_offset=None, in_=v_dram,
                                        in_offset=bass.IndirectOffsetOnAxis(ap=rows_i[:, 1, j:j + 1], axis=0),
                                        compute_op=ALU.add).then_inc(sem(f"gathered{j % NM}"), 16)
            source_part(0)
            source_part(1)
            for j in range(2, ST):
                source_part(j)
                target_part(j - 2)
            target_part(ST - 2)
            target_part(ST - 1)
            psum.computed(pool, f"ao{MH - 1}")
            pool.dma_start(RG[3][:, 0:C * NP], typed_dram).then_inc(sem("typed_back"), 16)
            psum.computed(pool, "aoT5")
            pool.dma_start(msg_b2, a["msg_b2"]).then_inc(sem("msg_b2"), 16)

            psum.computed(pool, "a1_5")
            pool.memset(sel, 1.0).then_inc(sem("sel"), 1)
            pool.wait_ge(sem("sel"), 1)
            pool.affine_select(out=sel, in_=sel, compare_op=ALU.is_ge, fill=0.0, base=0, pattern=[[1, 2 * D]],
                               channel_multiplier=-FF).then_inc(sem("sel"), 1)
            pool.wait_ge(sem("sel"), 2)
            pool.affine_select(out=sel, in_=sel, compare_op=ALU.is_ge, fill=0.0, base=FF - 1, pattern=[[-1, 2 * D]],
                               channel_multiplier=FF).then_inc(sem("sel"), 1)

        @block.vector
        def _(dve):
            steps = [0]

            def link(ins):
                steps[0] += 1
                ins.then_inc(sem("dve_step"), 1)
                dve.wait_ge(sem("dve_step"), steps[0])

            def statistics(src, k, tiles):
                lo, hi = tiles[0], tiles[-1] + 1
                for t in tiles:
                    for b in range(2):
                        last = dve.bn_stats(stats[0:TN, t, b, :], src[:, t, b * 384:(b + 1) * 384])
                link(last)
                for t in tiles:
                    last = dve.bn_aggr(mv[0:TN, t, :], stats[0:TN, t, :, :].rearrange("p b s -> p (b s)"))
                link(last)
                r = lnt[0:TN, :, lo:hi]
                link(dve.tensor_scalar(r[:, 0, :], mv[0:TN, lo:hi, 1], 1e-5, None, ALU.add))
                dve.reciprocal(r[:, 1, :], r[:, 0, :]).then_inc(sem("ln_inverse"), 1)
                dve.wait_ge(sem("ln_root"), k)
                link(dve.tensor_tensor(r[:, 3, :], r[:, 2, :], r[:, 2, :], ALU.mult))
                link(dve.tensor_tensor(r[:, 3, :], r[:, 3, :], r[:, 0, :], ALU.mult))
                link(dve.tensor_scalar(r[:, 3, :], r[:, 3, :], -0.5, 1.5, ALU.mult, ALU.add))
                link(dve.tensor_tensor(r[:, 3, :], r[:, 3, :], r[:, 2, :], ALU.mult))

            def normalise(src, dst, k, tiles=range(NT)):
                statistics(src, k, tiles)
                for t in tiles:
                    last = dve.tensor_scalar(dst[:, t, :], src[:, t, :], mv[0:TN, t, 0:1], lnt[0:TN, 3, t:t + 1],
                                             ALU.subtract, ALU.mult)
                return last

            dve.memset(one[:, :], 1.0)
            dve.memset(sv("mask"), 1.0)
            dve.memset(sv("one5", 128), 1.0)
            dve.memset(rfe[64:128, :], -0.5)
            dve.memset(rfo[0:64, :], -0.5)
            dve.memset(gsm[:, 31:32], 2.0)
            dve.memset(asT(2)[:, :, N:NP], 0.0)
            link(dve.memset(asV(4)[:, :, :, 64:65], 1.0))
            dve.memset(sv5("mask")[:, :, 0:1], 0.0).then_inc(sem("consts"), 1)

            dve.wait_ge(sem("edges_loaded"), 16)
            dve.wait_ge(sem("consts"), 2)
            dve.wait_ge(sem("iotas"), 4)
            dve.tensor_copy(sv("src"), srcdst[:, 0:EJ])
            link(dve.tensor_copy(sv("dst"), srcdst[:, EJ:2 * EJ]))
            link(dve.tensor_scalar(sv("dt"), sv("dst"), float(TN), None, ALU.is_ge))
            for c in range(2, NT):
                link(dve.scalar_tensor_tensor(sv("dt"), sv("dst"), float(c * TN), sv("dt"), ALU.is_ge, ALU.add))
            link(dve.scalar_tensor_tensor(sv("dl"), sv("dt"), -float(TN), sv("dst"), ALU.mult, ALU.add))
            link(dve.tensor_scalar(sv("dl"), sv("dl"), 1.0, None, ALU.add))
            for c in range(NT):
                last = dve.tensor_scalar(sv5("ind")[:, c, :], sv("dt"), float(c), None, ALU.is_equal)
            link(last)
            link(dve.tensor_tensor_scan(sv("incl"), sv("mask"), sv("ind"), 0.0, ALU.mult, ALU.add))
            link(dve.tensor_tensor(sv("excl"), sv("incl"), sv("ind"), ALU.subtract))
            dve.tensor_copy(sv("tot"), sv5("incl")[:, :, EJ - 1]).then_inc(sem("rank_totals"), 1)

            dve.wait_ge(sem("x_loaded"), 16)
            normalise(asR(0), asR(1), 1).then_inc(sem("normed"), 1)

            ps, free = psum.computed(dve, "rank")
            dve.wait_ge(sem("iotas"), 4)
            nti, posi = sv("nti", 128).bitcast(I32), sv("posi").bitcast(I32)
            hii, loi = sv("hii").bitcast(I32), sv("loi").bitcast(I32)
            link(dve.tensor_scalar(nti, ps[:, 512:512 + NT], 127.0, None, ALU.add))
            link(dve.tensor_scalar(nti, nti, 7, None, ALU.arith_shift_right))
            link(dve.tensor_copy(sv("ntf", 128), nti))
            link(dve.tensor_tensor_scan(sv("incl5", 128), sv("one5", 128), sv("ntf", 128), 0.0, ALU.mult, ALU.add))
            link(dve.tensor_tensor(sv("ts", 128), sv("incl5", 128), sv("ntf", 128), ALU.subtract))
            dve.scalar_tensor_tensor(sv("base"), sv("ts"), 128.0, ps[0:TN, 0:NT], ALU.mult, ALU.add)\
               .then_inc(free, 1)
            psum.drained(dve, "rank")
            link(dve.tensor_tensor(sv5("part"), sv5("excl"), sv("base").unsqueeze(2).broadcast_to([TN, NT, EJ]),
                                   ALU.add))
            link(dve.tensor_tensor(sv("part"), sv("part"), sv("ind"), ALU.mult))
            link(dve.tensor_reduce(sv("pos"), sv5("part").rearrange("p c j -> p j c"), AX.X, ALU.add))
            link(dve.tensor_copy(posi, sv("pos")))
            link(dve.tensor_scalar(hii, posi, 7, None, ALU.arith_shift_right))
            link(dve.tensor_scalar(loi, posi, 127, None, ALU.bitwise_and))
            link(dve.tensor_copy(sv("hi"), hii))
            dve.tensor_copy(sv("lo"), loi).then_inc(sem("places"), 1)
            link(dve.tensor_scalar(sv("tmf", 128), sv("kio", 128), sv("ts", 128)[:, 1:2], None, ALU.is_ge))
            for c in range(2, NT):
                link(dve.scalar_tensor_tensor(sv("tmf", 128), sv("kio", 128), sv("ts", 128)[:, c:c + 1],
                                              sv("tmf", 128), ALU.is_ge, ALU.add))
            link(dve.tensor_copy(tmap[:, :], sv("tmf", 128)))

            dve.wait_ge(sem("edge_weights"), 1)
            o = so["src"][0]
            edge_values = RG[5][0:TN, o:o + 3 * EJ].rearrange("p (k j) -> p k j", k=3)

            def place(j, u):
                dve.scalar_tensor_tensor(oh_hi(u), sv("kio").unsqueeze(1).broadcast_to([TN, 3, ST]),
                                         sv("hi")[:, bass.ds(j, 1)],
                                         edge_values[:, :, bass.ds(j, 1)].broadcast_to([TN, 3, ST]),
                                         ALU.is_equal, ALU.mult)
                dve.tensor_scalar(oh_lo(u), iota_n[0:TN, 0:128], sv("lo")[:, bass.ds(j, 1)], None,
                                  ALU.is_equal).then_inc(sem("onehot_edge"), 1)
            for j in range(4):
                place(j, j)
            with dve.Fori(1, EJ // 4) as i:
                for u in range(4):
                    dve.wait_ge(sem("onehot_used"), 4 * i + u - 3)
                    place(4 * i + u, u)
            dve.wait_ge(sem("onehot_used"), EJ - 4)
            place(EJ - 1, 0)
            link(dve.memset(asN(6), 0.0))
            for t in range(NT):
                last = dve.tensor_copy(asN(6)[:, t, t * TN:(t + 1) * TN], ident[0:TN, 0:TN])
            link(last)
            ps, free = psum.computed(dve, "sorted")
            dve.tensor_copy(slots[:, :, :].rearrange("p k s -> p (k s)"), ps[:, 0:3 * ST]).then_inc(free, 1)
            psum.drained(dve, "sorted")
            dve.tensor_copy(rows_i[:, 0, :], slots[:, 0, :])
            link(dve.scalar_tensor_tensor(sv("tmp", 128), sv("tmf", 128), float(TN), slots[:, 1, :], ALU.mult, ALU.add))
            dve.tensor_scalar(rows_i[:, 1, :], sv("tmp", 128), -1.0, 0.0, ALU.add, ALU.max)\
               .then_inc(sem("slots_ready"), 1)
            dve.wait_ge(sem("slots_ready"), 1)

            def tile_of(j):
                return dve.value_load(tmap[0:1, j:j + 1], min_val=0, max_val=NT - 1)

            def copies(k, nm, c):
                ps, free = psum.computed(dve, f"{nm}{c}")
                if c:
                    psum.computed(dve, f"kp{2 * c - 1}b")
                dve.tensor_copy(two(eqk(k, 0)[0:64, :]), halves(ps, HN, 0, 64)).then_inc(free, 1)
                dve.tensor_copy(two(eqk(k, 1)[64:128, :]), halves(ps, HN, 64, 128)).then_inc(free, 1)

            def onehots_of(j):
                if j >= 4:
                    psum.computed(dve, f"counts{j - 4}")
                dve.tensor_scalar(oh_src(j % 4)[:, 0:N], iota_n[:, 0:N], slots[:, 0, j:j + 1], None, ALU.is_equal)
                dve.tensor_scalar(oh_dst(j % 4)[:, 0:TN], iota_n[:, 1:TN + 1], slots[:, 1, j:j + 1], None,
                                  ALU.is_equal).then_inc(sem("onehot_dst"), 1)
            AT = asN(6).rearrange("p t (v n) -> p t v n", v=NT)

            def add_counts(j):
                v = tile_of(j)
                ps, free = psum.computed(dve, f"counts{j}")
                if j:
                    psum.drained(dve, f"counts{j - 1}")
                dst = AT[:, :, bass.ds(v, 1), :]
                dve.tensor_tensor(dst, dst, blocks(ps).unsqueeze(2), ALU.add).then_inc(free, 1)

            def head_out(name, h, eps, dst, widths=65):
                ps, free = psum.computed(dve, name)
                v = ps[0:TN, 0:NT * 65].rearrange("p (t d) -> p t d", t=NT)
                r = rden[0:TN, :, :]
                link(dve.tensor_scalar(r[:, 0, :], v[:, :, 64], eps, None, ALU.add))
                link(dve.reciprocal(r[:, 1, :], r[:, 0, :]))
                dve.tensor_tensor(dst[:, :, h * 64:(h + 1) * 64], v[:, :, 0:64],
                                  r[:, 1, :].unsqueeze(2).broadcast_to([TN, NT, 64]), ALU.mult).then_inc(free, 1)

            onehots_of(0)
            onehots_of(1)
            for k, (nm, n, part) in enumerate(mixer0):
                if nm in ("q", "k"):
                    copies(int(nm == "k"), nm, n)
                elif nm == "kv":
                    ps, free = psum.computed(dve, f"kv{n}")
                    if n >= 2:
                        psum.computed(dve, f"mo{n - 2}")
                    dve.tensor_copy(kvs[:, n % 2, :, :], halves(ps, 65, 0, 128)).then_inc(free, 1)
                elif nm == "mo":
                    head_out(f"mo{n}", n, 256e-6, asR(5))
                for j in tiles_behind(mixer0, k, 0):
                    if j + 2 < ST:
                        onehots_of(j + 2)
                    add_counts(j)
            for t in range(NT):
                ps, free = psum.computed(dve, f"A{t}")
                dve.tensor_scalar(neg[:, t, :].rearrange("p (s n) -> p s n", s=NT), blocks(ps), 0.0, NEG,
                                  ALU.is_equal, ALU.mult).then_inc(free, 1)
            dve.memset(asG(4)[:, :, :, GC:GC + 1], 1.0)
            dve.tensor_tensor(asR(1), asR(1), row5(dve, "mix_b_proj"), ALU.add).then_inc(sem("row_used"), 1)
            dve.wait_ge(sem("row_used"), 1)
            for t in range(NT):
                ps, free = psum.computed(dve, f"mp{t}")
                dve.tensor_tensor(two(asR(1)[:, t, :]), two(asR(1)[:, t, :]), halves(ps, 384), ALU.add)\
                   .then_inc(free, 1)
            psum.drained(dve, *[f"mp{t}" for t in range(NT)])
            link(normalise(asR(1), asR(1), 2))
            dve.tensor_tensor(asR(1), asR(1), row5(dve, "mix_gamma"), ALU.mult).then_inc(sem("row_used"), 1)
            dve.wait_ge(sem("row_used"), 2)
            dve.tensor_tensor(asR(1), asR(1), row5(dve, "mix_beta"), ALU.add).then_inc(sem("row_used"), 1)
            dve.wait_ge(sem("row_used"), 3)
            dve.tensor_tensor(asR(0), asR(0), asR(1), ALU.add).then_inc(sem("sum0"), 1)

            unread = oh_raw[0:TN, :].bitcast(BF16)
            s8 = asd[0:TN]
            for g in range(3):
                psum.drained(dve, *[f"h{g}_{t}" for t in range(NT)])
                for k, nm in enumerate(("a_src", "a_dst")):
                    r = row(dve, f"{nm}{g}")
                    for t in range(NT):
                        for hh in range(GH):
                            w = (GH * t + hh) % 16 * GC
                            last = dve.tensor_tensor_reduce(unread[:, w:w + GC], asG(4)[:, t, hh, 0:GC],
                                                            r[:, hh * GC:(hh + 1) * GC], 1.0, 0.0, ALU.mult, ALU.add,
                                                            s8[:, k, t, hh:hh + 1])
                        if t % 2:
                            link(last)
                    last.then_inc(sem("row_used"), 1)
                    dve.wait_ge(sem("row_used"), 4 + 2 * g + k)
                dve.tensor_scalar(s8[:, 7], s8[:, 0], 0.2, None, ALU.mult).then_inc(sem("scores_src"), 1)
                for hh in range(GH):
                    ps, free = psum.computed(dve, f"asb{g}{hh}")
                    if hh:
                        psum.drained(dve, f"asb{g}{hh - 1}")
                    for t in range(NT):
                        dst = unread[:, t * N:(t + 1) * N].rearrange("p (s n) -> p s n", s=NT)
                        last = dve.tensor_tensor_reduce(dst, blocks(ps),
                                                        neg[:, t, :].rearrange("p (s n) -> p s n", s=NT), 1.0,
                                                        3.0 * NEG, ALU.add, ALU.max, s8[:, 2, t, hh:hh + 1])
                    last.then_inc(free, 1)
                psum.drained(dve, *[f"asb{g}{hh}" for hh in range(GH)])
                link(dve.tensor_tensor(s8[:, 3], s8[:, 2], s8[:, 1], ALU.add))
                link(dve.scalar_tensor_tensor(s8[:, 4], s8[:, 3], 0.2, s8[:, 3], ALU.mult, ALU.max))
                dve.tensor_tensor(s8[:, 5], s8[:, 1], s8[:, 4], ALU.subtract).then_inc(sem("offsets"), 1)
                dve.scalar_tensor_tensor(s8[:, 6], s8[:, 1], 0.2, s8[:, 4], ALU.mult, ALU.subtract)\
                   .then_inc(sem("offsets"), 1)

                def weights_of(hh):
                    P = asN(P_REGION[hh % 2])
                    ps, free = psum.computed(dve, f"off{g}{hh}0")
                    for s in range(NT):
                        psum.reads(dve, f"off{g}{hh}1", s + 1, NT)
                        p = P[:, s, :].rearrange("p (t n) -> p t n", t=NT)
                        dve.scalar_tensor_tensor(p, blocks(ps), s8[:, 0, s, hh:hh + 1], p, ALU.add, ALU.max)\
                           .then_inc(free, 1)

                def denominators(hh):
                    b = 2 * (hh % 2)
                    for part, lo, hi in (("a", 0, 4), ("b", 4, 5)):
                        ps, free = psum.computed(dve, f"gat{g}{hh}{part}")
                        if hh >= 2:
                            psum.drained(dve, f"gat{g}{hh - 2}{part}")
                        link(dve.tensor_scalar(rden[0:TN, b, lo:hi],
                                               ps[0:TN, :].rearrange("p (t n) -> p t n", t=4)[:, 0:hi - lo, GC],
                                               1e-16, None, ALU.add))
                        dve.reciprocal(rden[0:TN, b + 1, lo:hi], rden[0:TN, b, lo:hi]).then_inc(sem("row_inverse"), 1)
                weights_of(0)
                weights_of(1)
                for hh in range(GH):
                    denominators(hh)
                    if hh + 2 < GH:
                        weights_of(hh + 2)
                for t in range(NT):
                    ps, free = psum.computed(dve, f"wo{g}_{t}")
                    dst = two(asR(1)[:, t, :])
                    if g == 0:
                        dve.tensor_copy(dst, halves(ps, 384)).then_inc(free, 1)
                    else:
                        dve.tensor_tensor(dst, dst, halves(ps, 384), ALU.add).then_inc(free, 1)
                psum.drained(dve, *[f"wo{g}_{t}" for t in range(NT)])
            dve.tensor_tensor(asR(1), asR(1), row5(dve, "gnn_b_out"), ALU.add).then_inc(sem("row_used"), 1)
            dve.wait_ge(sem("row_used"), 10)
            dve.wait_ge(sem("sum_back"), 16)
            link(dve.scalar_tensor_tensor(asR(0), asR(1), 0.0, asR(0), ALU.max, ALU.add))
            normalise(asR(0), asR(5), 3).then_inc(sem("normed"), 1)

            psum.drained(dve, *[f"xlT{c}" for c in range(C)])
            dve.sem_inc(sem("sums"), 1)
            ps, free = psum.computed(dve, "gate")
            G = gsm
            dve.tensor_scalar(G[:, 0:3], ps[:, 0:3], 1.0 / N, None, ALU.mult).then_inc(free, 1)
            psum.drained(dve, "gate")
            link(dve.tensor_reduce(G[:, 6:7], G[:, 0:3], AX.X, ALU.max))
            dve.tensor_scalar(G[:, 0:3], G[:, 0:3], G[:, 6:7], None, ALU.subtract).then_inc(sem("gate_shifted"), 1)
            dve.wait_ge(sem("gate_exp"), 1)
            link(dve.tensor_reduce(G[:, 8:9], G[:, 3:6], AX.X, ALU.add))
            link(dve.reciprocal(G[:, 9:10], G[:, 8:9]))
            link(dve.tensor_scalar(G[:, 10:13], G[:, 3:6], G[:, 9:10], None, ALU.mult))
            link(dve.tensor_reduce(G[:, 6:7], G[:, 10:13], AX.X, ALU.max))
            link(dve.scalar_tensor_tensor(G[:, 16:19], G[:, 10:13], G[:, 6:7], G[:, 26:29], ALU.is_equal, ALU.mult))
            link(dve.tensor_reduce(G[:, 19:20], G[:, 16:19], AX.X, ALU.max))
            link(dve.tensor_scalar(G[:, 20:23], G[:, 16:19], G[:, 19:20], None, ALU.is_equal))
            link(dve.tensor_tensor(G[:, 23:26], G[:, 20:23], G[:, 10:13], ALU.mult))
            for e in range(3):
                pick, score = G[:, 20 + e:21 + e], G[:, 23 + e:24 + e]

                def take(dst, src, w, p):
                    if e == 0:
                        return dve.tensor_scalar(dst, src, w[0:p, :], None, ALU.mult)
                    return dve.scalar_tensor_tensor(dst, src, w[0:p, :], dst, ALU.mult, ALU.add)
                for half in range(2):
                    weights(dve, "ffn1", 3 * half)
                    src = ring[(2 * pindex["ffn1"] + half) % 5][:, :, e * FF:(e + 1) * FF]
                    take(w1s[:, 3 * half:3 * half + 3, :], src, pick, 128)
                for m in range(2):
                    src = weights(dve, "ffn2", 2 * e + m)[0:96, :]
                    take(w2s[:, m, :], src, score, 96)
                link(take(gsm[0:96, 29:31], cols[0:96, PL["ffn_b1"][0] + 2 * e:PL["ffn_b1"][0] + 2 * e + 2], pick, 96))
                take(b2s, row(dve, f"ffn_b2_{e}"), score, TN).then_inc(sem("row_used"), 1)
                dve.wait_ge(sem("row_used"), 11 + e)
            dve.tensor_tensor(asR(0), asR(0), b2s.unsqueeze(1).broadcast_to([TN, NT, D]), ALU.add)\
               .then_inc(sem("chosen"), 1)
            dve.wait_ge(sem("chosen"), 1)
            for t in range(NT):
                ps, free = psum.computed(dve, f"f2_{t}")
                dst = two(asR(0)[:, t, :])
                dve.tensor_tensor(dst, dst, halves(ps, 384), ALU.add).then_inc(free, 1)
            psum.drained(dve, *[f"f2_{t}" for t in range(NT)])
            if stop == "L0":
                dve.sem_inc(sem("final"), 1)
                return

            normalise(asR(0), asR(1), 4).then_inc(sem("normed"), 1)
            link(dve.memset(types_i[:, N:NP], 0.0))
            dve.wait_ge(sem("types_loaded"), 16)
            for t in range(TYPES):
                last = dve.tensor_scalar(masks[:, t, :], types_i, float(t), None, ALU.is_equal)
            link(last)
            n = 0
            for t in range(TYPES):
                for m in range(C):
                    ps, free = psum.computed(dve, f"ty{t}_{m}")
                    dst = asT(3)[:, m, :] if t == 0 else typed[n % 2]
                    if t:
                        if n >= 2:
                            dve.wait_ge(sem("typed"), n - 1)
                        n += 1
                    dve.scalar_tensor_tensor(two(dst), halves(ps, HN, 0, 128), col("b_type", C * t + m),
                                             two(masks[:, t, :]), ALU.add, ALU.mult).then_inc(free, 1)
                    if t:
                        psum.drained(dve, f"ty{t}_{m}")
                        dve.sem_inc(sem("typed_part"), 1)
            dve.wait_ge(sem("typed"), C * (TYPES - 1))
            dve.memset(asT(4)[:, :, N:NP], 0.0)
            psum.computed(dve, "xlT5")
            link(dve.memset(S4, 0.0))
            psum.drained(dve, *[f"Vm{t}" for t in range(NT)])
            dve.tensor_tensor(asR(6), asR(6), row5(dve, "msg_b1"), ALU.add).then_inc(sem("row_used"), 1)

            dve.wait_ge(sem("typed_spilled"), 16)
            psum.computed(dve, "Vm4")
            dve.memset(asV(3)[:, :, :, 64:65], 1.0).then_inc(sem("ones1"), 1)
            dve.tensor_tensor(asR(0), asR(0), row5(dve, "mix1_proj_b"), ALU.add).then_inc(sem("row_used"), 1)
            dve.wait_ge(sem("row_used"), 15)
            dve.tensor_tensor(asR(1), asR(1), row5(dve, "out_b"), ALU.add).then_inc(sem("row_used"), 1)

            def onehot_of(j):
                if j >= 4:
                    psum.computed(dve, f"scattered{j - 4}")
                dve.tensor_scalar(oh_dst32(j % 4), iota_n[:, 1:TN + 1], slots[:, 1, j:j + 1], None, ALU.is_equal)\
                   .then_inc(sem("onehot_dst1"), 1)

            def add_messages(j):
                v = tile_of(j)
                ps, free = psum.computed(dve, f"scattered{j}")
                if j:
                    psum.drained(dve, f"scattered{j - 1}")
                dst = S4[:, bass.ds(v, 1), :, 0:384]
                dve.tensor_tensor(dst, dst, halves(ps, 384).unsqueeze(1), ALU.add)
                dst = S4[:, bass.ds(v, 1), 0:1, 384:385]
                dve.tensor_tensor(dst, dst, ps[0:TN, 384:385].unsqueeze(1).unsqueeze(1), ALU.add).then_inc(free, 1)
            onehot_of(0)
            onehot_of(1)
            for k, (nm, n) in enumerate(mixer1):
                if nm == "k1_":
                    ps, free = psum.computed(dve, f"k1_{n}")
                    if n >= 2:
                        psum.computed(dve, f"sc{2 * n - 3}_4")
                    dve.tensor_copy(two(qk1(1, n % 2)), halves(ps, HN, 0, 128)).then_inc(free, 1)
                elif nm == "ao":
                    head_out(f"ao{n}", n, 0.0, asR(8))
                for j in tiles_behind(mixer1, k, 2):
                    if j + 2 < ST:
                        onehot_of(j + 2)
                    add_messages(j)

            dve.wait_ge(sem("row_used"), 16)
            psum.drained(dve, *[f"aoT{c}" for c in range(C)])
            dve.memset(ewsum[:, N:NP], 0.0).then_inc(sem("ewsum_padded"), 1)
            dve.wait_ge(sem("typed_back"), 16)
            for m in range(C):
                ps, free = psum.computed(dve, f"a2_{m}")
                dst = two(asT(3)[:, m, :])
                dve.scalar_tensor_tensor(dst, halves(ps, HN, 0, 128), col("agg_b2", m), dst, ALU.add, ALU.add)\
                   .then_inc(free, 1)
            for t in range(NT):
                ps, free = psum.computed(dve, f"o_{t}")
                dst = two(asR(1)[:, t, :])
                dve.tensor_tensor(dst, dst, halves(ps, 384), ALU.add).then_inc(free, 1)
            psum.drained(dve, *[f"o_{t}" for t in range(NT)])
            link(normalise(asR(1), asR(1), 5))
            dve.tensor_tensor(asR(1), asR(1), row5(dve, "ln_g"), ALU.mult).then_inc(sem("row_used"), 1)
            dve.wait_ge(sem("row_used"), 17)
            dve.tensor_tensor(asR(1), asR(1), row5(dve, "ln_b"), ALU.add).then_inc(sem("row_used"), 1)
            dve.wait_ge(sem("row_used"), 18)
            link(dve.tensor_tensor(asR(0), asR(0), asR(1), ALU.add))

            for k, tiles in ((6, range(0, 3)), (8, range(3, NT))):
                lo, hi = tiles[0], tiles[-1] + 1
                for t in tiles:
                    ps, free = psum.computed(dve, f"p1_{t}")
                    dst = two(asR(0)[:, t, :])
                    dve.tensor_tensor(dst, dst, halves(ps, 384), ALU.add).then_inc(free, 1)
                psum.drained(dve, *[f"p1_{t}" for t in tiles])
                link(normalise(asR(0), asR(1), k, tiles))
                normalise(asR(1), asR(7), k + 1, tiles).then_inc(sem("tokens"), 1)
            link(dve.tensor_tensor(asR(0), asR(0), asR(1), ALU.add))
            ps, free = psum.computed(dve, "router")

            def wide(x):
                return x.unsqueeze(2).broadcast_to([TN, NT, EXPERTS])
            lg = ps[0:TN, 0:NT * EXPERTS].rearrange("p (t e) -> p t e", t=NT)
            link(dve.tensor_reduce(gq[:, 0, :], lg, AX.X, ALU.max))
            dve.tensor_tensor(gate_v[:, 0], lg, wide(gq[:, 0, :]), ALU.subtract).then_inc(free, 1)
            psum.drained(dve, "router")
            dve.sem_inc(sem("router_shifted"), 1)
            for e in range(EXPERTS):
                dve.memset(gate_v[:, 4, :, e:e + 1], float(EXPERTS - e))
            link(dve.memset(gT[:, N:NP], 0.0))
            dve.wait_ge(sem("router_exp"), 1)
            link(dve.tensor_reduce(gq[:, 1, :], gate_v[:, 1], AX.X, ALU.add))
            link(dve.reciprocal(gq[:, 2, :], gq[:, 1, :]))
            link(dve.tensor_tensor(gate_v[:, 1], gate_v[:, 1], wide(gq[:, 2, :]), ALU.mult))
            link(dve.tensor_copy(gate_v[:, 0], gate_v[:, 1]))
            for k in range(2):
                link(dve.tensor_reduce(gq[:, 0, :], gate_v[:, 0], AX.X, ALU.max))
                link(dve.tensor_tensor(gate_v[:, 2], gate_v[:, 0], wide(gq[:, 0, :]), ALU.is_equal))
                link(dve.tensor_tensor(gate_v[:, 2], gate_v[:, 2], gate_v[:, 4], ALU.mult))
                link(dve.tensor_reduce(gq[:, 1, :], gate_v[:, 2], AX.X, ALU.max))
                link(dve.tensor_tensor(gate_v[:, 2], gate_v[:, 2], wide(gq[:, 1, :]), ALU.is_equal))
                if k == 0:
                    link(dve.tensor_copy(gate_v[:, 3], gate_v[:, 2]))
                    link(dve.scalar_tensor_tensor(gate_v[:, 0], gate_v[:, 2], -2.0, gate_v[:, 0], ALU.mult, ALU.add))
                else:
                    link(dve.tensor_tensor(gate_v[:, 3], gate_v[:, 3], gate_v[:, 2], ALU.add))
            link(dve.tensor_tensor(gate_v[:, 3], gate_v[:, 3], gate_v[:, 1], ALU.mult))
            link(dve.tensor_reduce(gq[:, 1, :], gate_v[:, 3], AX.X, ALU.add))
            link(dve.reciprocal(gq[:, 2, :], gq[:, 1, :]))
            dve.tensor_tensor(gate_v[:, 3], gate_v[:, 3], wide(gq[:, 2, :]), ALU.mult).then_inc(sem("gates"), 1)
            psum.computed(dve, "ao11")
            for j in range(12):
                psum.drained(dve, f"up{j}")
                ps, free = psum.computed(dve, f"gb{j}")
                dve.tensor_tensor(two(asT(3 + j // C)[:, j % C, :]), two(silu[j % 2]), halves(ps, HN, 0, 128),
                                  ALU.mult).then_inc(free, 1)
            for t in range(NT):
                ps, free = psum.computed(dve, f"y_{t}")
                dst = two(asR(0)[:, t, :])
                dve.tensor_tensor(dst, dst, halves(ps, 384), ALU.add).then_inc(free, 1)


def kernel(**inputs):
    import numpy as np
    import concourse.bacc as bacc
    from concourse.bass_utils import run_bass_kernel_spmd as run

    v = {k: np.asarray(x) for k, x in inputs.items()}
    g0, m0, f0, g1 = "L0_gnn_", "L0_mix_", "L0_ffn_", "L1_gnn_"

    def chunks(x, p=128):
        x = x.reshape(-1, x.shape[-1] // p, p)
        return x.transpose(2, 0, 1).reshape(p, -1)

    parts = {"b_ah": chunks(v[g0 + "b_ah"]), "b0": chunks(v[g0 + "b0"]), "b1": chunks(v[g0 + "b1"]),
             "b2": chunks(v[g0 + "b2"]), "agg_b1": chunks(v[g1 + "agg_b1"]), "agg_b2": chunks(v[g1 + "agg_b2"]),
             "b_type": chunks(v[g1 + "b_type"]), "ffn_b1": chunks(v[f0 + "b1"], 96),
             "edge_b1": chunks(v[g1 + "edge_b1"], 96), "edge_w2": chunks(v[g1 + "edge_W2"].T, 96),
             "moe_g": chunks(v["L1_ffn_ln_gamma"]), "moe_b": chunks(v["L1_ffn_ln_beta"]),
             "wg": v[f0 + "Wg"].T.reshape(C, 128, 3).transpose(1, 0, 2).reshape(128, 18),
             "rw": v["L1_ffn_router_w"].reshape(C, 128, 8).transpose(1, 0, 2).reshape(128, 48)}
    places = column_places()
    cols = np.zeros((128, places["all"][1]), np.float32)
    for name, x in parts.items():
        cols[0:x.shape[0], places[name][0]:places[name][0] + x.shape[1]] = x
    rows = [v[m0 + "b_proj"], v[m0 + "gamma"], v[m0 + "beta"]]
    for i in range(3):
        rows += [v[f"{g0}a_src{i}"].reshape(-1), v[f"{g0}a_dst{i}"].reshape(-1)]
    rows += [v[g0 + "b_out"], *v[f0 + "b2"], v[g1 + "msg_b1"], v["L1_mix_proj_b"], v[g1 + "out_b"],
             v[g1 + "ln_g"], v[g1 + "ln_b"]]

    def flat(x):
        return x.transpose(1, 0, 2).reshape(x.shape[1], -1)
    arrays = {
        "x": v["x"], "srcdst": np.stack([v["src"].reshape(EJ, TN).T, v["dst"].reshape(EJ, TN).T], 1).reshape(TN, -1),
        "attrT": v["edge_attr_32"].T, "types": v["node_type_6"].reshape(1, N), "cols": cols, "rows": np.stack(rows),
        "W_ah": v[g0 + "W_ah"], "W0": v[g0 + "W0"], "W1": v[g0 + "W1"], "W2": v[g0 + "W2"], "W_out": v[g0 + "W_out"],
        "W_qkv": v[m0 + "W_qkv"], "W_proj": v[m0 + "W_proj"], "rfT": v[m0 + "random_features"].T,
        "ffn_W1": flat(v[f0 + "W1"]), "ffn_W2": v[f0 + "W2"].reshape(-1, D),
        "W_type": v[g1 + "W_type"].reshape(-1, D), "msg_W1": v[g1 + "msg_W1"], "msg_W2": v[g1 + "msg_W2"],
        "msg_b2": v[g1 + "msg_b2"].reshape(1, D), "edge_W1": v[g1 + "edge_W1"], "edge_b2": v[g1 + "edge_b2"].reshape(1, 1),
        "agg_W1": v[g1 + "agg_W1"], "agg_W2": v[g1 + "agg_W2"], "out_W": v[g1 + "out_W"],
        "qkv1_w": v["L1_mix_qkv_w"].T, "proj1_w": v["L1_mix_proj_w"].T,
        "moe_w1": flat(v["L1_ffn_w1"]), "moe_w2": v["L1_ffn_w2"].reshape(-1, D),
    }
    nc = bacc.Bacc("TRN2", target_bir_lowering=False, num_devices=1)
    aps, given = {}, {}
    for name, x in arrays.items():
        x = np.ascontiguousarray(x)
        given[f"in_{name}_dram"] = x
        aps[name] = nc.dram_tensor(f"in_{name}_dram", x.shape, mybir.dt.from_np(x.dtype), kind="ExternalInput").ap()
    aps["out"] = nc.dram_tensor("out_0_dram", (N, D), F32, kind="ExternalOutput").ap()
    gps_block(nc, aps)
    r = run(nc, [given], core_ids=[0])
    return r.results[0]["out_0_dram"]
```

```python
import concourse.bass as bass
from concourse import mybir
from contextlib import ExitStack

F32, BF16, F16, I32 = mybir.dt.float32, mybir.dt.bfloat16, mybir.dt.float16, mybir.dt.int32
F32R = mybir.dt.float32r
ACT = mybir.ActivationFunctionType
ALU = mybir.AluOpType
AX = mybir.AxisListType

N = 625
TN, NT = 125, 5
D, C = 768, 6
NP, HN = 628, 314
E = 10625
EJ = 85
ST = 88
GH, GC = 4, 192
MH, MD = 12, 64
RF = 256
EC = 500
ES = -(-E // EC)
TYPES, EXPERTS, FF = 6, 8, 192
NEG = -1.0e30


def row_order():
    rows = ["a_src0", "a_dst0", "mix_b_proj", "mix_gamma", "mix_beta", "a_src1", "a_dst1", "a_src2", "a_dst2"]
    rows += ["gnn_b_out", "ffn_b2_0", "ffn_b2_1", "ffn_b2_2",
             "msg_b1", "mix1_proj_b", "out_b", "ln_b", "ln_g"]
    return rows


def column_places():
    at, out = 0, {}
    for name, n in (("b_ah", 6), ("b0", 6), ("b1", 6), ("b2", 6), ("agg_b1", 6), ("agg_b2", 6),
                    ("b_type", 36), ("ffn_b1", 6), ("wg", 18), ("rw", 48), ("moe_g", 6), ("moe_b", 6)):
        out[name] = (at, n)
        at += n
    out["all"] = (0, at)
    return out


class PsumRing:

    def __init__(self, nc, ctx):
        self.tiles = [ctx.enter_context(nc.psum_tensor(f"ps{i}", [128, 1024], F32)) for i in range(4)]
        self.full = [ctx.enter_context(nc.semaphore(f"psum_computed{i}")) for i in range(4)]
        self.free = [ctx.enter_context(nc.semaphore(f"psum_drained{i}")) for i in range(4)]
        self.filled, self.freed, self.opened, self.where = [0] * 4, [0] * 4, 0, {}

    def open(self, pe, name, reads=1):
        s = self.opened % 4
        self.opened += 1
        if self.freed[s]:
            pe.wait_ge(self.free[s], self.freed[s])
        self.freed[s] += reads
        self.filled[s] += 1
        assert name not in self.where, name
        self.where[name] = (s, self.filled[s], self.freed[s])
        return self.tiles[s], self.full[s]

    def computed(self, eng, name):
        s, n, _ = self.where[name]
        eng.wait_ge(self.full[s], n)
        return self.tiles[s], self.free[s]

    def reads(self, eng, name, k, total):
        s, _, n = self.where[name]
        eng.wait_ge(self.free[s], n - total + k)

    def drained(self, eng, *names):
        most = {}
        for name in names:
            s, _, n = self.where[name]
            most[s] = max(most.get(s, 0), n)
        for s, n in most.items():
            eng.wait_ge(self.free[s], n)



def gps_block(nc, a, stop=None):
    ctx = ExitStack()
    with ctx:
        def sb(name, shape, dt=F32):
            return ctx.enter_context(nc.sbuf_tensor(name, shape, dt))

        def sb_both(name, shape):
            with nc.sbuf_tensor(name, shape, F32) as plain:
                pass
            return plain, sb(name + "_r", shape, F32R)

        sems = {}

        def sem(name):
            if name not in sems:
                sems[name] = ctx.enter_context(nc.semaphore(name))
            return sems[name]

        psum = PsumRing(nc, ctx)
        ring, ring_r = zip(*[sb_both(f"wring{i}", [128, 3, D]) for i in range(5)])
        RG, RG_R = zip(*[sb_both(f"region{i}", [128, 3904]) for i in range(9)])
        rowbuf, rowbuf_r = zip(*[sb_both(f"rowbuf{i}", [128, D]) for i in range(3)])

        def asR(r):
            return RG[r][0:TN, 0:NT * D].rearrange("p (t d) -> p t d", t=NT)

        def asT(r):
            return RG[r][:, 0:C * NP].rearrange("p (c n) -> p c n", c=C)

        def asV(r):
            return RG[r][0:TN, 0:NT * MH * 65].rearrange("p (t h d) -> p t h d", t=NT, h=MH)

        def asG(r):
            return RG[r][0:TN, 0:NT * GH * 193].rearrange("p (t h d) -> p t h d", t=NT, h=GH)

        def asN(r, w=N):
            return RG[r][0:TN, 0:NT * w].rearrange("p (t n) -> p t n", t=NT)

        def blocks(ps, p=TN, w=125):
            return ps[0:p, 0:640].rearrange("p (t n) -> p t n", n=128)[:, :, 0:w]

        def halves(ps, n, lo=0, hi=TN):
            return ps[lo:hi, :].rearrange("p (b n) -> p b n", b=2)[:, :, 0:n]

        def two(x):
            return x.rearrange("p (b n) -> p b n", b=2)

        ident = sb("ident", [128, 128])
        one = sb("one", [128, 1])
        mix0_consts, mix0_consts_r = sb_both("mix0_consts", [128, 2 * RF + 260])
        rfe, rfo = mix0_consts[:, 0:RF], mix0_consts[:, RF:2 * RF]
        kvs = mix0_consts[:, 2 * RF:2 * RF + 260].rearrange("p (b m d) -> p b m d", b=2, m=2)
        PL = column_places()
        cols = sb("cols", [128, PL["all"][1]])
        slots = sb("slots", [128, 3, ST])
        rows_i = sb("rows_i", [128, 2, ST], I32)
        tmap = sb("tmap", [128, ST], I32)
        iota_n = sb("iota_n", [128, N + 1], F16)
        oh_raw, oh_raw_r = sb_both("oh_raw", [128, 1696])
        stats = sb("stats", [128, NT, 2, 6])
        mv = sb("mv", [128, NT, 2])
        lnt = sb("lnt", [128, 4, NT])
        asd = sb("asd", [128, 8, NT, GH])
        rden = sb("rden", [128, 4, NT])
        eb2 = sb("eb2", [128, 1])

        def oh_lo(u):
            return oh_raw[0:TN, u * 128:(u + 1) * 128]

        def oh_hi(u):
            return oh_raw[0:TN, 512 + u * 3 * ST:512 + (u + 1) * 3 * ST].rearrange("p (k s) -> p k s", k=3)

        def oh_src(u):
            return oh_raw[:, u * 313:(u + 1) * 313].bitcast(BF16)

        def oh_dst(u):
            return oh_raw[:, 1252 + u * 63:1252 + (u + 1) * 63].bitcast(BF16)

        def oh_dst32(u):
            return oh_raw[:, u * TN:(u + 1) * TN]

        so = {}
        at = 0
        for nm, n in (("src", EJ), ("dl", EJ), ("ew", EJ), ("dst", EJ), ("dt", EJ), ("ind", 5 * EJ), ("incl", 5 * EJ),
                      ("excl", 5 * EJ), ("mask", 5 * EJ), ("tot", 5), ("base", 5), ("pos", EJ), ("part", 5 * EJ),
                      ("hi", EJ), ("lo", EJ), ("posi", EJ), ("hii", EJ), ("loi", EJ), ("nti", 5), ("ntf", 5),
                      ("incl5", 5), ("ts", 5), ("one5", 5), ("kio", ST), ("tmf", ST), ("tmp", ST),
                      ("tri", TN)):
            so[nm] = (at, n)
            at += n
        assert at <= 3904

        def sv(nm, p=TN):
            o, n = so[nm]
            return RG[5][0:p, o:o + n]

        def sv5(nm):
            return sv(nm).rearrange("p (c j) -> p c j", c=5)

        srcdst = RG[6][0:TN, 3200:3200 + 2 * EJ].bitcast(I32)
        edge_w1 = RG[6][0:33, 3400:3400 + FF]
        edge_w2 = RG[6][0:TN, 3600:3600 + FF]

        def attr_of(s):
            return RG[8][0:33, s % 7 * EC:(s % 7 + 1) * EC]

        def col(name, k, p=128):
            return cols[0:p, PL[name][0] + k:PL[name][0] + k + 1]

        PANELS = [("W_ah", a["W_ah"], 0, D, 128), ("Wv", a["W_qkv"], 2 * D, D, 128),
                  ("Wq", a["W_qkv"], 0, D, 128), ("Wk", a["W_qkv"], D, D, 128), ("W0", a["W0"], 0, D, 128),
                  ("Wproj", a["W_proj"], 0, D, 128)]
        for i in range(3):
            if i < 2:
                PANELS.append((f"W{i + 1}", a[f"W{i + 1}"], 0, D, 128))
            PANELS.append((f"Wout{i}", a["W_out"][i * D:(i + 1) * D, :], 0, D, 128))
        PANELS += [("ffn1", a["ffn_W1"], 0, 3 * FF, 128), ("ffn2", a["ffn_W2"], 0, D, 96)]
        if stop != "L0":
            PANELS += [(f"Wt{t}", a["W_type"][t * D:(t + 1) * D, :], 0, D, 128) for t in range(TYPES)]
            PANELS += [("msgU", a["msg_W1"][0:D, :], 0, D, 128), ("msgV", a["msg_W1"][D:2 * D, :], 0, D, 128),
                       ("Wv1", a["qkv1_w"], 2 * D, D, 128), ("Wq1", a["qkv1_w"], 0, D, 128),
                       ("Wk1", a["qkv1_w"], D, D, 128),
                       ("msg2", a["msg_W2"], 0, D, 128), ("agg1", a["agg_W1"], 0, D, 128),
                       ("agg2", a["agg_W2"], 0, D, 128), ("outW", a["out_W"], 0, D, 128),
                       ("Wproj1", a["proj1_w"], 0, D, 128),
                       ("moe1a", a["moe_w1"], 0, D, 128), ("moe1b", a["moe_w1"], D, D, 128),
                       ("moe2a", a["moe_w2"][0:D, :], 0, D, 128), ("moe2b", a["moe_w2"][D:2 * D, :], 0, D, 128)]
        pindex = {p[0]: i for i, p in enumerate(PANELS)}
        panel_last = {}

        def weights(eng, name, c):
            q = 2 * pindex[name] + c // 3
            eng.wait_ge(sem(f"weights_loaded{q % 5}"), 16 * (q // 5 + 1))
            return ring[q % 5][:, c % 3, :]

        ROWS = row_order()

        def row(eng, name):
            k = ROWS.index(name)
            eng.wait_ge(sem(f"row_loaded{k % 3}"), 16 * (k // 3 + 1))
            return rowbuf[k % 3][0:TN, :]

        def row5(eng, name):
            return row(eng, name).unsqueeze(1).broadcast_to([TN, NT, D])

        def eqk(which, odd):
            o = (2 * which + odd) * NP
            return RG[7][:, o:o + NP]

        def qp(b):
            return RG[8][:, b * 2 * NP:(b + 1) * 2 * NP].rearrange("p (m n) -> p m n", m=2)

        def kp(b):
            return RG[8 - b][0:TN, 4 * NP - 0:4 * NP + NT * RF].rearrange("p (t m) -> p t m", t=NT)

        def qk1(which, b):
            o = (2 * which + b) * NP
            return RG[4][:, o:o + NP]
        hid = [RG[7][0:TN, u * D:(u + 1) * D] for u in range(5)]
        w1s = RG[3][:, 0:C * FF].rearrange("p (c f) -> p c f", c=C)
        w2s = RG[3][0:96, C * FF:C * FF + 2 * D].rearrange("p (c n) -> p c n", c=2)
        b2s = RG[3][0:TN, 2688:2688 + D]
        fh = RG[4][0:96, 0:2 * NP].rearrange("p (m n) -> p m n", m=2)
        neg = RG[7][0:TN, 0:1565].bitcast(BF16)[:, 0:NT * N].rearrange("p (t n) -> p t n", t=NT)
        lsum = sb("lsum", [128, C])
        gsm = sb("gsm", [128, 32])
        P_REGION = [8, 0]
        masks = RG[4][:, 0:1884].bitcast(BF16).rearrange("p (t n) -> p t n", t=TYPES)
        typed = [RG[4][:, 1884 + u * NP:1884 + (u + 1) * NP] for u in range(2)]
        types_i = RG[4][:, 3200:3200 + NP].bitcast(I32)
        msg = [RG[r][:, at:at + D] for r, at in ((4, 4 * NP), (5, NT * 626), (6, NT * 626))]
        msg += [oh_raw[:, 500:500 + D], mix0_consts[:, 0:D], rowbuf[0][:, :]]
        NM = len(msg)
        S4 = RG[7][0:TN, 0:NT * 770].rearrange("p (t b n) -> p t b n", t=NT, b=2)
        ewsum = oh_raw[0:1, 0:NP]
        msg_b2 = oh_raw[0:1, 700:700 + D]
        sel = RG[6][0:EXPERTS, 640:640 + 2 * D]
        gT = RG[6][0:EXPERTS, 0:NP]
        silu = [RG[6][:, 2180 + u * NP:2180 + (u + 1) * NP] for u in range(2)]
        gate_v = RG[6][0:TN, 3440:3440 + NT * EXPERTS * 5].rearrange("p (k t e) -> p k t e", k=5, t=NT)
        gq = RG[6][0:TN, 3640:3640 + 4 * NT].rearrange("p (k t) -> p k t", k=4)

        def split_T(r):
            return RG_R[r][:, 0:C * NP].rearrange("p (c n) -> p c n", c=C)

        def weight_high(n):
            return RG_R[7 + n % 10 // 5][:, n % 5 * D:(n % 5 + 1) * D]

        def weight_chunk(panel, c, ring=ring):
            return ring[(2 * pindex[panel] + c // 3) % 5][:, c % 3, :]

        high_at = {}

        def places(panel, *at):
            for c, (buf, k) in enumerate(at):
                high_at[panel, c] = buf[:, k * D:(k + 1) * D]
        places("msgU", (oh_raw_r, 0), (oh_raw_r, 1), *[(RG_R[4], k) for k in range(4)])
        places("msgV", *[(RG_R[8], k) for k in range(5)], (mix0_consts_r, 0))

        places("msg2", *[(RG_R[8], k) for k in range(5)], (mix0_consts_r, 0))
        places("agg1", (rowbuf_r[0], 0), *[(RG_R[8], k) for k in range(5)])
        places("agg2", (oh_raw_r, 0), (oh_raw_r, 1), (mix0_consts_r, 0), *[(RG_R[8], k) for k in range(3)])
        places("outW", *[(RG_R[7], k) for k in range(5)], (rowbuf_r[0], 0))
        places("moe1a", *[(RG_R[8], k) for k in range(5)], (oh_raw_r, 0))
        places("Wproj1", *[(RG_R[4], k) for k in range(5)], (mix0_consts_r, 0))
        places("moe1b", *[(RG_R[7], k) for k in range(5)], (oh_raw_r, 1))
        places("moe2a", *[(RG_R[8], k) for k in range(5)], (oh_raw_r, 0))
        places("moe2b", *[(RG_R[7], k) for k in range(5)], (oh_raw_r, 1))

        def hidden_at(j, RG=RG):
            return RG[3 if j < C else 1][:, j % C * NP:(j % C + 1) * NP]

        def hidden_high(j):
            return RG_R[2 if j < C else 5][:, j % C * NP:(j % C + 1) * NP]

        def low_part(eng, panel, c):
            eng.wait_ge(sem(f"high_{panel}"), c + 1)
            eng.tensor_tensor(weight_chunk(panel, c, ring_r), weight_chunk(panel, c), high_at[panel, c].bitcast(F32),
                              ALU.subtract).then_inc(split_of(panel, c)[0], 1)

        def split_of(panel, c):
            if panel == "agg2" and c >= 3:
                return sem("split_agg2_last"), c - 2
            return sem(f"split_{panel}"), c + 1

        u_dram = nc.dram_tensor("msg_source_part", [N, D], F32, kind="Internal").ap()
        v_dram = nc.dram_tensor("msg_target_part", [N, D], F32, kind="Internal").ap()
        typed_dram = nc.dram_tensor("typed_nodes", [128, C * NP], F32, kind="Internal").ap()
        mixed_dram = nc.dram_tensor("mixed", [N, D], F32, kind="Internal").ap()

        mixer1 = [("V1", t) for t in range(NT)]
        for h in range(MH):
            mixer1 += ([("q1_", h // 2), ("k1_", h // 2)] if h % 2 == 0 else []) + [(f"sc{h}_", s) for s in range(NT)]
            mixer1 += [("ao", h - 1)] if h else []
        mixer1.append(("ao", MH - 1))

        def tiles_behind(groups, k, first):
            n = len(groups) - first
            return range(ST * (k - first) // n, ST * (k + 1 - first) // n) if k >= first else range(0)

        mixer0 = []
        for c in range(C):
            mixer0.append(("q", c, 0))
            mixer0 += [("mo", 2 * c - 2, 0), ("kv", 2 * c - 1, 0)] if c else []
            mixer0.append(("k", c, 0))
            mixer0 += [("mo", 2 * c - 1, 0)] if c else []
            mixer0 += [(nm, h, m) for nm in ("qp", "kp") for h in (2 * c, 2 * c + 1) for m in range(2)]
            mixer0.append(("kv", 2 * c, 0))
        mixer0 += [("mo", MH - 2, 0), ("kv", MH - 1, 0), ("mo", MH - 1, 0)]

        beside_edges = [("xnT", c) for c in range(C)] + [("x1T", m) for m in range(C)] + [("V", t) for t in range(NT)]
        FIRST_BESIDE = 5

        def edge_tiles(s):
            return min(4, EJ - 4 * s)

        def behind_edges(s):
            k = s - FIRST_BESIDE
            return beside_edges[k:k + 1] if 0 <= k else []
        assert ES - FIRST_BESIDE >= len(beside_edges)


        block = ctx.enter_context(nc.Block())

        @block.tensor
        def _(pe):
            def transposes_part(name, src, c, ready=None, count=0):
                ps, full = psum.open(pe, f"{name}{c}")
                if ready is not None:
                    pe.wait_ge(ready, count)
                for t in range(NT):
                    last = pe.transpose(ps[:, t * 128:t * 128 + TN], src(t, c), ident[0:TN, 0:TN])
                last.then_inc(full, 1)

            def transposes(name, src, ready=None, count=0):
                for c in range(C):
                    transposes_part(name, src, c, ready, count)

            def linear_R(name, panels, chunk):
                n = C * len(panels)
                for t in range(NT):
                    ps, full = psum.open(pe, f"{name}{t}")
                    for c in range(n):
                        w = weights(pe, panels[c // C], c % C)
                        for h in range(2):
                            last = pe.matmul(ps[0:TN, 512 * h:512 * h + 384], chunk(c)[:, t * TN:(t + 1) * TN],
                                             w[:, h * 384:(h + 1) * 384], start=(c == 0), stop=(c == n - 1))
                    last.then_inc(full, 1)
                for p in panels:
                    panel_last[p] = f"{name}{NT - 1}"

            def chunk_of(r):
                return lambda c: asT(r)[:, c, :]

            def of_R(r):
                return lambda t, c: asR(r)[:, t, c * 128:(c + 1) * 128]

            pe.wait_ge(sem("consts"), 2)
            pe.wait_ge(sem("small_loads"), 16 * 6)

            def hidden(s):
                ps, full = psum.open(pe, f"hidden{s}")
                pe.wait_ge(sem(f"attr_loaded{s % 7}"), 16 * (s // 7 + 1))
                for i in range(edge_tiles(s)):
                    at = 512 * (i // 2) + FF * (i % 2)
                    last = pe.matmul(ps[0:TN, at:at + FF], attr_of(s)[:, i * TN:(i + 1) * TN], edge_w1,
                                     start=True, stop=True)
                last.then_inc(full, 1)

            def ranks():
                ps, full = psum.open(pe, "rank")
                pe.wait_ge(sem("rank_totals"), 1)
                pe.matmul(ps[0:TN, 0:NT], sv("tri"), sv("tot"), start=True, stop=True)
                pe.matmul(ps[:, 512:512 + NT], one[0:TN, :].broadcast_to([TN, 128]), sv("tot"),
                          start=True, stop=True).then_inc(full, 1)

            def linear_T_part(name, panel, xT, m, reads=1):
                ps, full = psum.open(pe, f"{name}{m}", reads)
                for c in range(C):
                    w = weights(pe, panel, c)
                    for h in range(2):
                        last = pe.matmul(ps[:, 512 * h:512 * h + HN], w[:, m * 128:(m + 1) * 128],
                                         xT[:, c, h * HN:(h + 1) * HN], start=(c == 0), stop=(c == C - 1))
                last.then_inc(full, 1)
                panel_last[panel] = f"{name}{m}"

            def linear_R_part(name, panel, xT, t):
                ps, full = psum.open(pe, f"{name}{t}")
                for c in range(C):
                    w = weights(pe, panel, c)
                    for h in range(2):
                        last = pe.matmul(ps[0:TN, 512 * h:512 * h + 384], xT[:, c, t * TN:(t + 1) * TN],
                                         w[:, h * 384:(h + 1) * 384], start=(c == 0), stop=(c == C - 1))
                last.then_inc(full, 1)
                panel_last[panel] = f"{name}{t}"
            for s in range(max(ES, FIRST_BESIDE + len(beside_edges))):
                if s < ES:
                    hidden(s)
                if s == 1:
                    ranks()
                for nm, k in behind_edges(s):
                    if nm == "xnT":
                        transposes_part("xnT", of_R(1), k, sem("normed"), 1)
                    elif nm == "x1T":
                        if k == 0:
                            psum.drained(pe, *[f"xnT{c}" for c in range(C)])
                        linear_T_part("x1T", "W_ah", asT(2), k)
                    else:
                        linear_R_part("V", "Wv", asT(2), k)

            ps, full = psum.open(pe, "sorted")

            def permute(j, u, first=False, final=False):
                pe.wait_ge(sem("onehot_edge"), j + 1)
                return pe.matmul(ps[:, 0:3 * ST], oh_lo(u), oh_raw[0:TN, 512 + u * 3 * ST:512 + (u + 1) * 3 * ST],
                                 start=first, stop=final, skip_group_check=True)
            for u in range(4):
                permute(u, u, first=(u == 0)).then_inc(sem("onehot_used"), 1)
            with pe.Fori(1, EJ // 4) as i:
                for u in range(4):
                    permute(4 * i + u, u).then_inc(sem("onehot_used"), 1)
            permute(EJ - 1, 0, final=True).then_inc(full, 1)

            def count_edges(j):
                ps, full = psum.open(pe, f"counts{j}")
                pe.wait_ge(sem("onehot_dst"), j + 1)
                for t in range(NT):
                    last = pe.matmul(ps[0:TN, t * 128:t * 128 + TN], oh_src(j % 4)[:, t * TN:(t + 1) * TN],
                                     oh_dst(j % 4)[:, 0:TN], start=True, stop=True)
                last.then_inc(full, 1)

            def mix0_query_features(h, m):
                c, odd = h // 2, h % 2
                ps, full = psum.open(pe, f"qp{h}_{m}")
                if m == 0:
                    pe.wait_ge(sem("squares"), 4 * c + 2)
                for x in range(2):
                    last = pe.matmul(ps[:, 512 * x:512 * x + HN], (rfo if odd else rfe)[:, m * 128:(m + 1) * 128],
                                     eqk(0, odd)[:, x * HN:(x + 1) * HN], start=True, stop=True)
                last.then_inc(full, 1)

            def mix0_key_features(h, part):
                odd = h % 2
                ps, full = psum.open(pe, f"kp{h}{'ab'[part]}")
                if part == 0:
                    pe.wait_ge(sem("squares"), 4 * (h // 2) + 4)
                for t in (range(4, 5) if part else range(4)):
                    last = pe.matmul(ps[0:TN, (t % 4) * RF:(t % 4 + 1) * RF], eqk(1, odd)[:, t * TN:(t + 1) * TN],
                                     rfo if odd else rfe, start=True, stop=True)
                last.then_inc(full, 1)

            def mix0_key_values(h):
                b = h % 2
                ps, full = psum.open(pe, f"kv{h}")
                psum.drained(pe, f"kp{h}a", f"kp{h}b", *([f"V{t}" for t in range(NT)] if h == 0 else []))
                for m in range(2):
                    for t in range(NT):
                        last = pe.matmul(ps[:, 512 * m:512 * m + 65], kp(b)[:, t, m * 128:(m + 1) * 128],
                                         asV(4)[:, t, h, :], start=(t == 0), stop=(t == NT - 1))
                last.then_inc(full, 1)

            def mix0_out(h):
                b = h % 2
                ps, full = psum.open(pe, f"mo{h}")
                psum.drained(pe, f"kv{h}", f"qp{h}_0", f"qp{h}_1")
                for t in range(NT):
                    for m in range(2):
                        last = pe.matmul(ps[0:TN, t * 65:(t + 1) * 65], qp(b)[:, m, t * TN:(t + 1) * TN],
                                         kvs[:, b, m, :], start=(m == 0), stop=(m == 1))
                last.then_inc(full, 1)
            for k, (nm, n, part) in enumerate(mixer0):
                if nm in ("q", "k"):
                    linear_T_part(nm, "Wq" if nm == "q" else "Wk", asT(2), n, 2)
                elif nm == "qp":
                    mix0_query_features(n, part)
                elif nm == "kp":
                    mix0_key_features(n, part)
                elif nm == "kv":
                    mix0_key_values(n)
                else:
                    mix0_out(n)
                for j in tiles_behind(mixer0, k, 0):
                    count_edges(j)
            psum.drained(pe, f"mo{MH - 1}")
            transposes("moT", of_R(5))
            for t in range(NT):
                ps, full = psum.open(pe, f"A{t}")
                psum.drained(pe, *[f"counts{j}" for j in range(ST - 4, ST)])
                for s in range(NT):
                    last = pe.transpose(ps[0:TN, s * 128:s * 128 + TN], asN(6)[:, s, t * TN:(t + 1) * TN],
                                        ident[0:TN, 0:TN])
                last.then_inc(full, 1)
            linear_R("h0_", ["W0"], chunk_of(3))
            psum.drained(pe, *[f"moT{c}" for c in range(C)])

            def with_sources(g, name, panel, xT):
                for t in range(NT):
                    linear_R_part(name, panel, xT, t)
                    if g < 3 and t < GH:
                        ps, full = psum.open(pe, f"asb{g}{t}")
                        pe.wait_ge(sem("scores_src"), g + 1)
                        for s in range(NT):
                            last = pe.matmul(ps[0:TN, s * 128:s * 128 + TN],
                                             asd[0:TN, 0, s, t:t + 1].broadcast_to([TN, TN]),
                                             ident[0:TN, 0:TN], start=True, stop=True)
                        last.then_inc(full, 1)
            with_sources(0, "mp", "Wproj", asT(8))

            for g in range(3):

                def offsets(hh):
                    for k in range(2):
                        ps, full = psum.open(pe, f"off{g}{hh}{k}", NT)
                        pe.wait_ge(sem("offsets"), 2 * (g + 1))
                        for t in range(NT):
                            last = pe.matmul(ps[0:TN, t * 128:t * 128 + TN],
                                             asd[0:TN, 5 + k, t, hh:hh + 1].broadcast_to([TN, TN]),
                                             ident[0:TN, 0:TN], start=True, stop=True)
                        last.then_inc(full, 1)

                def attend(hh):
                    P = asN(P_REGION[hh % 2])
                    for part, tiles in (("a", range(4)), ("b", range(4, 5))):
                        ps, full = psum.open(pe, f"gat{g}{hh}{part}")
                        pe.wait_ge(sem("attention"), NT * (GH * g + hh + 1))
                        for t in tiles:
                            for s in range(NT):
                                last = pe.matmul(ps[0:TN, (t % 4) * 256:(t % 4) * 256 + 193],
                                                 P[:, s, t * TN:(t + 1) * TN], asG(4)[:, s, hh, :],
                                                 start=(s == 0), stop=(s == NT - 1))
                        last.then_inc(full, 1)
                offsets(0)
                offsets(1)
                for hh in range(GH):
                    attend(hh)
                    if hh + 2 < GH:
                        offsets(hh + 2)
                if g < 2:
                    linear_R(f"h{g + 1}_", [f"W{g + 1}"], chunk_of(3))
                for c in range(C):
                    ps, full = psum.open(pe, f"embT{g}_{c}")
                    if c == 0:
                        psum.drained(pe, f"gat{g}{GH - 1}a", f"gat{g}{GH - 1}b")
                    for t in range(NT):
                        last = pe.transpose(ps[:, t * 128:t * 128 + TN], asR(5)[:, t, c * 128:(c + 1) * 128],
                                            ident[0:TN, 0:TN])
                    last.then_inc(full, 1)
                psum.drained(pe, *[f"embT{g}_{c}" for c in range(C)])
                with_sources(g + 1, f"wo{g}_", f"Wout{g}", asT(2))

            transposes("xlT", of_R(5), sem("normed"), 3)
            ps, full = psum.open(pe, "gate")
            psum.drained(pe, *[f"xlT{c}" for c in range(C)])
            pe.wait_ge(sem("sums"), 1)
            for c in range(C):
                last = pe.matmul(ps[:, 0:3], lsum[:, c:c + 1].broadcast_to([128, 128]),
                                 cols[:, PL["wg"][0] + 3 * c:PL["wg"][0] + 3 * c + 3], start=(c == 0), stop=(c == C - 1))
            last.then_inc(full, 1)
            pe.wait_ge(sem("first_chosen"), 1)
            for m in range(2):
                ps, full = psum.open(pe, f"f1_{m}")
                for c in range(C):
                    for h in range(2):
                        last = pe.matmul(ps[0:96, 512 * h:512 * h + HN], w1s[:, c, m * 96:(m + 1) * 96],
                                         asT(2)[:, c, h * HN:(h + 1) * HN], start=(c == 0), stop=(c == C - 1))
                last.then_inc(full, 1)
            for t in range(NT):
                ps, full = psum.open(pe, f"f2_{t}")
                if t == 0:
                    pe.wait_ge(sem("chosen"), 1)
                    psum.drained(pe, "f1_0", "f1_1")
                for m in range(2):
                    for h in range(2):
                        last = pe.matmul(ps[0:TN, 512 * h:512 * h + 384], fh[:, m, t * TN:(t + 1) * TN],
                                         w2s[:, m, h * 384:(h + 1) * 384], start=(m == 0), stop=(m == 1))
                last.then_inc(full, 1)
            if stop == "L0":
                return

            transposes("x1nT", of_R(1), sem("normed"), 4)
            for t in range(TYPES):
                for m in range(C):
                    ps, full = psum.open(pe, f"ty{t}_{m}")
                    rows = slice(m * 128, (m + 1) * 128)
                    for c in range(C):
                        n = C * t + c
                        if m == 0:
                            pe.wait_ge(sem("types_split_pool" if c < 4 else "types_split_dve"),
                                       4 * t + c + 1 if c < 4 else 2 * t + c - 3)
                            if t == 0:
                                pe.wait_ge(sem("nodes_low"), c + 1)
                        wh, wl = weight_high(n)[:, rows], weight_chunk(f"Wt{t}", c, ring_r)[:, rows]
                        for k, (w, x) in enumerate(((wh, 5), (wh, 6), (wl, 5))):
                            for h in range(2):
                                last = pe.matmul(ps[:, 512 * h:512 * h + HN], w,
                                                 split_T(x)[:, c, h * HN:(h + 1) * HN],
                                                 start=(c == 0 and k == 0), stop=(c == C - 1 and k == 2))
                    last.then_inc(full, 1)
                panel_last[f"Wt{t}"] = f"ty{t}_{C - 1}"
            def split_linear_R(name, panels, high, low, ready):
                for t in range(NT):
                    ps, full = psum.open(pe, f"{name}{t}")
                    nodes = slice(t * TN, t * TN + TN + 1)
                    for c in range(C * len(panels)):
                        panel = panels[c // C]
                        if t == 0:
                            pe.wait_ge(sem(f"split_{panel}"), c % C + 1)
                            pe.wait_ge(sem(ready), c + 1)
                        wh, wl = high_at[panel, c % C], weight_chunk(panel, c % C, ring_r)
                        xh, xl = high(c)[:, nodes], low(c)[:, nodes]
                        for k, (x, w) in enumerate(((xh, wh), (xh, wl), (xl, wh))):
                            for h in range(2):
                                last = pe.matmul(ps[0:TN + 1, 512 * h:512 * h + 384], x, w[:, h * 384:(h + 1) * 384],
                                                 start=(c == 0 and k == 0),
                                                 stop=(c == C * len(panels) - 1 and k == 2))
                    last.then_inc(full, 1)
                for panel in panels:
                    panel_last[panel] = f"{name}{NT - 1}"
            for name, panel in (("U", "msgU"), ("Vm", "msgV")):
                split_linear_R(name, [panel], lambda c: split_T(5)[:, c, :], lambda c: split_T(6)[:, c, :], "typed_low")
            def mix1_scores(h, s):
                c, o = h // 2, 64 * (h % 2)
                ps, full = psum.open(pe, f"sc{h}_{s}")
                if s == 0:
                    psum.drained(pe, f"q1_{c}", f"k1_{c}")
                for x in range(2):
                    last = pe.matmul(ps[0:TN, 512 * x:512 * x + 313], qk1(1, c % 2)[o:o + 64, s * TN:(s + 1) * TN],
                                     qk1(0, c % 2)[o:o + 64, x * 313:(x + 1) * 313], start=True, stop=True)
                last.then_inc(full, 1)

            def mix1_out(h):
                P = asN(5 + h % 2, 626)
                ps, full = psum.open(pe, f"ao{h}")
                psum.drained(pe, *[f"sc{h}_{s}" for s in range(NT)], *([f"V1{t}" for t in range(NT)] if h == 0 else []))
                for t in range(NT):
                    for s in range(NT):
                        last = pe.matmul(ps[0:TN, t * 65:(t + 1) * 65], P[:, s, t * TN:(t + 1) * TN],
                                         asV(3)[:, s, h, :], start=(s == 0), stop=(s == NT - 1))
                last.then_inc(full, 1)

            def scatter(j):
                ps, full = psum.open(pe, f"scattered{j}")
                pe.wait_ge(sem("messages"), j + 1)
                pe.wait_ge(sem("onehot_dst1"), j + 1)
                onehot = oh_dst32(j % 4)
                for b in range(2):
                    pe.matmul(ps[0:TN, 512 * b:512 * b + 384], onehot, msg[j % NM][:, 384 * b:384 * (b + 1)],
                              start=True, stop=True)
                pe.matmul(ps[0:TN, 384:385], onehot, slots[:, 2, j:j + 1], start=True, stop=True).then_inc(full, 1)
            for k, (nm, n) in enumerate(mixer1):
                if nm == "V1":
                    linear_R_part("V1", "Wv1", asT(2), n)
                elif nm in ("q1_", "k1_"):
                    linear_T_part(nm, "Wq1" if nm == "q1_" else "Wk1", asT(2), n)
                elif nm == "ao":
                    mix1_out(n)
                else:
                    mix1_scores(int(nm[2:-1]), n)
                for j in tiles_behind(mixer1, k, 2):
                    scatter(j)

            psum.drained(pe, f"ao{MH - 1}")
            transposes("aoT", of_R(8))
            psum.drained(pe, *[f"scattered{j}" for j in range(ST - 4, ST)])
            transposes("ST", lambda t, c: S4[:, t, c // 3, (c % 3) * 128:(c % 3 + 1) * 128])
            ps, full = psum.open(pe, "ewT")
            for t in range(NT):
                last = pe.transpose(ps[0:1, t * 128:t * 128 + TN], S4[:, t, 0, 384:385], ident[0:TN, 0:TN])
            last.then_inc(full, 1)
            psum.drained(pe, *[f"ST{c}" for c in range(C)], "ewT")
            pe.wait_ge(sem("msg_b2"), 16)
            pe.wait_ge(sem("ewsum_padded"), 1)

            def split_linear_T(name, panel, high, low, ready, outer=None, reads=1):
                for m in range(C):
                    ps, full = psum.open(pe, f"{name}{m}", reads)
                    rows = slice(m * 128, (m + 1) * 128)
                    if outer is not None:
                        for h in range(2):
                            pe.matmul(ps[:, 512 * h:512 * h + HN], outer[0][:, rows],
                                      outer[1][:, h * HN:(h + 1) * HN], start=True, stop=False)
                    for c in range(C):
                        if m == 0:
                            pe.wait_ge(*split_of(panel, c))
                            ready(c)
                        wh, wl = high_at[panel, c][:, rows], weight_chunk(panel, c, ring_r)[:, rows]
                        for k, (w, x) in enumerate(((wh, high), (wh, low), (wl, high))):
                            for h in range(2):
                                last = pe.matmul(ps[:, 512 * h:512 * h + HN], w,
                                                 split_T(x)[:, c, h * HN:(h + 1) * HN],
                                                 start=(c == 0 and k == 0 and outer is None),
                                                 stop=(c == C - 1 and k == 2))
                    last.then_inc(full, 1)
                panel_last[panel] = f"{name}{C - 1}"
            split_linear_T("m2_", "msg2", 2, 4, lambda c: pe.wait_ge(sem("sums_low"), c + 1), outer=(msg_b2, ewsum), reads=2)
            split_linear_T("a1_", "agg1", 6, 7, lambda c: psum.drained(pe, f"m2_{c}"))
            split_linear_T("a2_", "agg2", 2, 4, lambda c: pe.wait_ge(sem("a1_low"), c + 1))
            split_linear_R("o_", ["outW"], lambda c: split_T(6)[:, c, :], lambda c: split_T(3)[:, c, :], "aggregated_low")
            split_linear_R("p1_", ["Wproj1"], lambda c: split_T(2)[:, c, :], lambda c: split_T(5)[:, c, :], "ao_low")

            transposes("tokT", of_R(3), sem("tokens"), 2)
            ps, full = psum.open(pe, "router")
            psum.drained(pe, *[f"tokT{c}" for c in range(C)])
            for t in range(NT):
                for c in range(C):
                    last = pe.matmul(ps[0:TN, t * 8:t * 8 + 8], asT(2)[:, c, t * TN:(t + 1) * TN],
                                     cols[:, PL["rw"][0] + 8 * c:PL["rw"][0] + 8 * c + 8],
                                     start=(c == 0), stop=(c == C - 1))
            last.then_inc(full, 1)

            def up(j):
                ps, full = psum.open(pe, f"up{j}")
                panel = "moe1a" if j < C else "moe1b"
                rows = slice(j % C * 128, (j % C + 1) * 128)
                for c in range(C):
                    if j % C == 0:
                        pe.wait_ge(sem(f"split_{panel}"), c + 1)
                        pe.wait_ge(sem("tokens_low"), c + 1)
                    wh, wl = high_at[panel, c][:, rows], weight_chunk(panel, c, ring_r)[:, rows]
                    for k, (w, x) in enumerate(((wh, 5), (wh, 4), (wl, 5))):
                        for h in range(2):
                            last = pe.matmul(ps[:, 512 * h:512 * h + HN], w, split_T(x)[:, c, h * HN:(h + 1) * HN],
                                             start=(c == 0 and k == 0), stop=(c == C - 1 and k == 2))
                last.then_inc(full, 1)

            def gates_of(j):
                ps, full = psum.open(pe, f"gb{j}")
                for h in range(2):
                    last = pe.matmul(ps[:, 512 * h:512 * h + HN], sel[:, j * 128:(j + 1) * 128],
                                     gT[:, h * HN:(h + 1) * HN], start=True, stop=True)
                last.then_inc(full, 1)
            up(0)
            ps, full = psum.open(pe, "gT")
            pe.wait_ge(sem("gates"), 1)
            for t in range(NT):
                last = pe.transpose(ps[0:EXPERTS, t * 128:t * 128 + TN], gate_v[:, 3, t, :], ident[0:TN, 0:TN])
            last.then_inc(full, 1)
            psum.drained(pe, "gT")
            pe.wait_ge(sem("sel"), 3)
            for j in range(12):
                gates_of(j)
                if j + 1 < 12:
                    up(j + 1)
            panel_last["moe1a"], panel_last["moe1b"] = "up5", "up11"
            split_linear_R("y_", ["moe2a", "moe2b"], hidden_high, lambda j: hidden_at(j, RG_R), "hidden_low")

        @block.sync
        def _(sp):
            def attr(s):
                if s >= 7:
                    psum.computed(sp, f"hidden{s - 7}")
                n = TN * edge_tiles(s)
                sp.dma_start(attr_of(s)[:, 0:n], a["attrT"][:, s * EC:s * EC + n])\
                  .then_inc(sem(f"attr_loaded{s % 7}"), 16)

            def half(q):
                name, w, c0, n, p = PANELS[q // 2]
                if q >= 5:
                    prev = PANELS[(q - 5) // 2][0]
                    if prev in panel_last:
                        psum.computed(sp, panel_last[prev])
                    else:
                        sp.wait_ge(sem("chosen"), 1)
                if name == "msg2":
                    psum.computed(sp, f"scattered{ST - 4}")
                src = w.rearrange("(c p) n -> p c n", p=p)[:, 3 * (q % 2):3 * (q % 2) + 3, c0:c0 + n]
                sp.dma_start(ring[q % 5][0:p, :, 0:n], src).then_inc(sem(f"weights_loaded{q % 5}"), 16)

            def load_row(k):
                if k >= 3:
                    sp.wait_ge(sem("row_used"), k - 2)
                sp.dma_start(rowbuf[k % 3][0:TN, :], a["rows"][k:k + 1, :].broadcast_to([TN, D]))\
                  .then_inc(sem(f"row_loaded{k % 3}"), 16)

            sp.dma_start(srcdst, a["srcdst"]).then_inc(sem("edges_loaded"), 16)
            for s in range(7):
                attr(s)
            sp.dma_start(asR(0), a["x"].rearrange("(t p) d -> p t d", p=TN)).then_inc(sem("x_loaded"), 16)
            for q in range(5):
                half(q)
            for k in range(3):
                load_row(k)
            for s in range(7, ES):
                attr(s)
            behind = {"W1": [3, 4, 5], "Wout0": [6, 7], "W2": [8, 9], "Wout1": [10, 11], "ffn1": [12],
                      "Wt0": [13, 14, 15], "Wk1": [16, 17]}
            for q in range(5, 2 * len(PANELS)):
                half(q)
                if q % 2:
                    for k in behind.get(PANELS[q // 2][0], []):
                        load_row(k)
            if stop == "L0":
                sp.wait_ge(sem("final"), 1)
                sp.dma_start(a["out"].rearrange("(t p) d -> p t d", p=TN), asR(0)).then_inc(sem("stored"), 16)
                sp.wait_ge(sem("stored"), 16)
                return
            for t in range(NT):
                psum.drained(sp, f"y_{t}")
                sp.dma_start(a["out"][t * TN:(t + 1) * TN, :], asR(0)[:, t, :]).then_inc(sem("stored"), 16)
            sp.wait_ge(sem("stored"), 16 * NT)

        @block.scalar
        def _(act):
            A = act.activation

            def root(k, lo=0, hi=NT):
                act.wait_ge(sem("ln_inverse"), k)
                A(lnt[0:TN, 2, lo:hi], lnt[0:TN, 1, lo:hi], ACT.Sqrt).then_inc(sem("ln_root"), 1)

            act.dma_start(cols[:, :], a["cols"]).then_inc(sem("small_loads"), 16)
            act.dma_start(edge_w1, a["edge_W1"]).then_inc(sem("small_loads"), 16)
            act.dma_start(eb2[:, :], a["edge_b2"].broadcast_to([128, 1])).then_inc(sem("small_loads"), 16)
            act.dma_start(rfe[0:64, :], a["rfT"]).then_inc(sem("small_loads"), 16)
            act.dma_start(rfo[64:128, :], a["rfT"]).then_inc(sem("small_loads"), 16)
            act.dma_start(edge_w2, a["edge_w2"].broadcast_to([TN, FF])).then_inc(sem("small_loads"), 16)
            act.wait_ge(sem("small_loads"), 16 * 6)

            def turned(name, r, func=ACT.Identity, bias=None, sums=None, scale=None):
                for c in range(C):
                    ps, free = psum.computed(act, f"{name}{c}")
                    dst = asT(r)[:, c, 0:N].rearrange("p (t n) -> p t n", t=NT)
                    kw = {"bias": col(bias, c)} if bias else {}
                    if scale:
                        kw["scale"] = col(scale, c)
                    if sums is not None:
                        kw["accum_out"] = sums[:, c:c + 1]
                    A(dst, blocks(ps, 128), func, **kw).then_inc(free, 1)

            def turned_part(name, r, c):
                ps, free = psum.computed(act, f"{name}{c}")
                A(asT(r)[:, c, 0:N].rearrange("p (t n) -> p t n", t=NT), blocks(ps, 128), ACT.Identity)\
                    .then_inc(free, 1)

            def values_part(name, r, t):
                ps, free = psum.computed(act, f"{name}{t}")
                A(asV(r)[:, t, :, 0:64].rearrange("p (b h) d -> p b h d", b=2),
                  halves(ps, 384).rearrange("p b (h d) -> p b h d", h=6), ACT.Identity).then_inc(free, 1)

            for s in range(max(ES, FIRST_BESIDE + len(beside_edges))):
                if s < ES:
                    ps, free = psum.computed(act, f"hidden{s}")
                    if s >= 5:
                        act.wait_ge(sem("logits"), s - 4)
                    if edge_tiles(s) == 4:
                        A(two(hid[s % 5]), halves(ps, 2 * FF), ACT.Relu).then_inc(free, 1)
                    else:
                        A(hid[s % 5][:, 0:FF], ps[0:TN, 0:FF], ACT.Relu).then_inc(free, 1)
                if s == 2:
                    root(1)
                for nm, k in behind_edges(s):
                    if nm == "xnT":
                        turned_part("xnT", 2, k)
                    elif nm == "x1T":
                        ps, free = psum.computed(act, f"x1T{k}")
                        A(two(asT(3)[:, k, :]), halves(ps, HN, 0, 128), ACT.Relu, bias=col("b_ah", k)).then_inc(free, 1)
                    else:
                        values_part("V", 4, k)
            act.wait_ge(sem("logits"), ES)
            A(sv("ew"), sv("ew"), ACT.Sigmoid, bias=eb2[0:TN, :]).then_inc(sem("edge_weights"), 1)

            for nm, n, part in mixer0:
                if nm in ("q", "k"):
                    k = int(nm == "k")
                    psum.drained(act, f"{nm}{n}")
                    A(eqk(k, 0)[64:128, :], eqk(k, 0)[0:64, :], ACT.Square).then_inc(sem("squares"), 1)
                    A(eqk(k, 1)[0:64, :], eqk(k, 1)[64:128, :], ACT.Square).then_inc(sem("squares"), 1)
                elif nm == "qp":
                    if n >= 2:
                        psum.computed(act, f"mo{n - 2}")
                    ps, free = psum.computed(act, f"qp{n}_{part}")
                    A(two(qp(n % 2)[:, part, :]), halves(ps, HN, 0, 128), ACT.Exp).then_inc(free, 1)
                elif nm == "kp" and part == 0:
                    ps, free = psum.computed(act, f"kp{n}a")
                    A(kp(n % 2)[:, 0:4, :], ps[0:TN, :].rearrange("p (t m) -> p t m", t=4), ACT.Exp).then_inc(free, 1)
                elif nm == "kp":
                    ps, free = psum.computed(act, f"kp{n}b")
                    A(kp(n % 2)[:, 4, :], ps[0:TN, 0:RF], ACT.Exp).then_inc(free, 1)
            psum.computed(act, f"mo{MH - 1}")
            turned("moT", 8)

            def node_values(g):
                for t in range(NT):
                    ps, free = psum.computed(act, f"h{g}_{t}")
                    A(asG(4)[:, t, :, 0:GC].rearrange("p (b h) d -> p b h d", b=2),
                      halves(ps, 384).rearrange("p b (h d) -> p b h d", h=2), ACT.Identity).then_inc(free, 1)
            node_values(0)
            for g in range(3):
                def weights_of(hh):
                    P = asN(P_REGION[hh % 2])
                    if hh >= 2:
                        psum.computed(act, f"gat{g}{hh - 2}b")
                    elif g:
                        psum.computed(act, f"gat{g - 1}{hh + 2}b")
                    elif hh == 0:
                        psum.computed(act, "mp4")
                    ps, free = psum.computed(act, f"off{g}{hh}1")
                    for s in range(NT + 1):
                        if s < NT:
                            A(P[:, s, :].rearrange("p (t n) -> p t n", t=NT), blocks(ps), ACT.Identity,
                              bias=asd[0:TN, 7, s, hh:hh + 1]).then_inc(free, 1)
                        if s:
                            psum.reads(act, f"off{g}{hh}0", s, NT)
                            A(P[:, s - 1, :], P[:, s - 1, :], ACT.Exp).then_inc(sem("exped"), 1)

                def normalised(hh):
                    for k, (part, tiles) in enumerate((("a", range(4)), ("b", range(4, 5)))):
                        ps, free = psum.computed(act, f"gat{g}{hh}{part}")
                        act.wait_ge(sem("row_inverse"), 2 * (GH * g + hh) + k + 1)
                        if hh == 0 and k == 0:
                            psum.computed(act, f"embT{g - 1}_5" if g else "moT5")
                        for t in tiles:
                            last = A(asR(5)[:, t, hh * GC:(hh + 1) * GC], ps[0:TN, (t % 4) * 256:(t % 4) * 256 + GC],
                                     ACT.Copy, scale=rden[0:TN, 2 * (hh % 2) + 1, t:t + 1])
                        last.then_inc(free, 1)
                weights_of(0)
                weights_of(1)
                for hh in range(GH):
                    normalised(hh)
                    if hh + 2 < GH:
                        weights_of(hh + 2)
                if g == 0:
                    root(2)
                if g < 2:
                    node_values(g + 1)
                psum.computed(act, f"wo{g - 1}_4" if g else "k5")
                turned(f"embT{g}_", 2, ACT.Relu, f"b{g}")

            root(3, 0, 3)
            root(4, 3, NT)
            psum.computed(act, "wo2_4")
            turned("xlT", 2, sums=lsum)
            act.wait_ge(sem("gate_shifted"), 1)
            A(gsm[:, 3:6], gsm[:, 0:3], ACT.Exp).then_inc(sem("gate_exp"), 1)
            act.wait_ge(sem("first_chosen"), 1)
            for m in range(2):
                ps, free = psum.computed(act, f"f1_{m}")
                A(two(fh[:, m, :]), halves(ps, HN, 0, 96), ACT.Gelu, bias=gsm[0:96, 29 + m:30 + m]).then_inc(free, 1)
            if stop == "L0":
                return

            root(5)
            psum.computed(act, "f1_1")
            def type_weights_high(t):
                for c in range(C):
                    n = C * t + c
                    w = weights(act, f"Wt{t}", c)
                    if n >= 10:
                        psum.computed(act, f"ty{(n - 10) // C}_5")
                    A(weight_high(n), w, ACT.Identity).then_inc(sem("types_high"), 1)
            type_weights_high(0)
            turned("x1nT", 2)
            for c in range(C):
                psum.drained(act, f"x1nT{c}")
                A(split_T(5)[:, c, :], asT(2)[:, c, :], ACT.Identity).then_inc(sem("nodes_high"), 1)
            for t in range(1, TYPES):
                type_weights_high(t)

            def high_part(panel, c):
                A(high_at[panel, c], weights(act, panel, c), ACT.Identity).then_inc(sem(f"high_{panel}"), 1)
            psum.computed(act, "ty5_5")
            high_part("msgU", 0)
            high_part("msgU", 1)
            for c in range(C):
                act.wait_ge(sem("typed"), C * (TYPES - 2) + c + 1)
                A(split_T(5)[:, c, :], asT(3)[:, c, :], ACT.Identity).then_inc(sem("typed_high"), 1)
                if c >= 2:
                    if c == 2:
                        act.wait_ge(sem("typed"), C * (TYPES - 1))
                    high_part("msgU", c)
            for c in range(C):
                high_part("msgV", c)
            psum.computed(act, "xlT5")
            for nm, r in (("U", 7), ("Vm", 4)):
                if nm == "Vm":
                    psum.computed(act, "U4")
                for t in range(NT):
                    ps, free = psum.computed(act, f"{nm}{t}")
                    A(two(asR(r)[:, t, :]), halves(ps, 384), ACT.Identity).then_inc(free, 1)
            two_col = gsm[:, 31:32]

            def message(j):
                act.wait_ge(sem(f"gathered{j % NM}"), 16 * (j // NM + 1))
                A(msg[j % NM], msg[j % NM], ACT.Relu, scale=slots[:, 2, j:j + 1]).then_inc(sem("messages"), 1)
            for k, (nm, n) in enumerate(mixer1):
                for j in tiles_behind(mixer1, k, 2):
                    message(j)
                if nm == "V1":
                    if n == 0:
                        act.wait_ge(sem("typed_spilled"), 16)
                        act.wait_ge(sem("ones1"), 1)
                    values_part("V1", 3, n)
                elif nm == "q1_":
                    if n == 0:
                        act.wait_ge(sem("target_part_stored"), 16)
                    ps, free = psum.computed(act, f"q1_{n}")
                    if n >= 2:
                        psum.computed(act, f"sc{2 * n - 3}_4")
                    A(two(qk1(0, n % 2)), halves(ps, HN, 0, 128), ACT.Identity).then_inc(free, 1)
                elif nm[0:2] == "sc":
                    h = int(nm[2:-1])
                    if n == 0:
                        if h >= 2:
                            psum.computed(act, f"ao{h - 2}")
                        psum.computed(act, "Vm4")
                    ps, free = psum.computed(act, f"sc{h}_{n}")
                    A(two(asN(5 + h % 2, 626)[:, n, :]), halves(ps, 313), ACT.Relu, bias=two_col[0:TN, :],
                      scale=0.0625).then_inc(free, 1)
            psum.computed(act, f"ao{MH - 1}")
            turned("aoT", 5)
            turned("ST", 4)
            ps, free = psum.computed(act, "ewT")
            A(ewsum[:, 0:N].rearrange("p (t n) -> p t n", t=NT), blocks(ps, 1), ACT.Identity).then_inc(free, 1)
            for c in range(C):
                if c == 0:
                    psum.computed(act, "aoT5")
                high_part("msg2", c)
            for c in range(C):
                psum.drained(act, f"ST{c}")
                A(split_T(2)[:, c, :], asT(4)[:, c, :], ACT.Identity).then_inc(sem("sums_high"), 1)
            high_part("agg1", 0)
            for m in range(C):
                ps, free = psum.computed(act, f"m2_{m}")
                A(two(split_T(6)[:, m, :]), halves(ps, HN, 0, 128), ACT.Identity).then_inc(free, 1)
            for c in range(1, C):
                high_part("agg1", c)
            for c in range(3):
                high_part("agg2", c)
            for m in range(C):
                ps, free = psum.computed(act, f"a1_{m}")
                A(two(asT(4)[:, m, :]), halves(ps, HN, 0, 128), ACT.Relu, bias=col("agg_b1", m)).then_inc(free, 1)
                psum.drained(act, f"a1_{m}")
                A(split_T(2)[:, m, :], asT(4)[:, m, :], ACT.Identity).then_inc(sem("a1_high"), 1)
            for c in range(3, C):
                high_part("agg2", c)
            for c in range(C):
                high_part("outW", c)
            for c in range(C):
                psum.drained(act, f"a2_{c}")
                A(split_T(6)[:, c, :], asT(3)[:, c, :], ACT.Identity).then_inc(sem("aggregated_high"), 1)
            for c in range(C):
                if c == 0:
                    psum.computed(act, "a2_5")
                A(split_T(2)[:, c, :], asT(5)[:, c, :], ACT.Identity).then_inc(sem("ao_high"), 1)
                high_part("Wproj1", c)
            for c in range(3):
                high_part("moe1a", c)
            root(6)
            for c in range(3, C):
                high_part("moe1a", c)
            for c in range(3):
                high_part("moe1b", c)
            for k in (7, 8):
                root(k, 0, 3)
            for k in (9, 10):
                root(k, 3, NT)
            turned("tokT", 2, bias="moe_b", scale="moe_g")
            for c in range(C):
                psum.drained(act, f"tokT{c}")
                A(split_T(5)[:, c, :], asT(2)[:, c, :], ACT.Identity).then_inc(sem("tokens_high"), 1)
            act.wait_ge(sem("router_shifted"), 1)
            A(gate_v[:, 1], gate_v[:, 0], ACT.Exp).then_inc(sem("router_exp"), 1)

            def hidden_high_part(j):
                psum.drained(act, f"gb{j}")
                A(hidden_high(j), hidden_at(j), ACT.Identity).then_inc(sem("hidden_high"), 1)
            for j in range(12):
                ps, free = psum.computed(act, f"up{j}")
                if j >= 2:
                    psum.drained(act, f"gb{j - 2}")
                A(two(silu[j % 2]), halves(ps, HN, 0, 128), ACT.Silu).then_inc(free, 1)
                if j == 0:
                    ps, free = psum.computed(act, "gT")
                    A(gT[:, 0:N].rearrange("p (t n) -> p t n", t=NT), blocks(ps, EXPERTS), ACT.Identity)\
                        .then_inc(free, 1)
                if 1 <= j < 4:
                    high_part("moe1b", j + 2)
                if 2 <= j < C + 2:
                    hidden_high_part(j - 2)
                if j >= C:
                    high_part("moe2a", j - C)
            for c in range(C):
                high_part("moe2b", c)
                hidden_high_part(C + c)

        @block.gpsimd
        def _(pool):
            pool.memset(ident[:, :], 0.0).then_inc(sem("pool_memset"), 1)
            pool.memset(sv("tri"), 1.0).then_inc(sem("pool_memset"), 1)
            pool.iota(sv("kio", 128), pattern=[[1, ST]], base=0, channel_multiplier=0,
                      allow_small_or_imprecise_dtypes=True).then_inc(sem("iotas"), 1)
            pool.iota(iota_n[:, :], pattern=[[1, N + 1]], base=0, channel_multiplier=0,
                      allow_small_or_imprecise_dtypes=True).then_inc(sem("iotas"), 1)
            pool.wait_ge(sem("pool_memset"), 2)
            pool.affine_select(out=ident[:, :], in_=ident[:, :], compare_op=ALU.not_equal, fill=1.0, base=0,
                               pattern=[[-1, 128]], channel_multiplier=1).then_inc(sem("consts"), 1)
            pool.affine_select(out=sv("tri"), in_=sv("tri"), compare_op=ALU.is_gt, fill=0.0, base=0,
                               pattern=[[1, TN]], channel_multiplier=-1).then_inc(sem("iotas"), 1)
            pool.iota(gsm[:, 26:29], pattern=[[-1, 3]], base=3, channel_multiplier=0,
                      allow_small_or_imprecise_dtypes=True).then_inc(sem("iotas"), 1)

            for g in range(3):
                for hh in range(GH):
                    P = asN(P_REGION[hh % 2])
                    for s in range(NT):
                        n = NT * (GH * g + hh) + s
                        pool.wait_ge(sem("exped"), n + 1)
                        pool.tensor_tensor(P[:, s, :], P[:, s, :], asN(6)[:, s, :], ALU.mult)\
                            .then_inc(sem("attention"), 1)
                if g == 0:
                    pool.wait_ge(sem("mixed"), 1)
                    pool.dma_start(mixed_dram.rearrange("(t p) d -> p t d", p=TN), asR(1)).then_inc(sem("mix_spilled"), 16)
            psum.computed(pool, "gat23b")
            pool.wait_ge(sem("mix_spilled"), 16)
            pool.dma_start(asR(8), mixed_dram.rearrange("(t p) d -> p t d", p=TN)).then_inc(sem("x_and_mix_back"), 16)
            pool.dma_start(asR(0), a["x"].rearrange("(t p) d -> p t d", p=TN)).then_inc(sem("x_and_mix_back"), 16)

            pool.wait_ge(sem("scored"), 1)
            psum.computed(pool, "xlT5")
            for e in range(3):
                r, score = row(pool, f"ffn_b2_{e}"), gsm[0:TN, 23 + e:24 + e]
                scored = RG[6][0:TN, 0:D] if e else b2s
                pool.tensor_scalar(scored, r, score, None, ALU.mult).then_inc(sem("row_used"), 1)
                pool.wait_ge(sem("row_used"), ROWS.index(f"ffn_b2_{e}") + 1)
                if e:
                    pool.tensor_tensor(b2s, b2s, scored, ALU.add).then_inc(sem("bias_summed"), 1)
                    pool.wait_ge(sem("bias_summed"), e)
            pool.tensor_tensor(asR(0), asR(0), b2s.unsqueeze(1).broadcast_to([TN, NT, D]), ALU.add)\
                .then_inc(sem("bias_added"), 1)
            if stop == "L0":
                return

            for c in range(4):
                pool.wait_ge(sem("types_high"), c + 1)
                w = weight_chunk("Wt0", c)
                pool.tensor_tensor(weight_chunk("Wt0", c, ring_r), w, weight_high(c).bitcast(F32), ALU.subtract)\
                    .then_inc(sem("types_split_pool"), 1)
            psum.computed(pool, "f2_4")
            pool.dma_start(types_i[:, 0:N], a["types"].broadcast_to([128, N])).then_inc(sem("types_loaded"), 16)

            def type_weights_low(t, c):
                pool.wait_ge(sem("types_high"), C * t + c + 1)
                w = weight_chunk(f"Wt{t}", c)
                pool.tensor_tensor(weight_chunk(f"Wt{t}", c, ring_r), w, weight_high(C * t + c).bitcast(F32), ALU.subtract)\
                    .then_inc(sem("types_split_pool"), 1)

            def add_type(t, m):
                n = C * (t - 1) + m
                pool.wait_ge(sem("typed_part"), n + 1)
                pool.tensor_tensor(asT(3)[:, m, :], asT(3)[:, m, :], typed[n % 2], ALU.add)\
                    .then_inc(sem("typed"), 1)
            for t in range(TYPES):
                for m in range(C):
                    if t:
                        add_type(t, m)
                    if t + 1 < TYPES and m < 4:
                        type_weights_low(t + 1, m)
            for c in range(C):
                low_part(pool, "msgU", c)
            pool.wait_ge(sem("typed"), C * (TYPES - 1))
            pool.dma_start(typed_dram, RG[3][:, 0:C * NP]).then_inc(sem("typed_spilled"), 16)
            psum.drained(pool, *[f"U{t}" for t in range(NT)])
            pool.dma_start(u_dram.rearrange("(t p) d -> p t d", p=TN), asR(7)).then_inc(sem("source_part_stored"), 16)
            pool.wait_ge(sem("row_used"), ROWS.index("msg_b1") + 1)
            pool.dma_start(v_dram.rearrange("(t p) d -> p t d", p=TN), asR(4)).then_inc(sem("target_part_stored"), 16)
            pool.wait_ge(sem("source_part_stored"), 16)
            pool.wait_ge(sem("target_part_stored"), 16)

            def source_part(j):
                if j >= NM:
                    psum.computed(pool, f"scattered{j - NM}")
                elif j == 5:
                    pool.wait_ge(sem("row_used"), ROWS.index("out_b") + 1)
                pool.indirect_dma_start(out=msg[j % NM], out_offset=None, in_=u_dram,
                                        in_offset=bass.IndirectOffsetOnAxis(ap=rows_i[:, 0, j:j + 1], axis=0))\
                    .then_inc(sem(f"source_gathered{j % NM}"), 16)

            def target_part(j):
                pool.wait_ge(sem(f"source_gathered{j % NM}"), 16 * (j // NM + 1))
                pool.indirect_dma_start(out=msg[j % NM], out_offset=None, in_=v_dram,
                                        in_offset=bass.IndirectOffsetOnAxis(ap=rows_i[:, 1, j:j + 1], axis=0),
                                        compute_op=ALU.add).then_inc(sem(f"gathered{j % NM}"), 16)
            source_part(0)
            source_part(1)
            for j in range(2, ST):
                source_part(j)
                target_part(j - 2)
            target_part(ST - 2)
            target_part(ST - 1)
            psum.computed(pool, f"ao{MH - 1}")
            pool.dma_start(RG[3][:, 0:C * NP], typed_dram).then_inc(sem("typed_back"), 16)
            psum.computed(pool, "aoT5")
            pool.dma_start(msg_b2, a["msg_b2"]).then_inc(sem("msg_b2"), 16)

            for c in range(C):
                low_part(pool, "msg2", c)
            for c in range(3):
                low_part(pool, "agg2", c)
            for c in range(C):
                low_part(pool, "outW", c)
            for c in range(C):
                low_part(pool, "Wproj1", c)
            for c in range(C):
                low_part(pool, "moe1a", c)
            for c in range(3):
                low_part(pool, "moe1b", c)
            psum.computed(pool, "a1_5")
            pool.memset(sel, 1.0).then_inc(sem("sel"), 1)
            pool.wait_ge(sem("sel"), 1)
            pool.affine_select(out=sel, in_=sel, compare_op=ALU.is_ge, fill=0.0, base=0, pattern=[[1, 2 * D]],
                               channel_multiplier=-FF).then_inc(sem("sel"), 1)
            pool.wait_ge(sem("sel"), 2)
            pool.affine_select(out=sel, in_=sel, compare_op=ALU.is_ge, fill=0.0, base=FF - 1, pattern=[[-1, 2 * D]],
                               channel_multiplier=FF).then_inc(sem("sel"), 1)
            for c in range(3, C):
                low_part(pool, "moe1b", c)
            for panel in ("moe2a", "moe2b"):
                for c in range(C):
                    low_part(pool, panel, c)

        @block.vector
        def _(dve):
            steps = [0]

            def link(ins):
                steps[0] += 1
                ins.then_inc(sem("dve_step"), 1)
                dve.wait_ge(sem("dve_step"), steps[0])

            def tile_statistics(src, t):
                for b in range(2):
                    last = dve.bn_stats(stats[0:TN, t, b, :], src[:, t, b * 384:(b + 1) * 384])
                return last

            def statistics(src, k, tiles, begun=False):
                lo, hi = tiles[0], tiles[-1] + 1
                if not begun:
                    for t in tiles:
                        last = tile_statistics(src, t)
                    link(last)
                for t in tiles:
                    last = dve.bn_aggr(mv[0:TN, t, :], stats[0:TN, t, :, :].rearrange("p b s -> p (b s)"))
                link(last)
                r = lnt[0:TN, :, lo:hi]
                link(dve.tensor_scalar(r[:, 0, :], mv[0:TN, lo:hi, 1], 1e-5, None, ALU.add))
                dve.reciprocal(r[:, 1, :], r[:, 0, :]).then_inc(sem("ln_inverse"), 1)
                dve.wait_ge(sem("ln_root"), k)
                link(dve.tensor_tensor(r[:, 3, :], r[:, 2, :], r[:, 2, :], ALU.mult))
                link(dve.tensor_tensor(r[:, 3, :], r[:, 3, :], r[:, 0, :], ALU.mult))
                link(dve.tensor_scalar(r[:, 3, :], r[:, 3, :], -0.5, 1.5, ALU.mult, ALU.add))
                link(dve.tensor_tensor(r[:, 3, :], r[:, 3, :], r[:, 2, :], ALU.mult))

            def normalise(src, dst, k, tiles=range(NT), begun=False):
                statistics(src, k, tiles, begun)
                for t in tiles:
                    last = dve.tensor_scalar(dst[:, t, :], src[:, t, :], mv[0:TN, t, 0:1], lnt[0:TN, 3, t:t + 1],
                                             ALU.subtract, ALU.mult)
                return last

            dve.memset(one[:, :], 1.0)
            dve.memset(sv("mask"), 1.0)
            dve.memset(sv("one5", 128), 1.0)
            dve.memset(rfe[64:128, :], -0.5)
            dve.memset(rfo[0:64, :], -0.5)
            dve.memset(gsm[:, 31:32], 2.0)
            dve.memset(asT(2)[:, :, N:NP], 0.0)
            link(dve.memset(asV(4)[:, :, :, 64:65], 1.0))
            dve.memset(sv5("mask")[:, :, 0:1], 0.0).then_inc(sem("consts"), 1)

            dve.wait_ge(sem("edges_loaded"), 16)
            dve.wait_ge(sem("consts"), 2)
            dve.wait_ge(sem("iotas"), 4)
            dve.tensor_copy(sv("src"), srcdst[:, 0:EJ])
            link(dve.tensor_copy(sv("dst"), srcdst[:, EJ:2 * EJ]))
            link(dve.tensor_scalar(sv("dt"), sv("dst"), float(TN), None, ALU.is_ge))
            for c in range(2, NT):
                link(dve.scalar_tensor_tensor(sv("dt"), sv("dst"), float(c * TN), sv("dt"), ALU.is_ge, ALU.add))
            link(dve.scalar_tensor_tensor(sv("dl"), sv("dt"), -float(TN), sv("dst"), ALU.mult, ALU.add))
            link(dve.tensor_scalar(sv("dl"), sv("dl"), 1.0, None, ALU.add))
            for c in range(NT):
                last = dve.tensor_scalar(sv5("ind")[:, c, :], sv("dt"), float(c), None, ALU.is_equal)
            link(last)
            link(dve.tensor_tensor_scan(sv("incl"), sv("mask"), sv("ind"), 0.0, ALU.mult, ALU.add))
            link(dve.tensor_tensor(sv("excl"), sv("incl"), sv("ind"), ALU.subtract))
            dve.tensor_copy(sv("tot"), sv5("incl")[:, :, EJ - 1]).then_inc(sem("rank_totals"), 1)

            dve.wait_ge(sem("x_loaded"), 16)
            normalise(asR(0), asR(1), 1).then_inc(sem("normed"), 1)

            ps, free = psum.computed(dve, "rank")
            dve.wait_ge(sem("iotas"), 4)
            nti, posi = sv("nti", 128).bitcast(I32), sv("posi").bitcast(I32)
            hii, loi = sv("hii").bitcast(I32), sv("loi").bitcast(I32)
            link(dve.tensor_scalar(nti, ps[:, 512:512 + NT], 127.0, None, ALU.add))
            link(dve.tensor_scalar(nti, nti, 7, None, ALU.arith_shift_right))
            link(dve.tensor_copy(sv("ntf", 128), nti))
            link(dve.tensor_tensor_scan(sv("incl5", 128), sv("one5", 128), sv("ntf", 128), 0.0, ALU.mult, ALU.add))
            link(dve.tensor_tensor(sv("ts", 128), sv("incl5", 128), sv("ntf", 128), ALU.subtract))
            dve.scalar_tensor_tensor(sv("base"), sv("ts"), 128.0, ps[0:TN, 0:NT], ALU.mult, ALU.add)\
               .then_inc(free, 1)
            psum.drained(dve, "rank")
            link(dve.tensor_tensor(sv5("part"), sv5("excl"), sv("base").unsqueeze(2).broadcast_to([TN, NT, EJ]),
                                   ALU.add))
            link(dve.tensor_tensor(sv("part"), sv("part"), sv("ind"), ALU.mult))
            link(dve.tensor_reduce(sv("pos"), sv5("part").rearrange("p c j -> p j c"), AX.X, ALU.add))
            link(dve.tensor_copy(posi, sv("pos")))
            link(dve.tensor_scalar(hii, posi, 7, None, ALU.arith_shift_right))
            link(dve.tensor_scalar(loi, posi, 127, None, ALU.bitwise_and))
            link(dve.tensor_copy(sv("hi"), hii))
            dve.tensor_copy(sv("lo"), loi).then_inc(sem("places"), 1)
            link(dve.tensor_scalar(sv("tmf", 128), sv("kio", 128), sv("ts", 128)[:, 1:2], None, ALU.is_ge))
            for c in range(2, NT):
                link(dve.scalar_tensor_tensor(sv("tmf", 128), sv("kio", 128), sv("ts", 128)[:, c:c + 1],
                                              sv("tmf", 128), ALU.is_ge, ALU.add))
            link(dve.tensor_copy(tmap[:, :], sv("tmf", 128)))

            unread = oh_raw[0:TN, :].bitcast(BF16)
            dve.wait_ge(sem("small_loads"), 16 * 6)
            for s in range(ES):
                psum.drained(dve, f"hidden{s}")
                if s >= 4:
                    dve.wait_ge(sem("logits"), s - 3)
                for i in range(edge_tiles(s)):
                    at = s % 4 * D + FF * i
                    last = dve.tensor_tensor_reduce(unread[:, at:at + FF], hid[s % 5][:, FF * i:FF * (i + 1)],
                                                    edge_w2, 1.0, 0.0, ALU.mult, ALU.add,
                                                    sv("ew")[:, 4 * s + i:4 * s + i + 1])
                last.then_inc(sem("logits"), 1)
            dve.wait_ge(sem("logits"), ES)
            dve.wait_ge(sem("edge_weights"), 1)
            o = so["src"][0]
            edge_values = RG[5][0:TN, o:o + 3 * EJ].rearrange("p (k j) -> p k j", k=3)

            def place(j, u):
                dve.scalar_tensor_tensor(oh_hi(u), sv("kio").unsqueeze(1).broadcast_to([TN, 3, ST]),
                                         sv("hi")[:, bass.ds(j, 1)],
                                         edge_values[:, :, bass.ds(j, 1)].broadcast_to([TN, 3, ST]),
                                         ALU.is_equal, ALU.mult)
                dve.tensor_scalar(oh_lo(u), iota_n[0:TN, 0:128], sv("lo")[:, bass.ds(j, 1)], None,
                                  ALU.is_equal).then_inc(sem("onehot_edge"), 1)
            for j in range(4):
                place(j, j)
            with dve.Fori(1, EJ // 4) as i:
                for u in range(4):
                    dve.wait_ge(sem("onehot_used"), 4 * i + u - 3)
                    place(4 * i + u, u)
            dve.wait_ge(sem("onehot_used"), EJ - 4)
            place(EJ - 1, 0)
            link(dve.memset(asN(6), 0.0))
            for t in range(NT):
                last = dve.tensor_copy(asN(6)[:, t, t * TN:(t + 1) * TN], ident[0:TN, 0:TN])
            link(last)
            ps, free = psum.computed(dve, "sorted")
            dve.tensor_copy(slots[:, :, :].rearrange("p k s -> p (k s)"), ps[:, 0:3 * ST]).then_inc(free, 1)
            psum.drained(dve, "sorted")
            dve.tensor_copy(rows_i[:, 0, :], slots[:, 0, :])
            link(dve.scalar_tensor_tensor(sv("tmp", 128), sv("tmf", 128), float(TN), slots[:, 1, :], ALU.mult, ALU.add))
            dve.tensor_scalar(rows_i[:, 1, :], sv("tmp", 128), -1.0, 0.0, ALU.add, ALU.max)\
               .then_inc(sem("slots_ready"), 1)
            dve.wait_ge(sem("slots_ready"), 1)

            def tile_of(j):
                return dve.value_load(tmap[0:1, j:j + 1], min_val=0, max_val=NT - 1)

            def copies(k, nm, c):
                ps, free = psum.computed(dve, f"{nm}{c}")
                if c:
                    psum.computed(dve, f"kp{2 * c - 1}b")
                dve.tensor_copy(two(eqk(k, 0)[0:64, :]), halves(ps, HN, 0, 64)).then_inc(free, 1)
                dve.tensor_copy(two(eqk(k, 1)[64:128, :]), halves(ps, HN, 64, 128)).then_inc(free, 1)

            def onehots_of(j):
                if j >= 4:
                    psum.computed(dve, f"counts{j - 4}")
                dve.tensor_scalar(oh_src(j % 4)[:, 0:N], iota_n[:, 0:N], slots[:, 0, j:j + 1], None, ALU.is_equal)
                dve.tensor_scalar(oh_dst(j % 4)[:, 0:TN], iota_n[:, 1:TN + 1], slots[:, 1, j:j + 1], None,
                                  ALU.is_equal).then_inc(sem("onehot_dst"), 1)
            AT = asN(6).rearrange("p t (v n) -> p t v n", v=NT)

            def add_counts(j):
                v = tile_of(j)
                ps, free = psum.computed(dve, f"counts{j}")
                if j:
                    psum.drained(dve, f"counts{j - 1}")
                dst = AT[:, :, bass.ds(v, 1), :]
                dve.tensor_tensor(dst, dst, blocks(ps).unsqueeze(2), ALU.add).then_inc(free, 1)

            def head_out(name, h, eps, dst, widths=65):
                ps, free = psum.computed(dve, name)
                v = ps[0:TN, 0:NT * 65].rearrange("p (t d) -> p t d", t=NT)
                r = rden[0:TN, :, :]
                link(dve.tensor_scalar(r[:, 0, :], v[:, :, 64], eps, None, ALU.add))
                link(dve.reciprocal(r[:, 1, :], r[:, 0, :]))
                dve.tensor_tensor(dst[:, :, h * 64:(h + 1) * 64], v[:, :, 0:64],
                                  r[:, 1, :].unsqueeze(2).broadcast_to([TN, NT, 64]), ALU.mult).then_inc(free, 1)

            onehots_of(0)
            onehots_of(1)
            for k, (nm, n, part) in enumerate(mixer0):
                if nm in ("q", "k"):
                    copies(int(nm == "k"), nm, n)
                elif nm == "kv":
                    ps, free = psum.computed(dve, f"kv{n}")
                    if n >= 2:
                        psum.computed(dve, f"mo{n - 2}")
                    dve.tensor_copy(kvs[:, n % 2, :, :], halves(ps, 65, 0, 128)).then_inc(free, 1)
                elif nm == "mo":
                    head_out(f"mo{n}", n, 256e-6, asR(5))
                for j in tiles_behind(mixer0, k, 0):
                    if j + 2 < ST:
                        onehots_of(j + 2)
                    add_counts(j)
            for t in range(NT):
                ps, free = psum.computed(dve, f"A{t}")
                dve.tensor_scalar(neg[:, t, :].rearrange("p (s n) -> p s n", s=NT), blocks(ps), 0.0, NEG,
                                  ALU.is_equal, ALU.mult).then_inc(free, 1)
            dve.memset(asG(4)[:, :, :, GC:GC + 1], 1.0)

            s8 = asd[0:TN]

            def used(name):
                dve.wait_ge(sem("row_used"), ROWS.index(name) + 1)

            def scores(g):
                for t in range(NT):
                    psum.drained(dve, f"h{g}_{t}")
                    for k, nm in enumerate(("a_src", "a_dst")):
                        r = row(dve, f"{nm}{g}")
                        for hh in range(GH):
                            w = (GH * k + hh + 8 * (t % 2)) * GC
                            last = dve.tensor_tensor_reduce(unread[:, w:w + GC], asG(4)[:, t, hh, 0:GC],
                                                            r[:, hh * GC:(hh + 1) * GC], 1.0, 0.0, ALU.mult, ALU.add,
                                                            s8[:, k, t, hh:hh + 1])
                    link(last)
                for k in range(2):
                    dve.sem_inc(sem("row_used"), 1)
                used(f"a_dst{g}")
                dve.tensor_scalar(s8[:, 7], s8[:, 0], 0.2, None, ALU.mult).then_inc(sem("scores_src"), 1)

            def maxima(g, hh):
                ps, free = psum.computed(dve, f"asb{g}{hh}")
                if hh:
                    psum.drained(dve, f"asb{g}{hh - 1}")
                for t in range(NT):
                    dst = unread[:, t * N:(t + 1) * N].rearrange("p (s n) -> p s n", s=NT)
                    last = dve.tensor_tensor_reduce(dst, blocks(ps), neg[:, t, :].rearrange("p (s n) -> p s n", s=NT),
                                                    1.0, 3.0 * NEG, ALU.add, ALU.max, s8[:, 2, t, hh:hh + 1])
                last.then_inc(free, 1)

            scores(0)
            dve.tensor_tensor(asR(1), asR(1), row5(dve, "mix_b_proj"), ALU.add).then_inc(sem("row_used"), 1)
            used("mix_b_proj")
            dve.wait_ge(sem("scores_src"), 1)
            for t in range(NT):
                ps, free = psum.computed(dve, f"mp{t}")
                dve.tensor_tensor(two(asR(1)[:, t, :]), two(asR(1)[:, t, :]), halves(ps, 384), ALU.add)\
                   .then_inc(free, 1)
                if t < GH:
                    maxima(0, t)
            for g in range(3):
                psum.drained(dve, *[f"asb{g}{hh}" for hh in range(GH)])
                link(dve.tensor_tensor(s8[:, 3], s8[:, 2], s8[:, 1], ALU.add))
                link(dve.scalar_tensor_tensor(s8[:, 4], s8[:, 3], 0.2, s8[:, 3], ALU.mult, ALU.max))
                dve.tensor_tensor(s8[:, 5], s8[:, 1], s8[:, 4], ALU.subtract).then_inc(sem("offsets"), 1)
                dve.scalar_tensor_tensor(s8[:, 6], s8[:, 1], 0.2, s8[:, 4], ALU.mult, ALU.subtract)\
                   .then_inc(sem("offsets"), 1)

                def weights_of(hh):
                    P = asN(P_REGION[hh % 2])
                    ps, free = psum.computed(dve, f"off{g}{hh}0")
                    for s in range(NT):
                        psum.reads(dve, f"off{g}{hh}1", s + 1, NT)
                        p = P[:, s, :].rearrange("p (t n) -> p t n", t=NT)
                        dve.scalar_tensor_tensor(p, blocks(ps), s8[:, 0, s, hh:hh + 1], p, ALU.add, ALU.max)\
                           .then_inc(free, 1)

                def denominators(hh):
                    b = 2 * (hh % 2)
                    for part, lo, hi in (("a", 0, 4), ("b", 4, 5)):
                        ps, free = psum.computed(dve, f"gat{g}{hh}{part}")
                        if hh >= 2:
                            psum.drained(dve, f"gat{g}{hh - 2}{part}")
                        link(dve.tensor_scalar(rden[0:TN, b, lo:hi],
                                               ps[0:TN, :].rearrange("p (t n) -> p t n", t=4)[:, 0:hi - lo, GC],
                                               1e-16, None, ALU.add))
                        dve.reciprocal(rden[0:TN, b + 1, lo:hi], rden[0:TN, b, lo:hi]).then_inc(sem("row_inverse"), 1)
                weights_of(0)
                weights_of(1)
                for hh in range(GH):
                    denominators(hh)
                    if hh + 2 < GH:
                        weights_of(hh + 2)
                if g == 0:
                    psum.drained(dve, *[f"mp{t}" for t in range(NT)])
                    link(normalise(asR(1), asR(1), 2))
                    dve.tensor_tensor(asR(1), asR(1), row5(dve, "mix_gamma"), ALU.mult).then_inc(sem("row_used"), 1)
                    used("mix_gamma")
                    dve.tensor_tensor(asR(1), asR(1), row5(dve, "mix_beta"), ALU.add).then_inc(sem("row_used"), 1)
                    used("mix_beta")
                    dve.sem_inc(sem("mixed"), 1)
                if g < 2:
                    scores(g + 1)
                    dve.wait_ge(sem("scores_src"), g + 2)
                    if g == 0:
                        dve.wait_ge(sem("mix_spilled"), 16)
                    for t in range(NT):
                        ps, free = psum.computed(dve, f"wo{g}_{t}")
                        dst = two(asR(1)[:, t, :])
                        if g == 0:
                            dve.tensor_copy(dst, halves(ps, 384)).then_inc(free, 1)
                        else:
                            dve.tensor_tensor(dst, dst, halves(ps, 384), ALU.add).then_inc(free, 1)
                        if t < GH:
                            maxima(g + 1, t)
                    psum.drained(dve, *[f"wo{g}_{t}" for t in range(NT)])
            link(dve.tensor_tensor(asR(1), asR(1), row5(dve, "gnn_b_out"), ALU.add))
            dve.wait_ge(sem("x_and_mix_back"), 32)
            dve.tensor_tensor(asR(0), asR(0), asR(8), ALU.add).then_inc(sem("row_used"), 1)
            used("gnn_b_out")
            for k, tiles in ((3, range(0, 3)), (4, range(3, NT))):
                for t in tiles:
                    ps, free = psum.computed(dve, f"wo2_{t}")
                    dst = two(asR(1)[:, t, :])
                    dve.tensor_tensor(dst, dst, halves(ps, 384), ALU.add).then_inc(free, 1)
                psum.drained(dve, *[f"wo2_{t}" for t in tiles])
                lo, hi = tiles[0], tiles[-1] + 1
                link(dve.scalar_tensor_tensor(asR(0)[:, lo:hi, :], asR(1)[:, lo:hi, :], 0.0, asR(0)[:, lo:hi, :],
                                              ALU.max, ALU.add))
                normalise(asR(0), asR(5), k, tiles).then_inc(sem("normed"), 1)

            psum.drained(dve, *[f"xlT{c}" for c in range(C)])
            dve.sem_inc(sem("sums"), 1)
            ps, free = psum.computed(dve, "gate")
            G = gsm
            dve.tensor_scalar(G[:, 0:3], ps[:, 0:3], 1.0 / N, None, ALU.mult).then_inc(free, 1)
            psum.drained(dve, "gate")
            link(dve.tensor_reduce(G[:, 6:7], G[:, 0:3], AX.X, ALU.max))
            dve.tensor_scalar(G[:, 0:3], G[:, 0:3], G[:, 6:7], None, ALU.subtract).then_inc(sem("gate_shifted"), 1)
            dve.wait_ge(sem("gate_exp"), 1)
            link(dve.tensor_reduce(G[:, 8:9], G[:, 3:6], AX.X, ALU.add))
            link(dve.reciprocal(G[:, 9:10], G[:, 8:9]))
            link(dve.tensor_scalar(G[:, 10:13], G[:, 3:6], G[:, 9:10], None, ALU.mult))
            link(dve.tensor_reduce(G[:, 6:7], G[:, 10:13], AX.X, ALU.max))
            link(dve.scalar_tensor_tensor(G[:, 16:19], G[:, 10:13], G[:, 6:7], G[:, 26:29], ALU.is_equal, ALU.mult))
            link(dve.tensor_reduce(G[:, 19:20], G[:, 16:19], AX.X, ALU.max))
            link(dve.tensor_scalar(G[:, 20:23], G[:, 16:19], G[:, 19:20], None, ALU.is_equal))
            link(dve.tensor_tensor(G[:, 23:26], G[:, 20:23], G[:, 10:13], ALU.mult))
            def take(e, dst, src, w):
                w = w[0:dst.shape[0], e:e + 1]
                if e == 0:
                    return dve.tensor_scalar(dst, src, w, None, ALU.mult)
                return dve.scalar_tensor_tensor(dst, src, w, dst, ALU.mult, ALU.add)
            pick, score = G[:, 20:23], G[:, 23:26]
            dve.sem_inc(sem("scored"), 1)
            for e in range(3):
                for half in range(2):
                    weights(dve, "ffn1", 3 * half)
                    src = ring[(2 * pindex["ffn1"] + half) % 5][:, :, e * FF:(e + 1) * FF]
                    take(e, w1s[:, 3 * half:3 * half + 3, :], src, pick)
                first = PL["ffn_b1"][0] + 2 * e
                link(take(e, gsm[0:96, 29:31], cols[0:96, first:first + 2], pick))
            dve.sem_inc(sem("first_chosen"), 1)
            for e in range(3):
                for m in range(2):
                    last = take(e, w2s[:, m, :], weights(dve, "ffn2", 2 * e + m)[0:96, :], score)
                link(last)
            dve.sem_inc(sem("chosen"), 1)
            dve.wait_ge(sem("bias_added"), 1)
            for t in range(NT):
                ps, free = psum.computed(dve, f"f2_{t}")
                dst = two(asR(0)[:, t, :])
                dve.tensor_tensor(dst, dst, halves(ps, 384), ALU.add).then_inc(free, 1)
                psum.drained(dve, f"f2_{t}")
                last = tile_statistics(asR(0), t)
            link(last)
            if stop == "L0":
                dve.sem_inc(sem("final"), 1)
                return

            normalise(asR(0), asR(1), 5, begun=True).then_inc(sem("normed"), 1)
            link(dve.memset(types_i[:, N:NP], 0.0))
            dve.wait_ge(sem("types_loaded"), 16)
            for t in range(TYPES):
                last = dve.tensor_scalar(masks[:, t, :], types_i, float(t), None, ALU.is_equal)
            link(last)

            def type_weights_low(t, c):
                dve.wait_ge(sem("types_high"), C * t + c + 1)
                w = weight_chunk(f"Wt{t}", c)
                dve.tensor_tensor(weight_chunk(f"Wt{t}", c, ring_r), w, weight_high(C * t + c).bitcast(F32), ALU.subtract)\
                   .then_inc(sem("types_split_dve"), 1)
            for c in range(C):
                dve.wait_ge(sem("nodes_high"), c + 1)
                dve.tensor_tensor(split_T(6)[:, c, :], asT(2)[:, c, :], split_T(5)[:, c, :].bitcast(F32), ALU.subtract)\
                   .then_inc(sem("nodes_low"), 1)
            type_weights_low(0, 4)
            type_weights_low(0, 5)
            n = 0
            for t in range(TYPES):
                for m in range(C):
                    if m == C - 1 and t + 1 < TYPES:
                        type_weights_low(t + 1, 4)
                        type_weights_low(t + 1, 5)
                    ps, free = psum.computed(dve, f"ty{t}_{m}")
                    dst = asT(3)[:, m, :] if t == 0 else typed[n % 2]
                    if t:
                        if n >= 2:
                            dve.wait_ge(sem("typed"), n - 1)
                        n += 1
                    dve.scalar_tensor_tensor(two(dst), halves(ps, HN, 0, 128), col("b_type", C * t + m),
                                             two(masks[:, t, :]), ALU.add, ALU.mult).then_inc(free, 1)
                    if t:
                        psum.drained(dve, f"ty{t}_{m}")
                        dve.sem_inc(sem("typed_part"), 1)
            dve.wait_ge(sem("typed"), C * (TYPES - 1))
            for c in range(C):
                dve.wait_ge(sem("typed_high"), c + 1)
                dve.tensor_tensor(split_T(6)[:, c, :], asT(3)[:, c, :], split_T(5)[:, c, :].bitcast(F32), ALU.subtract)\
                   .then_inc(sem("typed_low"), 1)
            for c in range(C):
                low_part(dve, "msgV", c)
            psum.drained(dve, *[f"Vm{t}" for t in range(NT)])
            dve.tensor_tensor(asR(4), asR(4), row5(dve, "msg_b1"), ALU.add).then_inc(sem("row_used"), 1)

            dve.wait_ge(sem("typed_spilled"), 16)
            psum.computed(dve, "Vm4")
            dve.wait_ge(sem("source_part_stored"), 16)
            link(dve.memset(S4, 0.0))
            dve.memset(asV(3)[:, :, :, 64:65], 1.0).then_inc(sem("ones1"), 1)
            dve.tensor_tensor(asR(0), asR(0), row5(dve, "mix1_proj_b"), ALU.add).then_inc(sem("row_used"), 1)
            dve.wait_ge(sem("row_used"), 15)
            dve.tensor_tensor(asR(1), asR(1), row5(dve, "out_b"), ALU.add).then_inc(sem("row_used"), 1)

            def onehot_of(j):
                if j >= 4:
                    psum.computed(dve, f"scattered{j - 4}")
                dve.tensor_scalar(oh_dst32(j % 4), iota_n[:, 1:TN + 1], slots[:, 1, j:j + 1], None, ALU.is_equal)\
                   .then_inc(sem("onehot_dst1"), 1)

            def add_messages(j):
                v = tile_of(j)
                ps, free = psum.computed(dve, f"scattered{j}")
                if j:
                    psum.drained(dve, f"scattered{j - 1}")
                dst = S4[:, bass.ds(v, 1), :, 0:384]
                dve.tensor_tensor(dst, dst, halves(ps, 384).unsqueeze(1), ALU.add)
                dst = S4[:, bass.ds(v, 1), 0:1, 384:385]
                dve.tensor_tensor(dst, dst, ps[0:TN, 384:385].unsqueeze(1).unsqueeze(1), ALU.add).then_inc(free, 1)
            onehot_of(0)
            onehot_of(1)
            for k, (nm, n) in enumerate(mixer1):
                if k == 20:
                    dve.wait_ge(sem("row_used"), 16)
                    dve.tensor_tensor(asR(0), asR(0), row5(dve, "ln_b"), ALU.add).then_inc(sem("row_used"), 1)
                if nm == "k1_":
                    if n == 0:
                        dve.wait_ge(sem("target_part_stored"), 16)
                    ps, free = psum.computed(dve, f"k1_{n}")
                    if n >= 2:
                        psum.computed(dve, f"sc{2 * n - 3}_4")
                    dve.tensor_copy(two(qk1(1, n % 2)), halves(ps, HN, 0, 128)).then_inc(free, 1)
                elif nm == "ao":
                    head_out(f"ao{n}", n, 0.0, asR(8))
                for j in tiles_behind(mixer1, k, 2):
                    if j + 2 < ST:
                        onehot_of(j + 2)
                    add_messages(j)

            used("ln_b")
            psum.computed(dve, "k1_5")
            psum.drained(dve, *[f"aoT{c}" for c in range(C)])
            dve.memset(asT(5)[:, :, N:NP], 0.0)
            dve.memset(ewsum[:, N:NP], 0.0).then_inc(sem("ewsum_padded"), 1)
            for c in range(C):
                dve.wait_ge(sem("sums_high"), c + 1)
                dve.tensor_tensor(split_T(4)[:, c, :], asT(4)[:, c, :], split_T(2)[:, c, :].bitcast(F32), ALU.subtract)\
                   .then_inc(sem("sums_low"), 1)
            low_part(dve, "agg1", 0)
            for m in range(C):
                ps, free = psum.computed(dve, f"m2_{m}")
                psum.reads(dve, f"m2_{m}", 1, 2)
                dve.tensor_tensor(two(split_T(7)[:, m, :]), halves(ps, HN, 0, 128),
                                  two(split_T(6)[:, m, :].bitcast(F32)), ALU.subtract).then_inc(free, 1)
            for c in range(1, C):
                low_part(dve, "agg1", c)
            for c in range(C):
                dve.wait_ge(sem("a1_high"), c + 1)
                dve.tensor_tensor(split_T(4)[:, c, :], asT(4)[:, c, :], split_T(2)[:, c, :].bitcast(F32), ALU.subtract)\
                   .then_inc(sem("a1_low"), 1)
            for c in range(3, C):
                low_part(dve, "agg2", c)
            dve.wait_ge(sem("typed_back"), 16)
            for m in range(C):
                ps, free = psum.computed(dve, f"a2_{m}")
                dst = two(asT(3)[:, m, :])
                dve.scalar_tensor_tensor(dst, halves(ps, HN, 0, 128), col("agg_b2", m), dst, ALU.add, ALU.add)\
                   .then_inc(free, 1)
            for c in range(C):
                dve.wait_ge(sem("aggregated_high"), c + 1)
                dve.tensor_tensor(split_T(3)[:, c, :], asT(3)[:, c, :], split_T(6)[:, c, :].bitcast(F32), ALU.subtract)\
                   .then_inc(sem("aggregated_low"), 1)
            for c in range(C):
                dve.wait_ge(sem("ao_high"), c + 1)
                dve.tensor_tensor(split_T(5)[:, c, :], asT(5)[:, c, :], split_T(2)[:, c, :].bitcast(F32), ALU.subtract)\
                   .then_inc(sem("ao_low"), 1)
            for t in range(NT):
                ps, free = psum.computed(dve, f"o_{t}")
                dst = two(asR(1)[:, t, :])
                dve.tensor_tensor(dst, dst, halves(ps, 384), ALU.add).then_inc(free, 1)
            psum.drained(dve, *[f"o_{t}" for t in range(NT)])
            statistics(asR(1), 6, range(NT))
            g = row(dve, "ln_g")
            for t in range(NT):
                last = dve.scalar_tensor_tensor(asR(1)[:, t, :], asR(1)[:, t, :], mv[0:TN, t, 0:1], g,
                                                ALU.subtract, ALU.mult)
            link(last)
            for t in range(NT):
                last = dve.scalar_tensor_tensor(asR(0)[:, t, :], asR(1)[:, t, :], lnt[0:TN, 3, t:t + 1],
                                                asR(0)[:, t, :], ALU.mult, ALU.add)
            last.then_inc(sem("row_used"), 1)
            used("ln_g")

            for k, tiles in ((7, range(0, 3)), (9, range(3, NT))):
                lo, hi = tiles[0], tiles[-1] + 1
                for t in tiles:
                    ps, free = psum.computed(dve, f"p1_{t}")
                    dst = two(asR(0)[:, t, :])
                    dve.tensor_tensor(dst, dst, halves(ps, 384), ALU.add).then_inc(free, 1)
                psum.drained(dve, *[f"p1_{t}" for t in tiles])
                link(normalise(asR(0), asR(1), k, tiles))
                if k == 9:
                    dve.memset(asT(2)[:, :, N:NP], 0.0)
                normalise(asR(1), asR(3), k + 1, tiles).then_inc(sem("tokens"), 1)
            link(dve.tensor_tensor(asR(0), asR(0), asR(1), ALU.add))
            for c in range(C):
                dve.wait_ge(sem("tokens_high"), c + 1)
                dve.tensor_tensor(split_T(4)[:, c, :], asT(2)[:, c, :], split_T(5)[:, c, :].bitcast(F32), ALU.subtract)\
                   .then_inc(sem("tokens_low"), 1)
            ps, free = psum.computed(dve, "router")

            def wide(x):
                return x.unsqueeze(2).broadcast_to([TN, NT, EXPERTS])
            lg = ps[0:TN, 0:NT * EXPERTS].rearrange("p (t e) -> p t e", t=NT)
            link(dve.tensor_reduce(gq[:, 0, :], lg, AX.X, ALU.max))
            dve.tensor_tensor(gate_v[:, 0], lg, wide(gq[:, 0, :]), ALU.subtract).then_inc(free, 1)
            psum.drained(dve, "router")
            dve.sem_inc(sem("router_shifted"), 1)
            for e in range(EXPERTS):
                dve.memset(gate_v[:, 4, :, e:e + 1], float(EXPERTS - e))
            link(dve.memset(gT[:, N:NP], 0.0))
            dve.wait_ge(sem("router_exp"), 1)
            link(dve.tensor_reduce(gq[:, 1, :], gate_v[:, 1], AX.X, ALU.add))
            link(dve.reciprocal(gq[:, 2, :], gq[:, 1, :]))
            link(dve.tensor_tensor(gate_v[:, 1], gate_v[:, 1], wide(gq[:, 2, :]), ALU.mult))
            link(dve.tensor_copy(gate_v[:, 0], gate_v[:, 1]))
            for k in range(2):
                link(dve.tensor_reduce(gq[:, 0, :], gate_v[:, 0], AX.X, ALU.max))
                link(dve.tensor_tensor(gate_v[:, 2], gate_v[:, 0], wide(gq[:, 0, :]), ALU.is_equal))
                link(dve.tensor_tensor(gate_v[:, 2], gate_v[:, 2], gate_v[:, 4], ALU.mult))
                link(dve.tensor_reduce(gq[:, 1, :], gate_v[:, 2], AX.X, ALU.max))
                link(dve.tensor_tensor(gate_v[:, 2], gate_v[:, 2], wide(gq[:, 1, :]), ALU.is_equal))
                if k == 0:
                    link(dve.tensor_copy(gate_v[:, 3], gate_v[:, 2]))
                    link(dve.scalar_tensor_tensor(gate_v[:, 0], gate_v[:, 2], -2.0, gate_v[:, 0], ALU.mult, ALU.add))
                else:
                    link(dve.tensor_tensor(gate_v[:, 3], gate_v[:, 3], gate_v[:, 2], ALU.add))
            link(dve.tensor_tensor(gate_v[:, 3], gate_v[:, 3], gate_v[:, 1], ALU.mult))
            link(dve.tensor_reduce(gq[:, 1, :], gate_v[:, 3], AX.X, ALU.add))
            link(dve.reciprocal(gq[:, 2, :], gq[:, 1, :]))
            dve.tensor_tensor(gate_v[:, 3], gate_v[:, 3], wide(gq[:, 2, :]), ALU.mult).then_inc(sem("gates"), 1)

            def hidden_low_part(j):
                dve.wait_ge(sem("hidden_high"), j + 1)
                dve.tensor_tensor(hidden_at(j, RG_R), hidden_at(j), hidden_high(j).bitcast(F32), ALU.subtract)\
                   .then_inc(sem("hidden_low"), 1)
            for j in range(12):
                psum.drained(dve, f"up{j}")
                ps, free = psum.computed(dve, f"gb{j}")
                dve.tensor_tensor(two(hidden_at(j)), two(silu[j % 2]), halves(ps, HN, 0, 128), ALU.mult)\
                   .then_inc(free, 1)
                if 3 <= j < C + 3:
                    hidden_low_part(j - 3)
            for j in range(C, 12):
                hidden_low_part(j)
            for t in range(NT):
                ps, free = psum.computed(dve, f"y_{t}")
                dst = two(asR(0)[:, t, :])
                dve.tensor_tensor(dst, dst, halves(ps, 384), ALU.add).then_inc(free, 1)


def kernel(**inputs):
    import numpy as np
    import concourse.bacc as bacc
    from concourse.bass_utils import run_bass_kernel_spmd as run

    v = {k: np.asarray(x) for k, x in inputs.items()}
    g0, m0, f0, g1 = "L0_gnn_", "L0_mix_", "L0_ffn_", "L1_gnn_"

    def chunks(x, p=128):
        x = x.reshape(-1, x.shape[-1] // p, p)
        return x.transpose(2, 0, 1).reshape(p, -1)

    parts = {"b_ah": chunks(v[g0 + "b_ah"]), "b0": chunks(v[g0 + "b0"]), "b1": chunks(v[g0 + "b1"]),
             "b2": chunks(v[g0 + "b2"]), "agg_b1": chunks(v[g1 + "agg_b1"]), "agg_b2": chunks(v[g1 + "agg_b2"]),
             "b_type": chunks(v[g1 + "b_type"]), "ffn_b1": chunks(v[f0 + "b1"], 96),
             "moe_g": chunks(v["L1_ffn_ln_gamma"]), "moe_b": chunks(v["L1_ffn_ln_beta"]),
             "wg": v[f0 + "Wg"].T.reshape(C, 128, 3).transpose(1, 0, 2).reshape(128, 18),
             "rw": v["L1_ffn_router_w"].reshape(C, 128, 8).transpose(1, 0, 2).reshape(128, 48)}
    places = column_places()
    cols = np.zeros((128, places["all"][1]), np.float32)
    for name, x in parts.items():
        cols[0:x.shape[0], places[name][0]:places[name][0] + x.shape[1]] = x
    a = [v[f"{g0}{nm}{i}"].reshape(-1) for i in range(3) for nm in ("a_src", "a_dst")]
    rows = [*a[0:2], v[m0 + "b_proj"], v[m0 + "gamma"], v[m0 + "beta"], *a[2:6]]
    rows += [v[g0 + "b_out"], *v[f0 + "b2"], v[g1 + "msg_b1"], v["L1_mix_proj_b"], v[g1 + "out_b"],
             v[g1 + "ln_b"], v[g1 + "ln_g"]]

    def flat(x):
        return x.transpose(1, 0, 2).reshape(x.shape[1], -1)
    arrays = {
        "x": v["x"], "srcdst": np.stack([v["src"].reshape(EJ, TN).T, v["dst"].reshape(EJ, TN).T], 1).reshape(TN, -1),
        "attrT": np.concatenate([v["edge_attr_32"].T, np.ones((1, E), np.float32)]),
        "edge_w2": v[g1 + "edge_W2"].reshape(1, FF), "types": v["node_type_6"].reshape(1, N), "cols": cols, "rows": np.stack(rows),
        "W_ah": v[g0 + "W_ah"], "W0": v[g0 + "W0"], "W1": v[g0 + "W1"], "W2": v[g0 + "W2"], "W_out": v[g0 + "W_out"],
        "W_qkv": v[m0 + "W_qkv"], "W_proj": v[m0 + "W_proj"], "rfT": v[m0 + "random_features"].T,
        "ffn_W1": flat(v[f0 + "W1"]), "ffn_W2": v[f0 + "W2"].reshape(-1, D),
        "W_type": v[g1 + "W_type"].reshape(-1, D), "msg_W1": v[g1 + "msg_W1"], "msg_W2": v[g1 + "msg_W2"],
        "msg_b2": v[g1 + "msg_b2"].reshape(1, D), "edge_W1": np.concatenate([v[g1 + "edge_W1"], v[g1 + "edge_b1"].reshape(1, FF)]), "edge_b2": v[g1 + "edge_b2"].reshape(1, 1),
        "agg_W1": v[g1 + "agg_W1"], "agg_W2": v[g1 + "agg_W2"], "out_W": v[g1 + "out_W"],
        "qkv1_w": v["L1_mix_qkv_w"].T, "proj1_w": v["L1_mix_proj_w"].T,
        "moe_w1": flat(v["L1_ffn_w1"]), "moe_w2": v["L1_ffn_w2"].reshape(-1, D),
    }
    nc = bacc.Bacc("TRN2", target_bir_lowering=False, num_devices=1)
    aps, given = {}, {}
    for name, x in arrays.items():
        x = np.ascontiguousarray(x)
        given[f"in_{name}_dram"] = x
        aps[name] = nc.dram_tensor(f"in_{name}_dram", x.shape, mybir.dt.from_np(x.dtype), kind="ExternalInput").ap()
    aps["out"] = nc.dram_tensor("out_0_dram", (N, D), F32, kind="ExternalOutput").ap()
    gps_block(nc, aps)
    r = run(nc, [given], core_ids=[0])
    return r.results[0]["out_0_dram"]
```
